# Optimizing a Trainium2 kernel written in Bass

```python
import numpy as np
import jax
import jax.numpy as jnp

def _softmax(x, axis=-1):
    return jax.nn.softmax(x, axis=axis)

def _gelu(x):
    return jax.nn.gelu(x, approximate=True)

def _silu(x):
    return jax.nn.silu(x)

def _sigmoid(x):
    return jax.nn.sigmoid(x)

def _layernorm(x, axis=-1, eps=1e-05):
    m = jnp.mean(x, axis=axis, keepdims=True)
    v = jnp.var(x, axis=axis, keepdims=True)
    return (x - m) / jnp.sqrt(v + eps)

def _scatter_add(tgt, idx, src, axis=0):
    return tgt.at[idx].add(src)

def _segment_sum(src, seg, n):
    return jax.ops.segment_sum(src, seg, n)
kernel_name = 'mk_flamingo_gated_d4_seqx_r8_5753fb'

def setup_inputs(seed: int=0):
    np.random.seed(seed)
    _w = jnp.asarray

    def _rec_inputs():
        import jax
        import jax.numpy as jnp
        _rk = jax.random.key(seed)
        x = 7.22e-05 + 1 * jax.random.normal(jax.random.fold_in(_rk, 1), (8, 256, 128), jnp.float32)
        _lenS = 256 - jax.random.randint(jax.random.fold_in(_rk, 7), (8,), 0, max(1, 256 // 4) + 1, jnp.int32)
        _lenS2 = 512 - jax.random.randint(jax.random.fold_in(_rk, 8), (8,), 0, max(1, 512 // 4) + 1, jnp.int32)
        _ctx_768P = jax.random.normal(jax.random.fold_in(_rk, 11), (8, 16, 96), jnp.float32)
        _ctx_768c = jax.random.dirichlet(jax.random.fold_in(_rk, 511), 0.3 * jnp.ones((16,), jnp.float32), (8, 512))
        _ctx_768t = jnp.einsum('bsk,bkd->bsd', _ctx_768c, _ctx_768P)
        _ctx_768t = _ctx_768t * jax.lax.rsqrt(jnp.mean(jnp.square(_ctx_768t)) + 1e-12) * 0.953939
        ctx_768 = -0.000191848 + 0.999787 * (_ctx_768t + 0.3 * jax.random.normal(jax.random.fold_in(_rk, 611), (8, 512, 96), jnp.float32))
        _validS = jnp.arange(256)[None, :] < _lenS[:, None]
        _validS2 = jnp.arange(512)[None, :] < _lenS2[:, None]
        _causal = jnp.tril(jnp.ones((256, 256), dtype=bool))
        mask_BxS2_bf1 = jnp.ones((8, 512), dtype=bool)
        _g = jax.random.normal(jax.random.fold_in(_rk, 9001), (2, 4), jnp.float32)
        _g = jnp.sign(_g) * jnp.maximum(jnp.abs(_g), 1.0) + (_g == 0) * 1.0
        g_xattn = _g[0]
        g_ffn = _g[1]
        return (x, ctx_768, mask_BxS2_bf1, g_xattn, g_ffn)
    x, ctx_768, mask_BxS2_bf1, g_xattn, g_ffn = _rec_inputs()

    def _L0_xattn_setup():
        import jax, jax.numpy as jnp
        import numpy as np
        NUM_HEADS = 16
        CLAMP = 10000.0
        key = jax.random.key(seed)
        ks = jax.random.split(key, 8)
        B, Nq, Nkv, Cq, Ckv = (4, 256, 256, 128, 96)
        s_q = 1.0 / np.sqrt(Cq)
        s_kv = 1.0 / np.sqrt(Ckv)
        return {'query': jax.random.normal(ks[0], (B, Nq, Cq), jnp.float32), 'key_value': jax.random.normal(ks[1], (B, Nkv, Ckv), jnp.float32), 'Wq': jax.random.normal(ks[2], (Cq, Cq), jnp.float32) * s_q, 'bq': jnp.zeros((Cq,), jnp.float32), 'Wk': jax.random.normal(ks[3], (Ckv, Cq), jnp.float32) * s_kv, 'bk': jnp.zeros((Cq,), jnp.float32), 'Wv': jax.random.normal(ks[4], (Ckv, Cq), jnp.float32) * s_kv, 'bv': jnp.zeros((Cq,), jnp.float32), 'Wo': jax.random.normal(ks[5], (Cq, Cq), jnp.float32) * s_q, 'bo': jnp.zeros((Cq,), jnp.float32)}
    _L0_xattn_all = _L0_xattn_setup()
    _L0_xattn_in = {k: v for k, v in _L0_xattn_all.items() if k in ('Wq', 'bq', 'Wk', 'bk', 'Wv', 'bv', 'Wo', 'bo')}
    del _L0_xattn_all

    def _L0_ffn_setup():
        import jax, jax.numpy as jnp
        import numpy as np
        D_MODEL = 128
        EXPANSION = 4
        D_HIDDEN = D_MODEL * EXPANSION
        NUM_STAGES = int(np.log2(D_HIDDEN))

        def butterfly(y, weights, dim):
            lead = y.shape[:-1]
            for stage in range(weights.shape[0]):
                s = 2 ** stage
                nb = dim // (2 * s)
                yr = y.reshape(*lead, nb, 2, s)
                a = yr[..., 0, :]
                b = yr[..., 1, :]
                w = weights[stage].reshape(nb, s, 2, 2)
                na = w[..., 0, 0] * a + w[..., 0, 1] * b
                nb2 = w[..., 1, 0] * a + w[..., 1, 1] * b
                y = jnp.stack([na, nb2], axis=-2).reshape(*lead, dim)
            return y
        key = jax.random.key(seed)
        ks = jax.random.split(key, 6)
        B, S = (4, 256)
        x = jax.random.normal(ks[0], (B, S, D_MODEL), jnp.float32)
        W_exp = jax.random.normal(ks[1], (D_MODEL, D_HIDDEN), jnp.float32) * 0.02
        b_exp = jnp.zeros((D_HIDDEN,), jnp.float32)
        up_weights = jax.random.normal(ks[2], (NUM_STAGES, D_HIDDEN // 2, 2, 2), jnp.float32) * 0.02
        up_bias = jnp.zeros((D_HIDDEN,), jnp.float32)
        down_weights = jax.random.normal(ks[3], (NUM_STAGES, D_HIDDEN // 2, 2, 2), jnp.float32) * 0.02
        W_con = jax.random.normal(ks[4], (D_HIDDEN, D_MODEL), jnp.float32) * 0.02
        b_con = jnp.zeros((D_MODEL,), jnp.float32)
        down_bias = jnp.zeros((D_MODEL,), jnp.float32)
        return dict(x=x, W_exp=W_exp, b_exp=b_exp, up_weights=up_weights, up_bias=up_bias, down_weights=down_weights, W_con=W_con, b_con=b_con, down_bias=down_bias)
    _L0_ffn_all = _L0_ffn_setup()
    _L0_ffn_in = {k: v for k, v in _L0_ffn_all.items() if k in ('W_exp', 'b_exp', 'up_weights', 'up_bias', 'down_weights', 'W_con', 'b_con', 'down_bias')}
    del _L0_ffn_all

    def _L1_xattn_setup():
        import jax, jax.numpy as jnp
        import numpy as np
        HEADS = 16
        DIM_HEAD = 64
        RANK = 32
        LORA_W = 1.0
        IPA_SCALE = 1.0
        IPA_TOKENS = 4
        SCALE = DIM_HEAD ** (-0.5)

        def _split_heads(t):
            b, n, _ = t.shape
            return t.reshape(b, n, HEADS, DIM_HEAD).transpose(0, 2, 1, 3)

        def _merge_heads(t):
            b, h, n, d = t.shape
            return t.transpose(0, 2, 1, 3).reshape(b, n, h * d)

        def _attention(q_in, k_in, v_in):
            q = _split_heads(q_in)
            k = _split_heads(k_in)
            v = _split_heads(v_in)
            s = jnp.einsum('bhid,bhjd->bhij', q, k) * SCALE
            p = jax.nn.softmax(s, axis=-1)
            o = jnp.einsum('bhij,bhjd->bhid', p, v)
            return _merge_heads(o)

        def _lora(t, down, up, alpha):
            return t @ down @ up * (LORA_W * alpha[0] / RANK)
        key = jax.random.key(seed)
        ks = jax.random.split(key, 20)
        B, N, QD, CD, ID = (8, 512, 128, 96, HEADS * DIM_HEAD)
        CTX = 77 + IPA_TOKENS
        s = 0.02
        return {'x': jax.random.normal(ks[0], (B, N, QD), jnp.float32), 'context': jax.random.normal(ks[1], (B, CTX, CD), jnp.float32), 'Wq': jax.random.normal(ks[2], (QD, ID), jnp.float32) * s, 'Wk': jax.random.normal(ks[3], (CD, ID), jnp.float32) * s, 'Wv': jax.random.normal(ks[4], (CD, ID), jnp.float32) * s, 'Wo': jax.random.normal(ks[5], (ID, QD), jnp.float32) * s, 'bo': jnp.zeros((QD,), jnp.float32), 'q_down': jax.random.normal(ks[6], (QD, RANK), jnp.float32) * s, 'q_up': jax.random.normal(ks[7], (RANK, ID), jnp.float32) * s, 'q_alpha': jnp.ones((1,), jnp.float32) * RANK, 'k_down': jax.random.normal(ks[8], (CD, RANK), jnp.float32) * s, 'k_up': jax.random.normal(ks[9], (RANK, ID), jnp.float32) * s, 'k_alpha': jnp.ones((1,), jnp.float32) * RANK, 'v_down': jax.random.normal(ks[10], (CD, RANK), jnp.float32) * s, 'v_up': jax.random.normal(ks[11], (RANK, ID), jnp.float32) * s, 'v_alpha': jnp.ones((1,), jnp.float32) * RANK, 'o_down': jax.random.normal(ks[12], (ID, RANK), jnp.float32) * s, 'o_up': jax.random.normal(ks[13], (RANK, QD), jnp.float32) * s, 'o_alpha': jnp.ones((1,), jnp.float32) * RANK, 'Wk_ipa': jax.random.normal(ks[14], (CD, ID), jnp.float32) * s, 'Wv_ipa': jax.random.normal(ks[15], (CD, ID), jnp.float32) * s}
    _L1_xattn_all = _L1_xattn_setup()
    _L1_xattn_in = {k: v for k, v in _L1_xattn_all.items() if k in ('Wq', 'Wk', 'Wv', 'Wo', 'bo', 'q_down', 'q_up', 'q_alpha', 'k_down', 'k_up', 'k_alpha', 'v_down', 'v_up', 'v_alpha', 'o_down', 'o_up', 'o_alpha', 'Wk_ipa', 'Wv_ipa')}
    del _L1_xattn_all

    def _L1_ffn_setup():
        import jax, jax.numpy as jnp
        import numpy as np
        DIM = 128
        HID = 512
        E = 8
        TOPK = 2
        ALPHA = 2.0
        B, T = (1, 256)
        DOWN_SCALE = 0.01
        key = jax.random.key(seed)
        ks = jax.random.split(key, 8)
        s = 1.0 / np.sqrt(DIM)
        sh = 1.0 / np.sqrt(HID)
        return {'x': jax.random.normal(ks[0], (B, T, DIM), jnp.float32), 'w_router': jax.random.uniform(ks[1], (DIM, E), jnp.float32, -s, s), 'w_up': jax.random.uniform(ks[2], (E - 1, DIM, HID), jnp.float32, -s, s), 'w_gate': jax.random.uniform(ks[3], (E - 1, DIM, HID), jnp.float32, -s, s), 'w_down': jax.random.normal(ks[4], (E - 1, HID, DIM), jnp.float32) * DOWN_SCALE, 'ws_up': jax.random.uniform(ks[5], (DIM, HID), jnp.float32, -s, s), 'ws_gate': jax.random.uniform(ks[6], (DIM, HID), jnp.float32, -s, s), 'ws_down': jax.random.normal(ks[7], (HID, DIM), jnp.float32) * DOWN_SCALE}
    _L1_ffn_all = _L1_ffn_setup()
    _L1_ffn_in = {k: v for k, v in _L1_ffn_all.items() if k in ('w_router', 'w_up', 'w_gate', 'w_down', 'ws_up', 'ws_gate', 'ws_down')}
    del _L1_ffn_all

    def _L2_xattn_setup():
        import jax, jax.numpy as jnp
        import numpy as np
        HEADS = 16
        DIM_HEAD = 64
        key = jax.random.key(seed)
        ks = jax.random.split(key, 8)
        B, S, D = (16, 512, 128)
        K, DE = (77, 96)
        inner = HEADS * DIM_HEAD
        hidden_states = jax.random.normal(ks[0], (B, S, D), dtype=jnp.float32)
        encoder_hidden_states = jax.random.normal(ks[1], (B, K, DE), dtype=jnp.float32)
        sc_q = 1.0 / np.sqrt(D)
        sc_kv = 1.0 / np.sqrt(DE)
        sc_o = 1.0 / np.sqrt(inner)
        Wq = jax.random.normal(ks[2], (D, inner), dtype=jnp.float32) * sc_q
        Wk = jax.random.normal(ks[3], (DE, inner), dtype=jnp.float32) * sc_kv
        Wv = jax.random.normal(ks[4], (DE, inner), dtype=jnp.float32) * sc_kv
        Wo = jax.random.normal(ks[5], (inner, D), dtype=jnp.float32) * sc_o
        bo = jax.random.normal(ks[6], (D,), dtype=jnp.float32) * 0.01
        return {'hidden_states': hidden_states, 'encoder_hidden_states': encoder_hidden_states, 'Wq': Wq, 'Wk': Wk, 'Wv': Wv, 'Wo': Wo, 'bo': bo}
    _L2_xattn_all = _L2_xattn_setup()
    _L2_xattn_in = {k: v for k, v in _L2_xattn_all.items() if k in ('Wq', 'Wk', 'Wv', 'Wo', 'bo')}
    del _L2_xattn_all

    def _L2_ffn_setup():
        import jax, jax.numpy as jnp
        import numpy as np
        NUM_COLUMNS = 16
        INPUT_DIM = 128
        NUM_NEURONS = 32
        SPARSITY = 0.05
        B, S = (4, 256)

        def _l2norm(v, axis=-1, eps=1e-12):
            n = jnp.sqrt(jnp.sum(v * v, axis=axis, keepdims=True))
            return v / jnp.maximum(n, eps)
        key = jax.random.key(seed)
        ks = jax.random.split(key, 12)
        D, C, N = (INPUT_DIM, NUM_COLUMNS, NUM_NEURONS)
        inp = {'x': jax.random.normal(ks[0], (B, S, D), dtype=jnp.float32), 'col_emb': jax.random.normal(ks[1], (C, D), dtype=jnp.float32) * 0.02, 'gate_w1': jax.random.normal(ks[2], (D, D // 2), dtype=jnp.float32) / np.sqrt(D), 'gate_b1': jnp.zeros((D // 2,), dtype=jnp.float32), 'gate_w2': jax.random.normal(ks[3], (D // 2, C), dtype=jnp.float32) / np.sqrt(D // 2), 'gate_b2': jnp.zeros((C,), dtype=jnp.float32), 'W_cols': jax.random.normal(ks[4], (C, D, N), dtype=jnp.float32) / np.sqrt(D), 'b_cols': jnp.zeros((C, N), dtype=jnp.float32), 'proj_w': jax.random.normal(ks[5], (C * N, D), dtype=jnp.float32) / np.sqrt(C * N), 'proj_b': jnp.zeros((D,), dtype=jnp.float32), 'ln_g': jnp.ones((D,), dtype=jnp.float32), 'ln_b': jnp.zeros((D,), dtype=jnp.float32)}
        return inp
    _L2_ffn_all = _L2_ffn_setup()
    _L2_ffn_in = {k: v for k, v in _L2_ffn_all.items() if k in ('col_emb', 'gate_w1', 'gate_b1', 'gate_w2', 'gate_b2', 'W_cols', 'b_cols', 'proj_w', 'proj_b', 'ln_g', 'ln_b')}
    del _L2_ffn_all

    def _L3_xattn_setup():
        import jax, jax.numpy as jnp
        import numpy as np
        DIM = 128
        CTX_DIM = 96
        HEADS = 16
        key = jax.random.key(seed)
        ks = jax.random.split(key, 7)
        B, N, M = (4, 512, 32)
        x = jax.random.normal(ks[0], (B, N, DIM), dtype=jnp.float32)
        context = jax.random.normal(ks[1], (B, M, CTX_DIM), dtype=jnp.float32)
        context_mask = jnp.ones((B, M), dtype=bool)
        s_d = 1.0 / np.sqrt(DIM)
        s_c = 1.0 / np.sqrt(CTX_DIM)
        Wq = jax.random.normal(ks[2], (DIM, DIM), dtype=jnp.float32) * s_d
        Wk = jax.random.normal(ks[3], (CTX_DIM, DIM), dtype=jnp.float32) * s_c
        Wv = jax.random.normal(ks[4], (CTX_DIM, DIM), dtype=jnp.float32) * s_c
        Wo = jax.random.normal(ks[5], (DIM, DIM), dtype=jnp.float32) * s_d
        return {'x': x, 'context': context, 'context_mask': context_mask, 'Wq': Wq, 'Wk': Wk, 'Wv': Wv, 'Wo': Wo}
    _L3_xattn_all = _L3_xattn_setup()
    _L3_xattn_in = {k: v for k, v in _L3_xattn_all.items() if k in ('Wq', 'Wk', 'Wv', 'Wo')}
    del _L3_xattn_all

    def _L3_ffn_setup():
        import jax, jax.numpy as jnp
        import numpy as np
        B, S, H = (4, 256, 128)
        E = 8
        GS = 2
        NG = E // GS
        F = int(H * 4 * (2.0 / 3.0))
        key = jax.random.key(seed)
        ks = jax.random.split(key, 7)
        sc_h = 1.0 / np.sqrt(H)
        sc_f = 1.0 / np.sqrt(F)
        return {'x': jax.random.normal(ks[0], (B, S, H), dtype=jnp.float32), 'Wr': jax.random.normal(ks[1], (H, E), dtype=jnp.float32) * sc_h, 'br': jnp.zeros((E,), dtype=jnp.float32), 'W_up': jax.random.normal(ks[2], (NG, H, F), dtype=jnp.float32) * sc_h, 'b_up': jax.random.normal(ks[3], (NG, F), dtype=jnp.float32) * 0.01, 'W_down': jax.random.normal(ks[4], (E, F, H), dtype=jnp.float32) * sc_f, 'b_down': jax.random.normal(ks[5], (E, H), dtype=jnp.float32) * 0.01}
    _L3_ffn_all = _L3_ffn_setup()
    _L3_ffn_in = {k: v for k, v in _L3_ffn_all.items() if k in ('Wr', 'br', 'W_up', 'b_up', 'W_down', 'b_down')}
    del _L3_ffn_all
    return {'x': x, 'ctx_768': ctx_768, 'mask_BxS2_bf1': mask_BxS2_bf1, 'g_xattn': g_xattn, 'g_ffn': g_ffn, 'L0_xattn_Wq': _L0_xattn_in['Wq'], 'L0_xattn_bq': _L0_xattn_in['bq'], 'L0_xattn_Wk': _L0_xattn_in['Wk'], 'L0_xattn_bk': _L0_xattn_in['bk'], 'L0_xattn_Wv': _L0_xattn_in['Wv'], 'L0_xattn_bv': _L0_xattn_in['bv'], 'L0_xattn_Wo': _L0_xattn_in['Wo'], 'L0_xattn_bo': _L0_xattn_in['bo'], 'L0_ffn_W_exp': _L0_ffn_in['W_exp'], 'L0_ffn_b_exp': _L0_ffn_in['b_exp'], 'L0_ffn_up_weights': _L0_ffn_in['up_weights'], 'L0_ffn_up_bias': _L0_ffn_in['up_bias'], 'L0_ffn_down_weights': _L0_ffn_in['down_weights'], 'L0_ffn_W_con': _L0_ffn_in['W_con'], 'L0_ffn_b_con': _L0_ffn_in['b_con'], 'L0_ffn_down_bias': _L0_ffn_in['down_bias'], 'L1_xattn_Wq': _L1_xattn_in['Wq'], 'L1_xattn_Wk': _L1_xattn_in['Wk'], 'L1_xattn_Wv': _L1_xattn_in['Wv'], 'L1_xattn_Wo': _L1_xattn_in['Wo'], 'L1_xattn_bo': _L1_xattn_in['bo'], 'L1_xattn_q_down': _L1_xattn_in['q_down'], 'L1_xattn_q_up': _L1_xattn_in['q_up'], 'L1_xattn_q_alpha': _L1_xattn_in['q_alpha'], 'L1_xattn_k_down': _L1_xattn_in['k_down'], 'L1_xattn_k_up': _L1_xattn_in['k_up'], 'L1_xattn_k_alpha': _L1_xattn_in['k_alpha'], 'L1_xattn_v_down': _L1_xattn_in['v_down'], 'L1_xattn_v_up': _L1_xattn_in['v_up'], 'L1_xattn_v_alpha': _L1_xattn_in['v_alpha'], 'L1_xattn_o_down': _L1_xattn_in['o_down'], 'L1_xattn_o_up': _L1_xattn_in['o_up'], 'L1_xattn_o_alpha': _L1_xattn_in['o_alpha'], 'L1_xattn_Wk_ipa': _L1_xattn_in['Wk_ipa'], 'L1_xattn_Wv_ipa': _L1_xattn_in['Wv_ipa'], 'L1_ffn_w_router': _L1_ffn_in['w_router'], 'L1_ffn_w_up': _L1_ffn_in['w_up'], 'L1_ffn_w_gate': _L1_ffn_in['w_gate'], 'L1_ffn_w_down': _L1_ffn_in['w_down'], 'L1_ffn_ws_up': _L1_ffn_in['ws_up'], 'L1_ffn_ws_gate': _L1_ffn_in['ws_gate'], 'L1_ffn_ws_down': _L1_ffn_in['ws_down'], 'L2_xattn_Wq': _L2_xattn_in['Wq'], 'L2_xattn_Wk': _L2_xattn_in['Wk'], 'L2_xattn_Wv': _L2_xattn_in['Wv'], 'L2_xattn_Wo': _L2_xattn_in['Wo'], 'L2_xattn_bo': _L2_xattn_in['bo'], 'L2_ffn_col_emb': _L2_ffn_in['col_emb'], 'L2_ffn_gate_w1': _L2_ffn_in['gate_w1'], 'L2_ffn_gate_b1': _L2_ffn_in['gate_b1'], 'L2_ffn_gate_w2': _L2_ffn_in['gate_w2'], 'L2_ffn_gate_b2': _L2_ffn_in['gate_b2'], 'L2_ffn_W_cols': _L2_ffn_in['W_cols'], 'L2_ffn_b_cols': _L2_ffn_in['b_cols'], 'L2_ffn_proj_w': _L2_ffn_in['proj_w'], 'L2_ffn_proj_b': _L2_ffn_in['proj_b'], 'L2_ffn_ln_g': _L2_ffn_in['ln_g'], 'L2_ffn_ln_b': _L2_ffn_in['ln_b'], 'L3_xattn_Wq': _L3_xattn_in['Wq'], 'L3_xattn_Wk': _L3_xattn_in['Wk'], 'L3_xattn_Wv': _L3_xattn_in['Wv'], 'L3_xattn_Wo': _L3_xattn_in['Wo'], 'L3_ffn_Wr': _L3_ffn_in['Wr'], 'L3_ffn_br': _L3_ffn_in['br'], 'L3_ffn_W_up': _L3_ffn_in['W_up'], 'L3_ffn_b_up': _L3_ffn_in['b_up'], 'L3_ffn_W_down': _L3_ffn_in['W_down'], 'L3_ffn_b_down': _L3_ffn_in['b_down']}

def reference(x, ctx_768, mask_BxS2_bf1, g_xattn, g_ffn, L0_xattn_Wq, L0_xattn_bq, L0_xattn_Wk, L0_xattn_bk, L0_xattn_Wv, L0_xattn_bv, L0_xattn_Wo, L0_xattn_bo, L0_ffn_W_exp, L0_ffn_b_exp, L0_ffn_up_weights, L0_ffn_up_bias, L0_ffn_down_weights, L0_ffn_W_con, L0_ffn_b_con, L0_ffn_down_bias, L1_xattn_Wq, L1_xattn_Wk, L1_xattn_Wv, L1_xattn_Wo, L1_xattn_bo, L1_xattn_q_down, L1_xattn_q_up, L1_xattn_q_alpha, L1_xattn_k_down, L1_xattn_k_up, L1_xattn_k_alpha, L1_xattn_v_down, L1_xattn_v_up, L1_xattn_v_alpha, L1_xattn_o_down, L1_xattn_o_up, L1_xattn_o_alpha, L1_xattn_Wk_ipa, L1_xattn_Wv_ipa, L1_ffn_w_router, L1_ffn_w_up, L1_ffn_w_gate, L1_ffn_w_down, L1_ffn_ws_up, L1_ffn_ws_gate, L1_ffn_ws_down, L2_xattn_Wq, L2_xattn_Wk, L2_xattn_Wv, L2_xattn_Wo, L2_xattn_bo, L2_ffn_col_emb, L2_ffn_gate_w1, L2_ffn_gate_b1, L2_ffn_gate_w2, L2_ffn_gate_b2, L2_ffn_W_cols, L2_ffn_b_cols, L2_ffn_proj_w, L2_ffn_proj_b, L2_ffn_ln_g, L2_ffn_ln_b, L3_xattn_Wq, L3_xattn_Wk, L3_xattn_Wv, L3_xattn_Wo, L3_ffn_Wr, L3_ffn_br, L3_ffn_W_up, L3_ffn_b_up, L3_ffn_W_down, L3_ffn_b_down):
    import jax
    import jax.numpy as jnp

    def _L0_xattn_ref(query, key_value, Wq, bq, Wk, bk, Wv, bv, Wo, bo):
        import jax, jax.numpy as jnp
        import numpy as np
        NUM_HEADS = 16
        CLAMP = 10000.0
        B, Nq, Cq = query.shape
        Nkv = key_value.shape[1]
        H = NUM_HEADS
        D = Cq // H
        scale = D ** (-0.5)
        q = (query @ Wq + bq).reshape(B, Nq, H, D).transpose(0, 2, 1, 3)
        k = (key_value @ Wk + bk).reshape(B, Nkv, H, D).transpose(0, 2, 1, 3)
        v = (key_value @ Wv + bv).reshape(B, Nkv, H, D).transpose(0, 2, 1, 3)
        attn = jnp.einsum('bhqd,bhkd->bhqk', q, k) * scale
        attn = jnp.clip(attn, -CLAMP, CLAMP)
        attn = jax.nn.softmax(attn, axis=-1)
        attn = jnp.where(jnp.any(jnp.isnan(attn)), jnp.asarray(1.0 / Nkv, attn.dtype), attn)
        x = jnp.einsum('bhqk,bhkd->bqhd', attn, v).reshape(B, Nq, Cq)
        return x @ Wo + bo

    def _L0_ffn_ref(x, W_exp, b_exp, up_weights, up_bias, down_weights, W_con, b_con, down_bias):
        import jax, jax.numpy as jnp
        import numpy as np
        D_MODEL = 128
        EXPANSION = 4
        D_HIDDEN = D_MODEL * EXPANSION
        NUM_STAGES = int(np.log2(D_HIDDEN))

        def butterfly(y, weights, dim):
            lead = y.shape[:-1]
            for stage in range(weights.shape[0]):
                s = 2 ** stage
                nb = dim // (2 * s)
                yr = y.reshape(*lead, nb, 2, s)
                a = yr[..., 0, :]
                b = yr[..., 1, :]
                w = weights[stage].reshape(nb, s, 2, 2)
                na = w[..., 0, 0] * a + w[..., 0, 1] * b
                nb2 = w[..., 1, 0] * a + w[..., 1, 1] * b
                y = jnp.stack([na, nb2], axis=-2).reshape(*lead, dim)
            return y
        h = jnp.einsum('bsd,dh->bsh', x, W_exp) + b_exp
        h = butterfly(h, up_weights, D_HIDDEN)
        h = jax.nn.gelu(h + up_bias, approximate=False)
        h = butterfly(h, down_weights, D_HIDDEN)
        y = jnp.einsum('bsh,hd->bsd', h, W_con) + b_con
        return y + down_bias

    def _L1_xattn_ref(x, context, Wq, Wk, Wv, Wo, bo, q_down, q_up, q_alpha, k_down, k_up, k_alpha, v_down, v_up, v_alpha, o_down, o_up, o_alpha, Wk_ipa, Wv_ipa):
        import jax, jax.numpy as jnp
        import numpy as np
        HEADS = 16
        DIM_HEAD = 64
        RANK = 32
        LORA_W = 1.0
        IPA_SCALE = 1.0
        IPA_TOKENS = 4
        SCALE = DIM_HEAD ** (-0.5)

        def _split_heads(t):
            b, n, _ = t.shape
            return t.reshape(b, n, HEADS, DIM_HEAD).transpose(0, 2, 1, 3)

        def _merge_heads(t):
            b, h, n, d = t.shape
            return t.transpose(0, 2, 1, 3).reshape(b, n, h * d)

        def _attention(q_in, k_in, v_in):
            q = _split_heads(q_in)
            k = _split_heads(k_in)
            v = _split_heads(v_in)
            s = jnp.einsum('bhid,bhjd->bhij', q, k) * SCALE
            p = jax.nn.softmax(s, axis=-1)
            o = jnp.einsum('bhij,bhjd->bhid', p, v)
            return _merge_heads(o)

        def _lora(t, down, up, alpha):
            return t @ down @ up * (LORA_W * alpha[0] / RANK)
        q_in = x @ Wq + _lora(x, q_down, q_up, q_alpha)
        end = context.shape[1] - IPA_TOKENS
        org_ctx = context[:, :end, :]
        ipa_ctx = context[:, end:, :]
        k_in = org_ctx @ Wk + _lora(org_ctx, k_down, k_up, k_alpha)
        v_in = org_ctx @ Wv + _lora(org_ctx, v_down, v_up, v_alpha)
        out = _attention(q_in, k_in, v_in)
        ipa_k = ipa_ctx @ Wk_ipa
        ipa_v = ipa_ctx @ Wv_ipa
        out_ipa = _attention(q_in, ipa_k, ipa_v)
        out = out + IPA_SCALE * out_ipa
        return out @ Wo + bo + _lora(out, o_down, o_up, o_alpha)

    def _L1_ffn_ref(x, w_router, w_up, w_gate, w_down, ws_up, ws_gate, ws_down):
        import jax, jax.numpy as jnp
        import numpy as np
        DIM = 128
        HID = 512
        E = 8
        TOPK = 2
        ALPHA = 2.0
        B, T = (1, 256)
        DOWN_SCALE = 0.01
        logits = x @ w_router
        probs = jax.nn.softmax(logits.astype(jnp.float32), axis=-1).astype(logits.dtype)
        topk_vals, topk_idx = jax.lax.top_k(probs, TOPK)
        up = jnp.einsum('btd,edh->ebth', x, w_up)
        gate = jax.nn.silu(jnp.einsum('btd,edh->ebth', x, w_gate))
        exp_out = jnp.einsum('ebth,ehd->ebtd', up * gate, w_down)
        out = jnp.zeros_like(x)
        eids = jnp.arange(E - 1)
        for i in range(TOPK - 1):
            idx_i = topk_idx[..., i]
            sel = (idx_i[None, :, :] == eids[:, None, None]).astype(x.dtype)
            gathered = jnp.einsum('ebt,ebtd->btd', sel, exp_out)
            out = out + ALPHA * topk_vals[..., i:i + 1] * gathered
        shared = x @ ws_up * jax.nn.silu(x @ ws_gate) @ ws_down
        return out + shared

    def _L2_xattn_ref(hidden_states, encoder_hidden_states, Wq, Wk, Wv, Wo, bo):
        import jax, jax.numpy as jnp
        import numpy as np
        HEADS = 16
        DIM_HEAD = 64
        B, S, D = hidden_states.shape
        K = encoder_hidden_states.shape[1]
        H, Dh = (HEADS, DIM_HEAD)
        scale = 1.0 / np.sqrt(Dh)
        q = hidden_states @ Wq
        k = encoder_hidden_states @ Wk
        v = encoder_hidden_states @ Wv
        q = q.reshape(B, S, H, Dh).transpose(0, 2, 1, 3)
        k = k.reshape(B, K, H, Dh).transpose(0, 2, 1, 3)
        v = v.reshape(B, K, H, Dh).transpose(0, 2, 1, 3)
        scores = jnp.einsum('bhsd,bhkd->bhsk', q, k) * scale
        probs = jax.nn.softmax(scores, axis=-1)
        out = jnp.einsum('bhsk,bhkd->bhsd', probs, v)
        out = out.transpose(0, 2, 1, 3).reshape(B, S, H * Dh)
        out = out @ Wo + bo
        return out

    def _L2_ffn_ref(x, col_emb, gate_w1, gate_b1, gate_w2, gate_b2, W_cols, b_cols, proj_w, proj_b, ln_g, ln_b):
        import jax, jax.numpy as jnp
        import numpy as np
        NUM_COLUMNS = 16
        INPUT_DIM = 128
        NUM_NEURONS = 32
        SPARSITY = 0.05
        B, S = (4, 256)

        def _l2norm(v, axis=-1, eps=1e-12):
            n = jnp.sqrt(jnp.sum(v * v, axis=axis, keepdims=True))
            return v / jnp.maximum(n, eps)
        Bq, Sq, D = x.shape
        C = col_emb.shape[0]
        similarity = jnp.einsum('bsd,cd->bsc', _l2norm(x), _l2norm(col_emb))
        h = jax.nn.gelu(x @ gate_w1 + gate_b1, approximate=False)
        gate_values = jax.nn.sigmoid(h @ gate_w2 + gate_b2)
        logits = similarity + gate_values
        k = max(1, int(C * SPARSITY))
        _, top_idx = jax.lax.top_k(logits, k)
        mask = jnp.sum(jax.nn.one_hot(top_idx, C, dtype=logits.dtype), axis=-2)
        weights = mask * jax.nn.softmax(logits, axis=-1)
        cols = jax.nn.gelu(jnp.einsum('bsd,cdn->bscn', x, W_cols) + b_cols, approximate=False)
        cols = cols * weights[..., None]
        combined = cols.reshape(Bq, Sq, -1)
        y = combined @ proj_w + proj_b + x
        mu = jnp.mean(y, axis=-1, keepdims=True)
        var = jnp.mean((y - mu) ** 2, axis=-1, keepdims=True)
        out = (y - mu) * jax.lax.rsqrt(var + 1e-05) * ln_g + ln_b
        return out

    def _L3_xattn_ref(x, context, context_mask, Wq, Wk, Wv, Wo):
        import jax, jax.numpy as jnp
        import numpy as np
        DIM = 128
        CTX_DIM = 96
        HEADS = 16
        B, N, _ = x.shape
        M = context.shape[1]
        hd = DIM // HEADS
        scale = hd ** (-0.5)
        q = (x @ Wq).reshape(B, N, HEADS, hd).transpose(0, 2, 1, 3)
        k = (context @ Wk).reshape(B, M, HEADS, hd).transpose(0, 2, 1, 3)
        v = (context @ Wv).reshape(B, M, HEADS, hd).transpose(0, 2, 1, 3)
        scores = jnp.einsum('bhid,bhjd->bhij', q, k) * scale
        max_neg = -jnp.finfo(scores.dtype).max
        scores = jnp.where(context_mask[:, None, None, :], scores, max_neg)
        attn = jax.nn.softmax(scores, axis=-1)
        out = jnp.einsum('bhij,bhjd->bhid', attn, v)
        out = out.transpose(0, 2, 1, 3).reshape(B, N, DIM)
        return out @ Wo

    def _L3_ffn_ref(x, Wr, br, W_up, b_up, W_down, b_down):
        import jax, jax.numpy as jnp
        import numpy as np
        B, S, H = (4, 256, 128)
        E = 8
        GS = 2
        NG = E // GS
        F = int(H * 4 * (2.0 / 3.0))
        b, s, h = x.shape
        n_tok = b * s
        k = n_tok // E
        xf = x.reshape(n_tok, h)
        logits = xf @ Wr + br
        Sm = jax.nn.softmax(logits, axis=-1)
        G_t, idx_t = jax.lax.top_k(Sm.T, k)
        G = G_t.T
        idx = idx_t.T
        tokens = xf[idx]
        group = jnp.arange(E) // GS
        Wu = W_up[group]
        bu = b_up[group]
        mid = jax.nn.silu(jnp.einsum('keh,ehf->kef', tokens, Wu) + bu)
        out = jnp.einsum('kef,efh->keh', mid, W_down) + b_down
        y = jnp.zeros_like(xf).at[idx].add(G[..., None] * out)
        return y.reshape(b, s, h)
    x = x + jnp.tanh(g_xattn[0]) * _L0_xattn_ref(_layernorm(x, axis=-1), ctx_768, L0_xattn_Wq, L0_xattn_bq, L0_xattn_Wk, L0_xattn_bk, L0_xattn_Wv, L0_xattn_bv, L0_xattn_Wo, L0_xattn_bo)
    x = x + jnp.tanh(g_ffn[0]) * _L0_ffn_ref(_layernorm(x, axis=-1), L0_ffn_W_exp, L0_ffn_b_exp, L0_ffn_up_weights, L0_ffn_up_bias, L0_ffn_down_weights, L0_ffn_W_con, L0_ffn_b_con, L0_ffn_down_bias)
    x = x + jnp.tanh(g_xattn[1]) * _L1_xattn_ref(_layernorm(x, axis=-1), ctx_768, L1_xattn_Wq, L1_xattn_Wk, L1_xattn_Wv, L1_xattn_Wo, L1_xattn_bo, L1_xattn_q_down, L1_xattn_q_up, L1_xattn_q_alpha, L1_xattn_k_down, L1_xattn_k_up, L1_xattn_k_alpha, L1_xattn_v_down, L1_xattn_v_up, L1_xattn_v_alpha, L1_xattn_o_down, L1_xattn_o_up, L1_xattn_o_alpha, L1_xattn_Wk_ipa, L1_xattn_Wv_ipa)
    x = x + jnp.tanh(g_ffn[1]) * _L1_ffn_ref(_layernorm(x, axis=-1), L1_ffn_w_router, L1_ffn_w_up, L1_ffn_w_gate, L1_ffn_w_down, L1_ffn_ws_up, L1_ffn_ws_gate, L1_ffn_ws_down)
    x = x + jnp.tanh(g_xattn[2]) * _L2_xattn_ref(_layernorm(x, axis=-1), ctx_768, L2_xattn_Wq, L2_xattn_Wk, L2_xattn_Wv, L2_xattn_Wo, L2_xattn_bo)
    x = x + jnp.tanh(g_ffn[2]) * _L2_ffn_ref(_layernorm(x, axis=-1), L2_ffn_col_emb, L2_ffn_gate_w1, L2_ffn_gate_b1, L2_ffn_gate_w2, L2_ffn_gate_b2, L2_ffn_W_cols, L2_ffn_b_cols, L2_ffn_proj_w, L2_ffn_proj_b, L2_ffn_ln_g, L2_ffn_ln_b)
    x = x + jnp.tanh(g_xattn[3]) * _L3_xattn_ref(_layernorm(x, axis=-1), ctx_768, mask_BxS2_bf1, L3_xattn_Wq, L3_xattn_Wk, L3_xattn_Wv, L3_xattn_Wo)
    x = x + jnp.tanh(g_ffn[3]) * _L3_ffn_ref(_layernorm(x, axis=-1), L3_ffn_Wr, L3_ffn_br, L3_ffn_W_up, L3_ffn_b_up, L3_ffn_W_down, L3_ffn_b_down)
    return x

_drawn_inputs = setup_inputs


def setup_inputs(seed=0):
    import zlib

    import numpy as np

    out = dict(_drawn_inputs(seed))
    spreads = {'L0_xattn_bq': (0.0, 0.1),
     'L0_xattn_bk': (0.0, 2.0),
     'L0_xattn_bv': (0.0, 0.1),
     'L0_xattn_bo': (0.0, 0.1),
     'L0_ffn_b_exp': (0.0, 0.1),
     'L0_ffn_up_bias': (0.0, 0.1),
     'L0_ffn_b_con': (0.0, 0.1),
     'L0_ffn_down_bias': (0.0, 0.1),
     'L1_xattn_bo': (0.0, 0.1),
     'L2_ffn_gate_b1': (0.0, 0.341),
     'L2_ffn_gate_b2': (0.0, 0.427),
     'L2_ffn_b_cols': (0.0, 0.506),
     'L2_ffn_proj_b': (0.0, 0.1),
     'L2_ffn_ln_g': (1.0, 0.2),
     'L2_ffn_ln_b': (0.0, 0.1),
     'L3_ffn_br': (0.0, 0.1)}
    factors = {'g_ffn': 25.624,
     'L1_xattn_Wq': 5.327,
     'L1_xattn_Wk': 8.0,
     'L1_xattn_q_down': 8.0,
     'L1_xattn_q_up': 8.0,
     'L1_xattn_k_down': 8.0,
     'L1_xattn_k_up': 8.0,
     'L1_xattn_v_down': 2.867,
     'L1_xattn_v_up': 2.913,
     'L1_xattn_Wk_ipa': 4.91,
     'L2_xattn_bo': 3.105,
     'L3_ffn_b_up': 8.0,
     'L3_ffn_b_down': 8.0}
    for name, (base, spread) in spreads.items():
        noise = np.random.default_rng([zlib.crc32(name.encode()), seed]).standard_normal(out[name].shape)
        drawn = base * np.exp(spread * noise) if base else spread * noise
        out[name] = jnp.asarray(drawn.astype(out[name].dtype))
    for name, factor in factors.items():
        out[name] = (out[name] * factor).astype(out[name].dtype)
    return out
```

```python
from contextlib import ExitStack

import numpy as np

import concourse.bass as bass
from concourse import mybir

ALU = mybir.AluOpType
ACT = mybir.ActivationFunctionType
AXX = mybir.AxisListType.X
F32 = mybir.dt.float32
F16 = mybir.dt.float16
BF16 = mybir.dt.bfloat16
U8 = mybir.dt.uint8
U32 = mybir.dt.uint32
I32 = mybir.dt.int32

P = 128
B, SQ, D = 8, 256, 128
SK, DC = 512, 96
QT = SQ // P
KC = SK // P
NT = B * QT
HEADS = 16
HG = 4
NG = HEADS // HG
EPS = 1e-5
CLAMP = 10000.0
IPA = 4
RANK = 32
HIDE_ROW, HIDE_KEY = 30000.0, -30000.0
MASK_Q, MASK_K = 60000.0, 60000.0


SEMAPHORES = []


def alloc(nc, ctx, name):
    def sb(n, shape, dt=F32):
        return ctx.enter_context(nc.sbuf_tensor(f"{name}_{n}", shape, dt))

    def ps(n, shape, dt=F32):
        return ctx.enter_context(nc.psum_tensor(f"{name}_{n}", shape, dt))

    def sem(n):
        SEMAPHORES.append(nc.alloc_semaphore(f"{name}_{n}"))
        return SEMAPHORES[-1]
    return sb, ps, sem


def wait(eng, sem, value):
    if not isinstance(value, int) or value > 0:
        eng.wait_ge(sem, value)


def at_batch(ap, b):
    return ap[b] if isinstance(b, int) else ap[bass.ds(b, 1)].rearrange("a p n -> (a p) n")


class Shape:

    def __init__(self, name, wide, clip=False, ipa=False, bias=False, mask=False, out_bias=True, gate=0):
        self.name, self.wide, self.clip, self.ipa = name, wide, clip, ipa
        self.bias, self.mask, self.out_bias, self.gate = bias, mask, out_bias, gate
        self.dh = 64 if wide else D // HEADS
        self.scale = self.dh ** -0.5
        self.stacks = 6 if wide else 2
        self.v_pieces = 2 if wide else 1
        self.parts = 2 if wide else 1
        self.in_stack = not wide and not clip
        self.keys = SK - IPA if ipa else SK
        if wide:
            self.pieces = [[("V", 0), ("V", 1)], [("K", 0), ("K", 1)], [("K", 2), ("K", 3)], [("Q", 0), ("Q", 1)]]
        else:
            self.pieces = [[("V", 0)], [("K", 0)], [("Q", 0)], []]

    def slots(self, kind):
        out = []
        for g in range(NG):
            for s in range(HG):
                pcs = self.pieces[s] if not (kind == "last" and g >= NG - 2) else []
                tail = []
                if self.ipa and (g, s) == (0, 2):
                    tail.append(("VI",))
                if self.ipa and (g, s) == (1, 0):
                    tail.append(("G",))
                if self.ipa and (g, s) == (3, 1):
                    tail.append(("PT",))
                if (g, s) == (2, 1) and kind != "last":
                    tail.append(("XT",))
                more = not (kind == "last" and g == NG - 1)
                if s == HG - 1 and more:
                    tail += [("MT",)] + [("NB", i) for i in range(2)] * self.clip
                if (g, s) == (0, HG - 1) and kind != "first":
                    tail.append(("OP",))
                out.append((g, s, pcs[0] if pcs else None, pcs[1] if len(pcs) > 1 else None, more and s < 2, tail))
        return out

    def opening(self):
        first = [p for ps_ in self.pieces for p in ps_]
        return ([("XT",)] + [(0,) + p for p in first] + [(1,) + p for p in first]
                + [("MT",)] + [("NB", i) for i in range(2)] * self.clip)

    def order(self, kind):
        out = []
        for g, s, p1, p2, _, tail in self.slots(kind):
            out += [(g, s) + p for p in (p1, p2) if p] + [(g, s) + t for t in tail]
        return out

    def turn(self, kind, b, key):
        n0 = len(self.opening())
        if kind == "opening":
            return self.opening().index(key)
        pos = self.order(kind).index(key)
        nf, nm = len(self.order("first")), len(self.order("mid"))
        if kind == "first":
            return n0 + pos
        if kind == "last":
            return n0 + nf + (B - 2) * nm + pos
        return (b - 1) * nm + (n0 + nf + pos)

    def end_turn(self):
        return len(self.opening()) + len(self.order("first")) + (B - 2) * len(self.order("mid")) + len(self.order("last"))


def attention(nc, sh, dram, res, const):
    wide, clip, ipa = sh.wide, sh.clip, sh.ipa
    x_res, gates = res
    ident, identb, cvec, bsel, ones, eps = const
    with ExitStack() as ctx:
        sb, ps, sem = alloc(nc, ctx, sh.name)
        in_stack = sh.in_stack
        rows = DC + 2 if sh.mask else DC + 1 if sh.bias else DC

        if wide:
            inner = HEADS * sh.dh
            wq, wk, wv = (sb(n, [P, inner]) for n in ("wq", "wk", "wv"))
            wo = sb("wo", [P, inner // P, D])
            if ipa:
                wki, wvi = sb("wki", [P, inner]), sb("wvi", [P, inner])
                lora_up = {n: sb(f"{n}_up", [RANK, inner]) for n in "qkv"}
                lora_dn = {n: sb(f"{n}_dn", [RANK, D]) for n in "qkv"}
                o_dn, o_up = sb("o_dn", [RANK, inner]), sb("o_up", [RANK, D])
                alpha = sb("alpha", [P, 4])
            v_ipa = sb("v_ipa", [P, HEADS // 2, 64]) if ipa else None
            g_ipa = sb("g_ipa", [64, D]) if ipa else None
            s_ipa = sb("s_ipa", [P, QT, HEADS, IPA]) if ipa else None
            e_ipa = sb("e_ipa", [P, QT * HEADS, IPA]) if ipa else None
            m_ipa = sb("m_ipa", [P, QT * HEADS]) if ipa else None
            r_ipa = sb("r_ipa", [P, QT * HEADS]) if ipa else None
            p_ipa = sb("p_ipa", [P, QT * HEADS, IPA]) if ipa else None
            pt_ipa = sb("pt_ipa", [64, SQ]) if ipa else None
        else:
            wq_in, wk_in = sb("wq_in", [P, D]), sb("wk_in", [P, D])
            wv = sb("wv", [P, D])
            wq, wk = sb("wq", [P, NG, P]), sb("wk", [P, NG, P])
            wo = sb("wo", [P, NG, D])
            q_row = sb("q_row", [1, NG, P])
        bo = sb("bo", [1, D]) if sh.out_bias else None
        sel = sb("sel", [32, HG, 2, P], F16)

        ctx_in = sb("ctx_in", [P, SK])
        ctxb = sb("ctxb", [P, SK])
        stats = sb("stats", [P, QT, 6])
        mv = sb("mv", [P, QT, 2])
        lnv = sb("lnv", [P, QT])
        rstd = sb("rstd", [P, QT])
        xn = sb("xn", [P, QT, D])
        xnT = sb("xnT", [P, SQ])
        chi = sb("chi", [P, SK], F16)
        kst = [sb(f"kst{i}", [P, 2, HG, SK] if wide else [P, SK], F16) for i in range(4)]
        qst = [sb(f"qst{i}", [P, HG, SQ] if wide else [P, SQ], F16) for i in range(4)]
        vst = [sb(f"vst{i}", [P, KC, HG * 64] if wide else [P, KC, HG, 32]) for i in range(4)]
        neg_max = sb("neg_max", [P, HG, QT])
        rest = sb("rest", [P, HG, QT])
        if in_stack:
            shift_parts = sb("shift_parts", [P, QT, HG, 32], F16)
        else:
            max_parts = sb("max_parts", [P, QT, 3, HG], BF16)
        mt = [sb(f"mt{i}", [32, SQ], BF16) for i in range(2)]
        probs = [sb(f"probs{i}", [P, KC, SQ]) for i in range(2 * HG)]
        attn = sb("attn", [P, HEADS * (64 if wide else 32) // P, SQ])
        r_sum = sb("r_sum", [P, SQ])
        if wide:
            fold = sb("fold", [P, 2, SQ])
            folded = [sb(f"folded{i}", [P, SQ]) for i in range(2 * HG)]
        else:
            u_sb = sb("u_sb", [P, SQ])
        if clip:
            shift = [sb(f"shift{i}", [P, HG, SQ]) for i in range(2)]
            zs = [sb(f"zs{i}", [P, KC, SQ]) for i in range(2)]

        rowmax_ps = ps("rowmax_ps", [P, QT, SK])
        st_ps = [ps(f"st_ps{i}", [P, KC, SQ]) for i in range(2)]
        u_ps = ps("u_ps", [P, 2, SQ])
        bank = ps("bank", [P, 512])

        loaded = sem("loaded")
        weights_ok = sem("weights_ok")
        preset = sem("preset")
        lora_ready = sem("lora_ready")
        ctx_loaded = sem("ctx_loaded")
        ctx_ready = sem("ctx_ready")
        stats_ready = sem("stats_ready")
        rstd_ready = sem("rstd_ready")
        xn_ready = sem("xn_ready")
        bank_full = sem("bank_full")
        bank_free = sem("bank_free")
        hi_ready = sem("hi_ready")
        rows_ready = sem("rows_ready")
        max_ready = sem("max_ready")
        parts_step = sem("parts_step")
        parts_ready = sem("parts_ready")
        z_ready = sem("z_ready")
        st_ready = sem("st_ready")
        exp_ready = sem("exp_ready")
        fold_step = sem("fold_step")
        pool_ready = sem("pool_ready")
        pv_ready = sem("pv_ready")
        u_ready = sem("u_ready")
        div_ready = sem("div_ready")
        rsum_ready = sem("rsum_ready")
        attn_ready = sem("attn_ready")
        passed = sem("passed")
        pool_passed = sem("pool_passed")
        pe_passed = sem("pe_passed")
        ipa_step = sem("ipa_step")
        ipa_exp = sem("ipa_exp")

        def batches(body, eng):
            body("first", 0)
            with eng.Fori(1, B - 1) as b:
                body("mid", b)
            body("last", B - 1)

        def shift_turn(kind, b, g):
            name = ("NB", 1) if clip else ("MT",)
            if g:
                return sh.turn(kind, b, (g - 1, HG - 1) + name) + 1
            if kind == "first":
                return len(sh.opening())
            return sh.turn(kind, b, sh.order(kind)[0])

        def lora_ps(i):
            if i < 4:
                return st_ps[i // 2][:, :, :].rearrange("p c q -> p (c q)")[:, (i % 2) * 512:(i % 2 + 1) * 512]
            if i < 6:
                return rowmax_ps[:, i - 4, :]
            return u_ps[:, :, :].rearrange("p a q -> p (a q)") if i == 6 else bank[:, :]

        def stats_of(dve, b):
            x = x_of(b)
            for t in range(QT):
                ins = dve.bn_stats(stats[:, t, :], x[:, t, :])
            ins.then_inc(stats_ready, 1)
            dve.wait_ge(stats_ready, 2 * b + 1)
            dve.sem_inc(passed, 1)
            for t in range(QT):
                ins = dve.bn_aggr(mv[:, t, :], stats[:, t, :])
            ins.then_inc(stats_ready, 1)

        def x_of(b):
            return x_res[:, b * QT:(b + 1) * QT, :] if isinstance(b, int) else x_res[:, bass.ds(b * QT, QT), :]

        block = ctx.enter_context(nc.Block())

        n_loads = 0

        @block.sync
        def _(sp):
            nonlocal n_loads

            def load(dst, src):
                nonlocal n_loads
                n_loads += 1
                sp.dma_start(dst, src).then_inc(loaded, 16)

            def load_ctx(b):
                sp.dma_start(ctx_in[0:DC, :], at_batch(dram["ctxT"], b)).then_inc(ctx_loaded, 16)
                if rows > DC:
                    src = at_batch(dram["mask_row"], b) if sh.mask else dram["ones_row"]
                    sp.dma_start(ctx_in[DC:DC + 1, :], src).then_inc(ctx_loaded, 16)
                if rows > DC + 1:
                    sp.dma_start(ctx_in[DC + 1:DC + 2, :], dram["ones_row"]).then_inc(ctx_loaded, 16)

            load_ctx(0)
            load(sel[:, :, :, :], dram["sel"])
            if wide:
                load(wq[:, :], dram["Wq"])
                load(wk[0:DC, :], dram["Wk"])
                load(wv[0:DC, :], dram["Wv"])
                load(wo[:, :, :], dram["Wo"].rearrange("(i p) n -> p i n", p=P))
                if ipa:
                    load(wki[0:DC, :], dram["Wk_ipa"])
                    load(wvi[0:DC, :], dram["Wv_ipa"])
                    for n in "qkv":
                        load(lora_up[n][:, :], dram[f"{n}_up"])
                        load(lora_dn[n][:, 0:D if n == "q" else DC], dram[f"{n}_downT"])
                    load(o_up[:, :], dram["o_up"])
                    load(o_dn[:, :], dram["o_downT"])
                    for i, n in enumerate("qkvo"):
                        load(alpha[:, i:i + 1], dram[f"{n}_alpha"].partition_broadcast(P))
            else:
                load(wq_in[:, :], dram["Wq"])
                load(wk_in[0:DC, :], dram["Wk"])
                load(wv[0:DC, :], dram["Wv"])
                if sh.bias:
                    load(wk_in[DC:DC + 1, :], dram["bk"].unsqueeze(0))
                    load(wv[DC:DC + 1, :], dram["bv"].unsqueeze(0))
                sp.wait_ge(preset, 1)
                for j in range(HG):
                    load(wo[32 * j:32 * j + sh.dh, :, :],
                         dram["Wo"].rearrange("(g j d) n -> j d g n", g=NG, j=HG)[j])
                if sh.bias:
                    qv = q_row[:, :, :].rearrange("a g (j s d) -> a g j s d", j=HG, s=4)
                    for s in range(3):
                        for g in range(NG):
                            load(qv[:, g, :, s, :], dram["bq"].rearrange("(a g j d) -> a g j d", a=1, g=NG, j=HG)[:, g])
                else:
                    load(q_row[:, :, :], dram["mask_q_row"])
                if sh.mask:
                    load(wk[DC:DC + 1, :, :], dram["mask_k_row"])
                    load(wk[DC + 1:DC + 2, :, :], dram["shift_k_row"])
            if sh.out_bias:
                load(bo[:, :], dram["bo"].unsqueeze(0))

            def body(kind, b):
                if kind != "last":
                    sp.wait_ge(ctx_ready, b + 1)
                    load_ctx(b + 1)
            batches(body, sp)

        n_loads = sum([1, 4 * wide, ipa * (2 + 6 + 2 + 4), (not wide) * (3 + HG + 2 * sh.bias), sh.bias * 12,
                       (not wide and not sh.bias) * 1, sh.mask * 2, sh.out_bias * 1])
        ctx_dmas = 16 * (1 + rows - DC)

        @block.gpsimd
        def _(pool):
            def copy_ctx(b):
                pool.wait_ge(ctx_loaded, (b + 1) * ctx_dmas)
                pool.sem_inc(pool_passed, 1)
                pool.tensor_copy(ctxb[0:rows, :], ctx_in[0:rows, :]).then_inc(ctx_ready, 1)

            copy_ctx(0)

            def body(kind, b):
                for g, s, *_ in sh.slots(kind):
                    n = (b * NG + g) * HG + s
                    pr = probs[(g % 2) * HG + s]
                    if clip or wide:
                        pool.wait_ge(exp_ready, n + 1)
                    if clip:
                        pool.sem_inc(pool_passed, 1)
                    if clip:
                        pool.tensor_scalar(pr[:, :, :], pr[:, :, :], 1.0, 0.0, ALU.min, ALU.max).then_inc(pool_ready, 1)
                    elif wide:
                        wait(pool, pool_ready, n)
                        pool.tensor_tensor(fold[:, :, :], pr[:, 0:2, :], pr[:, 2:4, :], ALU.add).then_inc(fold_step, 1)
                        pool.wait_ge(fold_step, n + 1)
                        pool.tensor_tensor(folded[(g % 2) * HG + s][:, :], fold[:, 0, :], fold[:, 1, :],
                                           ALU.add).then_inc(pool_ready, 1)
                    if (g, s) == (1, HG - 1) and kind != "last":
                        last = (1, 2, "K", 3) if wide else (1, 1, "K", 0)
                        pool.wait_ge(bank_full, sh.turn(kind, b, last) + 1)
                        copy_ctx(b + 1)
            batches(body, pool)

        @block.scalar
        def _(act):
            def ln_rstd(b):
                act.wait_ge(stats_ready, 2 * (b + 1))
                act.activation(lnv[:, :], mv[:, :, 1], ACT.Ln, bias=eps[:, 0:1]).then_inc(rstd_ready, 1)
                act.wait_ge(rstd_ready, 2 * b + 1)
                act.activation(rstd[:, :], lnv[:, :], ACT.Exp, scale=-0.5).then_inc(rstd_ready, 1)

            def evacuate(kind, b, key, u, what):
                turn = sh.turn(kind, b, key)
                name = what[0]
                if name in ("MT", "OP"):
                    return
                act.wait_ge(bank_full, turn + 1)
                ub = u % 4 if isinstance(u, int) else what[-1]
                if name == "V":
                    i = what[1]
                    if wide:
                        act.copy(vst[ub][:, 2 * i:2 * i + 2, :], bank[:, :].rearrange("p (c n) -> p c n", c=2))\
                           .then_inc(bank_free, 1)
                    else:
                        act.copy(vst[ub][:, :, :, 0:sh.dh],
                                 bank[:, 0:KC * 32].rearrange("p (c h d) -> p c h d", c=KC, h=HG)).then_inc(bank_free, 1)
                elif name == "K":
                    if wide:
                        act.copy(kst[ub][:, 0, what[1], :], bank[:, :]).then_inc(hi_ready, 1)
                    else:
                        act.activation(chi[:, :], bank[:, :], ACT.Copy, scale=cvec[:, 0:1]).then_inc(hi_ready, 1)
                elif name == "Q":
                    n = 2 * SQ if wide else SQ
                    col = 2 if wide else 1
                    act.activation(chi[:, 0:n], bank[:, 0:n], ACT.Copy, scale=cvec[:, col:col + 1]).then_inc(hi_ready, 1)
                elif name == "XT":
                    act.copy(xnT[:, :], bank[:, 0:SQ]).then_inc(bank_free, 1)
                elif name == "NB":
                    i = what[1]
                    act.copy(shift[what[-1] % 2][:, 2 * i:2 * i + 2, :],
                             bank[:, :].rearrange("p (h q) -> p h q", h=2)).then_inc(bank_free, 1)
                elif name == "VI":
                    src = bank[:, 0:HEADS // 2 * IPA].rearrange("p (i t) -> p i t", t=IPA)
                    flat = v_ipa[:, :, :].rearrange("p i n -> p (i n)")
                    for hh in range(2):
                        for i in range(HEADS // 2):
                            at = i * 64 + (2 * i + hh) * IPA
                            ins = act.copy(flat[64 * hh:64 * hh + 64, at:at + IPA], src[64 * hh:64 * hh + 64, i, :])
                    ins.then_inc(bank_free, 1)
                elif name == "G":
                    act.copy(g_ipa[:, :], bank[0:64, 0:D]).then_inc(bank_free, 1)
                elif name == "PT":
                    act.copy(pt_ipa[:, :], bank[0:64, 0:SQ]).then_inc(bank_free, 1)

            ln_rstd(0)
            for key in sh.opening():
                if key[0] in (0, 1):
                    evacuate("opening", 0, key, key[0], key[1:])
                else:
                    evacuate("opening", 0, key, 0, key + (0,))

            def body(kind, b):
                for g, s, p1, p2, more, tail in sh.slots(kind):
                    n = (b * NG + g) * HG + s
                    if p1:
                        evacuate(kind, b, (g, s) + p1, None, p1 + ((g + 2) % 4,))
                    act.wait_ge(z_ready if clip else st_ready, n + 1)
                    src = zs[s % 2] if clip else st_ps[s % 2]
                    act.activation(probs[(g % 2) * HG + s][:, :, :], src[:, :, :], ACT.Exp, scale=sh.scale)\
                       .then_inc(exp_ready, 1)
                    if p2:
                        evacuate(kind, b, (g, s) + p2, None, p2 + ((g + 2) % 4,))
                    if not wide and s == 1 and not (kind == "first" and g == 0):
                        act.wait_ge(pv_ready, b * NG + g)
                        act.copy(u_sb[:, :], u_ps[:, 0, :]).then_inc(u_ready, 1)
                    for t in tail:
                        evacuate(kind, b, (g, s) + t, None, t + ((g + 1) % 4,))
                    if (g, s) == (0, HG - 1) and kind != "last":
                        ln_rstd(b + 1)
                    if ipa and (g, s) == (2, HG - 1):
                        act.wait_ge(ipa_step, 5 * b + 2)
                        act.activation(e_ipa[:, :, :], s_ipa[:, :, :, :].rearrange("p a h t -> p (a h) t"), ACT.Exp,
                                       scale=sh.scale).then_inc(ipa_exp, 1)
            batches(body, act)
            if not wide:
                act.wait_ge(pv_ready, B * NG)
                act.copy(u_sb[:, :], u_ps[:, 0, :]).then_inc(u_ready, 1)

        @block.tensor
        def _(pe):
            full = bank[:, :]

            def use(kind, b, key, u, what):
                name = what[0]
                wait(pe, bank_free, sh.turn(kind, b, key))
                if name == "V":
                    i = what[1]
                    if wide:
                        for c in range(2):
                            at = (2 * i + c) * P
                            ins = pe.matmul(bank[:, c * 256:(c + 1) * 256], ctxb[0:DC, at:at + P],
                                            wv[0:DC, u * 256:(u + 1) * 256], start=True, stop=True)
                    else:
                        r = DC + 1 if sh.bias else DC
                        for c in range(KC):
                            ins = pe.matmul(bank[:, c * 32:(c + 1) * 32], ctxb[0:r, c * P:(c + 1) * P],
                                            wv[0:r, u * 32:(u + 1) * 32], start=True, stop=True)
                elif name == "K":
                    if wide:
                        h = u * HG + what[1]
                        for half in (bank[0:64, :], bank[64:P, :]):
                            ins = pe.matmul(half[:, 0:sh.keys], wk[0:DC, h * 64:(h + 1) * 64], ctxb[0:DC, 0:sh.keys],
                                            start=True, stop=True)
                        if ipa:
                            for half in (bank[0:64, :], bank[64:P, :]):
                                ins = pe.matmul(half[:, sh.keys:SK], wki[0:DC, h * 64:(h + 1) * 64],
                                                ctxb[0:DC, sh.keys:SK], start=True, stop=True)
                    else:
                        ins = pe.matmul(full, wk[0:rows, u, :], ctxb[0:rows, :], start=True, stop=True)
                elif name == "Q":
                    if wide:
                        for j in range(2):
                            h = u * HG + 2 * what[1] + j
                            for half in (bank[0:64, :], bank[64:P, :]):
                                ins = pe.matmul(half[:, j * SQ:(j + 1) * SQ], wq[:, h * 64:(h + 1) * 64], xnT[:, :],
                                                start=True, stop=True)
                    else:
                        pe.matmul(bank[:, 0:SQ], wq[:, u, :], xnT[:, :], start=True, stop=False)
                        ins = pe.matmul(bank[:, 0:SQ], q_row[0:1, u, :], ones[0:1, 0:SQ], start=False, stop=True)
                elif name == "XT":
                    pe.wait_ge(xn_ready, b_next(kind, b))
                    for t in range(QT):
                        ins = pe.transpose(bank[:, t * P:(t + 1) * P], xn[:, t, :], ident[:, :])
                elif name == "MT":
                    pe.wait_ge(parts_ready, unit_next(kind, b, key) + 1)
                    if in_stack:
                        for t in range(QT):
                            ins = pe.transpose(bank[:, :].bitcast(F16)[:, t * P:(t + 1) * P],
                                               shift_parts[:, t, :, :].rearrange("p h k -> p (h k)"), dram["identh"][:, :])
                        ins.then_inc(bank_full, 1)
                        return
                    view = bank[:, :].bitcast(BF16)
                    for t in range(QT):
                        ins = pe.transpose(view[0:12, t * P:(t + 1) * P],
                                           max_parts[:, t, :, :].rearrange("p k h -> p (k h)"), identb[:, :])
                elif name == "NB":
                    g1 = (key[0] + 1) % 4 if kind != "opening" else 0
                    for j in range(2):
                        ins = pe.matmul(bank[:, j * SQ:(j + 1) * SQ], sel[0:13, 2 * what[1] + j, 0, :],
                                        mt[g1 % 2][0:13, :], start=True, stop=True)
                elif name == "VI":
                    for i in range(HEADS // 2):
                        ins = pe.matmul(bank[:, i * IPA:(i + 1) * IPA], wvi[0:DC, i * P:(i + 1) * P],
                                        ctxb[0:DC, sh.keys:SK], start=True, stop=True)
                elif name == "G":
                    for i in range(HEADS // 2):
                        ins = pe.matmul(bank[0:64, 0:D], v_ipa[:, i, :], wo[:, i, :],
                                        start=(i == 0), stop=(i == HEADS // 2 - 1))
                elif name == "PT":
                    pe.wait_ge(ipa_step, 5 * b + 5)
                    pe.sem_inc(pe_passed, 1)
                    for t in range(QT):
                        ins = pe.transpose(bank[0:64, t * P:(t + 1) * P],
                                           p_ipa[:, t * HEADS:(t + 1) * HEADS, :].rearrange("p h t -> p (h t)"),
                                           ident[:, :])
                elif name == "OP":
                    ins = out_projection(b * NG * sh.parts)
                ins.then_inc(bank_full, 1)

            def b_next(kind, b):
                return 1 if kind == "opening" else b + 2

            def unit_next(kind, b, key):
                return 0 if kind == "opening" else b * NG + key[0] + 1

            def out_projection(parts_before):
                pe.wait_ge(attn_ready, parts_before)
                chunks = attn.shape[1]
                for t in range(QT):
                    dst = bank[:, t * D:(t + 1) * D]
                    rest_ = (1 if ipa else 0) + (1 if bo is not None else 0)
                    for i in range(chunks):
                        ins = pe.matmul(dst, attn[:, i, t * P:(t + 1) * P], wo[:, i, :],
                                        start=(i == 0), stop=(i == chunks - 1 and rest_ == 0))
                    if ipa:
                        ins = pe.matmul(dst, pt_ipa[:, t * P:(t + 1) * P], g_ipa[:, :], start=False, stop=(bo is None))
                    if bo is not None:
                        ins = pe.matmul(dst, ones[0:1, 0:P], bo[0:1, :], start=False, stop=True)
                return ins

            def row_scores(ub, u, h):
                wait(pe, max_ready, u * HG + h)
                for t in range(QT):
                    if wide:
                        ins = pe.matmul(rowmax_ps[:, t, :], qst[ub][:, h, t * P:(t + 1) * P], kst[ub][:, 0, h, :],
                                        start=True, stop=not ipa)
                        if ipa:
                            ins = pe.matmul(rowmax_ps[:, t, sh.keys:SK], qst[ub][:, h, t * P:(t + 1) * P],
                                            kst[ub][:, 1, h, sh.keys:SK], start=False, stop=True)
                    else:
                        r = slice(32 * h, 32 * h + 32)
                        ins = pe.matmul(rowmax_ps[:, t, :], qst[ub][r, t * P:(t + 1) * P], kst[ub][r, :],
                                        start=True, stop=True)
                ins.then_inc(rows_ready, 1)

            def key_scores(ub, u, h):
                wait(pe, z_ready if clip else exp_ready, u * HG + h - 1)
                for c in range(KC):
                    dst = st_ps[h % 2][:, c, :]
                    k = slice(c * P, (c + 1) * P)
                    if wide:
                        pe.matmul(dst, kst[ub][:, 0, h, k], qst[ub][:, h, :], start=True, stop=False)
                        pe.matmul(dst, kst[ub][:, 1, h, k], qst[ub][:, h, :], start=False, stop=False)
                    else:
                        r = slice(32 * h, 32 * h + 32)
                        ins = pe.matmul(dst, kst[ub][r, k], qst[ub][r, :], start=True, stop=True)
                    if wide:
                        hide = 1 if (ipa and c == KC - 1) else 0
                        ins = pe.matmul(dst, sel[0:13, h, hide, :], mt[ub % 2][0:13, :], start=False, stop=True)
                ins.then_inc(st_ready, 1)

            def values(ub, u, part):
                wait(pe, attn_ready, sh.parts * u + part)
                heads = range(2 * part, 2 * part + 2) if wide else range(HG)
                w = 64 if wide else 32
                pe.wait_ge(pool_ready if (clip or wide) else exp_ready, u * HG + heads[-1] + 1)
                for c in range(KC):
                    for n, h in enumerate(heads):
                        lhs = vst[ub][:, c, h * 64:(h + 1) * 64] if wide else vst[ub][:, c, h, :]
                        ins = pe.matmul(u_ps[w * n:w * n + w, 0, :], lhs, probs[(ub % 2) * HG + h][:, c, :],
                                        start=(c == 0), stop=(c == KC - 1), skip_group_check=True)
                if wide:
                    for n, h in enumerate(heads):
                        ins = pe.matmul(u_ps[w * n:w * n + w, 1, :], ones[:, 0:64], folded[(ub % 2) * HG + h][:, :],
                                        start=True, stop=True)
                ins.then_inc(pv_ready, 1)

            def divisors(u):
                pe.wait_ge(u_ready, u + 1)
                pe.matmul(u_ps[:, 1, :], bsel[:, :], u_sb[:, :], start=True, stop=True).then_inc(div_ready, 1)

            pe.wait_ge(loaded, 16 * n_loads)
            if ipa:
                for i, n in enumerate("qkv"):
                    r = D if n == "q" else DC
                    for half in range(2):
                        pe.matmul(lora_ps(2 * i + half)[0:r, :], lora_dn[n][:, 0:r],
                                  lora_up[n][:, half * 512:(half + 1) * 512], start=True, stop=True)
                for i in range(HEADS // 2):
                    ins = pe.matmul(lora_ps(6 + i // 4)[:, (i % 4) * D:(i % 4 + 1) * D],
                                    o_dn[:, i * P:(i + 1) * P], o_up[:, :], start=True, stop=True)
                ins.then_inc(lora_ready, 1)
            if ipa or not wide:
                pe.wait_ge(weights_ok, 1)
            pe.wait_ge(ctx_ready, 1)
            for key in sh.opening():
                if key[0] == "MT":
                    pe.wait_ge(bank_free, sh.turn("opening", 0, key))
                    for h in range(HG):
                        row_scores(0, 0, h)
                use("opening", 0, key, key[0] if key[0] in (0, 1) else 0, key[1:] if key[0] in (0, 1) else key)

            def body(kind, b):
                for g, s, p1, p2, more, tail in sh.slots(kind):
                    u = b * NG + g
                    g2 = (g + 2) % 4
                    if (g, s) == (2, 0) and kind != "last":
                        pe.wait_ge(ctx_ready, b + 2)
                    if p1:
                        use(kind, b, (g, s) + p1, g2, p1)
                    if more:
                        row_scores((g + 1) % 4, u + 1, 2 * s)
                    if s == 0:
                        pe.wait_ge(bank_free, shift_turn(kind, b, g))
                    key_scores(g, u, s)
                    if p2:
                        use(kind, b, (g, s) + p2, g2, p2)
                    if more:
                        row_scores((g + 1) % 4, u + 1, 2 * s + 1)
                    if not (kind == "first" and g == 0):
                        if wide and s in (0, 2):
                            values((g - 1) % 4, u - 1, s // 2)
                        if not wide and s == 1:
                            values((g - 1) % 4, u - 1, 0)
                        if not wide and s == 2:
                            divisors(u - 1)
                    for t in tail:
                        use(kind, b, (g, s) + t, None, t)
            batches(body, pe)
            for part in range(sh.parts):
                values(3, B * NG - 1, part)
            if not wide:
                divisors(B * NG - 1)
            wait(pe, bank_free, sh.end_turn())
            out_projection(B * NG * sh.parts).then_inc(bank_full, 1)

        @block.vector
        def _(dve):
            for m in mt:
                ins = dve.memset(m[:, :], HIDE_ROW)
            if in_stack:
                ins = dve.memset(shift_parts[:, :, :, :], 0.0)
            if ipa:
                ins = dve.memset(v_ipa[:, :, :], 0.0)
            if not wide:
                for w in [wq, wk, wo, q_row] + vst:
                    ins = dve.memset(w[tuple(slice(None) for _ in w.shape)], 0.0)
            ins.then_inc(preset, 1)
            if not wide:
                dve.wait_ge(preset, 1)
                for v in vst:
                    ins = dve.memset(v[:, :, :, sh.dh:sh.dh + 1], 1.0)
                ins.then_inc(preset, 1)
            stats_of(dve, 0)
            dve.wait_ge(loaded, 16 * n_loads)
            if ipa:
                dve.tensor_scalar(alpha[:, :], alpha[:, :], 1.0 / RANK, None, ALU.mult).then_inc(preset, 1)
                dve.wait_ge(preset, 2)
                dve.wait_ge(lora_ready, 1)
                for i, (w, r) in enumerate(((wq, D), (wk, DC), (wv, DC))):
                    for half in range(2):
                        cols = w[0:r, half * 512:(half + 1) * 512]
                        dve.scalar_tensor_tensor(cols, lora_ps(2 * i + half)[0:r, :], alpha[0:r, i:i + 1], cols,
                                                 ALU.mult, ALU.add)
                for i in range(2):
                    four = wo[:, 4 * i:4 * i + 4, :].rearrange("p i n -> p (i n)")
                    ins = dve.scalar_tensor_tensor(four, lora_ps(6 + i), alpha[:, 3:4], four, ALU.mult, ALU.add)
            elif not wide:
                for w, w_in, r in ((wq, wq_in, P), (wk, wk_in, DC + 1 if sh.bias else DC)):
                    dst = w[0:r, :, :].rearrange("p g (j s d) -> p (g j) s d", j=HG, s=4)
                    src = w_in[0:r, :].rearrange("p (h d) -> p h d", d=sh.dh)
                    for s in range(3):
                        ins = dve.tensor_copy(dst[:, :, s, :], src)
            if ipa or not wide:
                ins.then_inc(weights_ok, 1)

            def pair(kind, b, key, what, unit):
                name, i = what
                idx = i if name == "K" else sh.stacks - (2 if wide else 1) + i
                ub = (key[0] + 2) % 4 if kind != "opening" else key[0]
                dve.wait_ge(bank_full, sh.turn(kind, b, key) + 1)
                dve.wait_ge(hi_ready, sh.stacks * unit + idx + 1)
                if name == "K":
                    if wide:
                        hi, dst = kst[ub][:, 0, i, :], kst[ub][:, 1, i, :]
                    else:
                        hi, dst = chi[:, :], kst[ub][:, :]
                    src = bank[:, :]
                elif wide:
                    src, hi = (t[:, :].rearrange("p (h q) -> p h q", h=2) for t in (bank, chi))
                    dst = qst[ub][:, 2 * i:2 * i + 2, :]
                else:
                    src, hi, dst = bank[:, 0:SQ], chi[:, 0:SQ], qst[ub][:, :]
                dve.tensor_tensor(dst, src, hi, ALU.subtract).then_inc(bank_free, 1)

            def normalise(b):
                dve.wait_ge(rstd_ready, 2 * (b + 1))
                x = x_of(b)
                for t in range(QT):
                    ins = dve.tensor_scalar(xn[:, t, :], x[:, t, :], mv[:, t, 0:1], rstd[:, t:t + 1],
                                            ALU.subtract, ALU.mult)
                ins.then_inc(xn_ready, 1)

            def row_max(g1, u1, h):
                dve.wait_ge(rows_ready, u1 * HG + h + 1)
                ins = dve.tensor_reduce(neg_max[:, h, :], rowmax_ps[:, :, 0:sh.keys], AXX, ALU.max, negate=True)
                if ipa:
                    ins = dve.tensor_copy(s_ipa[:, :, g1 * HG + h, :], rowmax_ps[:, :, sh.keys:SK])
                ins.then_inc(max_ready, 1)

            def split_max(u1):
                steps = 3 if wide else 4
                at = 0
                dve.wait_ge(max_ready, u1 * HG + HG)
                if clip:
                    bound = CLAMP / sh.scale
                    dve.tensor_scalar(neg_max[:, :, :], neg_max[:, :, :], -bound, bound, ALU.max, ALU.min)\
                       .then_inc(parts_step, 1)
                    at = 1
                    dve.wait_ge(parts_step, u1 * steps + at)
                if in_stack:
                    dve.tensor_scalar(neg_max[:, :, :], neg_max[:, :, :], 1.0 / MASK_K, None, ALU.mult).then_inc(parts_step, 1)
                    at = 1
                    dve.wait_ge(parts_step, u1 * steps + at)
                part = [shift_parts[:, :, :, 25 + k] if in_stack else max_parts[:, :, k, :] for k in range(3)]
                turned = neg_max[:, :, :].rearrange("p h t -> p t h")
                left = rest[:, :, :].rearrange("p h t -> p t h")
                dve.tensor_copy(part[0], turned).then_inc(parts_step, 1)
                dve.wait_ge(parts_step, u1 * steps + at + 1)
                dve.tensor_tensor(left, turned, part[0], ALU.subtract).then_inc(parts_step, 1)
                dve.wait_ge(parts_step, u1 * steps + at + 2)
                dve.tensor_copy(part[1], left).then_inc(parts_step, 1)
                dve.wait_ge(parts_step, u1 * steps + at + 3)
                dve.tensor_tensor(part[2], left, part[1], ALU.subtract)\
                   .then_inc(parts_ready, 1)

            def clipped(g, s, n):
                dve.wait_ge(st_ready, n + 1)
                wait(dve, exp_ready, n - 1)
                dve.scalar_tensor_tensor(zs[s % 2][:, :, :], st_ps[s % 2][:, :, :], -CLAMP / sh.scale,
                                         shift[g % 2][:, s:s + 1, :].broadcast_to([P, KC, SQ]), ALU.max, ALU.add)\
                   .then_inc(z_ready, 1)

            def divide(g, u, part):
                n = u * sh.parts + part
                dve.wait_ge(pv_ready if wide else div_ready, n + 1)
                dve.reciprocal(r_sum[:, :], u_ps[:, 1, :]).then_inc(rsum_ready, 1)
                dve.wait_ge(rsum_ready, n + 1)
                dve.tensor_tensor(attn[:, g * sh.parts + part, :], u_ps[:, 0, :] if wide else u_sb[:, :], r_sum[:, :],
                                  ALU.mult).then_inc(attn_ready, 1)

            def take_maxima(turn, g1):
                dve.wait_ge(bank_full, turn + 1)
                if in_stack:
                    dve.tensor_tensor(qst[g1][:, :], bank[:, :].bitcast(F16)[:, 0:SQ], qst[g1][:, :], ALU.add)\
                       .then_inc(bank_free, 1)
                    return
                mt_of = mt[g1 % 2]
                dve.tensor_copy(mt_of[0:12, :], bank[:, :].bitcast(BF16)[0:12, 0:SQ]).then_inc(bank_free, 1)

            def add_residual(turn, b):
                dve.wait_ge(bank_full, turn + 1)
                x = x_of(b)
                dve.scalar_tensor_tensor(x, bank[:, 0:QT * D].rearrange("p (t n) -> p t n", t=QT),
                                         gates[:, sh.gate:sh.gate + 1], x, ALU.mult, ALU.add).then_inc(bank_free, 1)

            def small_softmax_scores(b):
                flat = s_ipa[:, :, :, :].rearrange("p a h t -> p (a h) t")
                dve.tensor_reduce(m_ipa[:, :], flat, AXX, ALU.max).then_inc(ipa_step, 1)
                dve.wait_ge(ipa_step, 5 * b + 1)
                dve.tensor_tensor(flat, flat, m_ipa[:, :].unsqueeze(2).broadcast_to([P, QT * HEADS, IPA]),
                                  ALU.subtract).then_inc(ipa_step, 1)

            def small_softmax(b):
                dve.wait_ge(ipa_exp, b + 1)
                dve.reduce_sum(r_ipa[:, :], e_ipa[:, :, :], AXX).then_inc(ipa_step, 1)
                dve.wait_ge(ipa_step, 5 * b + 3)
                dve.reciprocal(m_ipa[:, :], r_ipa[:, :]).then_inc(ipa_step, 1)
                dve.wait_ge(ipa_step, 5 * b + 4)
                dve.tensor_tensor(p_ipa[:, :, :], e_ipa[:, :, :],
                                  m_ipa[:, :].unsqueeze(2).broadcast_to([P, QT * HEADS, IPA]), ALU.mult)\
                   .then_inc(ipa_step, 1)

            normalise(0)
            for key in sh.opening():
                if key[0] in (0, 1) and key[1] != "V":
                    pair("opening", 0, key, key[1:], key[0])
                elif key[0] == "MT":
                    for h in range(HG):
                        row_max(0, 0, h)
                    split_max(0)
                    take_maxima(sh.turn("opening", 0, key), 0)

            def body(kind, b):
                for g, s, p1, p2, more, tail in sh.slots(kind):
                    u = b * NG + g
                    g1 = (g + 1) % 4
                    if p1 and p1[0] != "V":
                        pair(kind, b, (g, s) + p1, p1, u + 2)
                    if (g, s) == (1, 0) and kind != "last":
                        normalise(b + 1)
                    if ipa and (g, s) == (3, 0):
                        small_softmax(b)
                    if more:
                        row_max(g1, u + 1, 2 * s)
                    if clip:
                        if s == 0:
                            dve.wait_ge(bank_free, shift_turn(kind, b, g))
                        clipped(g, s, u * HG + s)
                    if p2 and p2[0] != "V":
                        pair(kind, b, (g, s) + p2, p2, u + 2)
                    if more:
                        row_max(g1, u + 1, 2 * s + 1)
                    if not (kind == "first" and g == 0):
                        if wide and s in (0, 2):
                            divide((g - 1) % 4, u - 1, s // 2)
                        if not wide and s == 2:
                            divide((g - 1) % 4, u - 1, 0)
                    if more and s == 1:
                        split_max(u + 1)
                    for t in tail:
                        if t[0] == "MT":
                            take_maxima(sh.turn(kind, b, (g, s) + t), g1)
                        if t[0] == "OP":
                            add_residual(sh.turn(kind, b, (g, s) + t), b - 1)
                    if (g, s) == (0, HG - 1) and kind != "last":
                        stats_of(dve, b + 1)
                    if ipa and (g, s) == (2, HG - 1):
                        small_softmax_scores(b)
            batches(body, dve)
            for part in range(sh.parts):
                divide(3, B * NG - 1, part)
            add_residual(sh.end_turn(), B - 1)


def layernorm_all(nc, name, x_res, xn, xnT, const, loads):
    ident, _, _, _, _, eps = const
    with ExitStack() as ctx:
        sb, ps, sem = alloc(nc, ctx, name + "n")
        stats, mv = sb("stats", [P, NT, 6]), sb("mv", [P, NT, 2])
        lnv, rstd = sb("lnv", [P, NT]), sb("rstd", [P, NT])
        turned = [ps(f"turned{i}", [P, 4, P]) for i in range(2)]
        loaded = sem("loaded")
        stats_ready = sem("stats_ready")
        rstd_ready = sem("rstd_ready")
        xn_ready = sem("xn_ready")
        turned_ready = sem("turned_ready")
        xnT_ready = sem("xnT_ready")
        with nc.Block() as block:
            @block.sync
            def _(sp):
                for dst, src in loads:
                    sp.dma_start(dst, src).then_inc(loaded, 16)
                if loads:
                    sp.wait_ge(loaded, 16 * len(loads))

            @block.vector
            def _(dve):
                for t in range(NT):
                    ins = dve.bn_stats(stats[:, t, :], x_res[:, t, :])
                ins.then_inc(stats_ready, 1)
                dve.wait_ge(stats_ready, 1)
                for t in range(NT):
                    ins = dve.bn_aggr(mv[:, t, :], stats[:, t, :])
                ins.then_inc(stats_ready, 1)
                dve.wait_ge(rstd_ready, 2)
                for t in range(NT):
                    ins = dve.tensor_scalar(xn[:, t, :], x_res[:, t, :], mv[:, t, 0:1], rstd[:, t:t + 1],
                                            ALU.subtract, ALU.mult)
                    if t % 4 == 3:
                        ins.then_inc(xn_ready, 1)

            @block.scalar
            def _(act):
                act.wait_ge(stats_ready, 2)
                act.activation(lnv[:, :], mv[:, :, 1], ACT.Ln, bias=eps[:, 0:1]).then_inc(rstd_ready, 1)
                act.wait_ge(rstd_ready, 1)
                act.activation(rstd[:, :], lnv[:, :], ACT.Exp, scale=-0.5).then_inc(rstd_ready, 1)
                for k in range(NT // 4):
                    act.wait_ge(turned_ready, k + 1)
                    act.copy(xnT[:, k * 512:(k + 1) * 512], turned[k % 2][:, :, :].rearrange("p t n -> p (t n)"))\
                       .then_inc(xnT_ready, 1)

            @block.tensor
            def _(pe):
                for k in range(NT // 4):
                    pe.wait_ge(xn_ready, k + 1)
                    if k >= 2:
                        pe.wait_ge(xnT_ready, k - 1)
                    for t in range(4):
                        ins = pe.transpose(turned[k % 2][:, t, :], xn[:, 4 * k + t, :], ident[:, :])
                    ins.then_inc(turned_ready, 1)


TB = 512
TT = TB // P


def mlp(nc, name, x_res, xnT, ones, func, jobs):
    gated = jobs[0]["up"][0][1] is not None
    items = sum(len(j["up"]) for j in jobs)
    experts = sum(len(j["down"]) for j in jobs)
    dbufs = min(2, experts)
    with ExitStack() as ctx:
        sb, ps, sem = alloc(nc, ctx, name + "m")
        chunks = max(len(j["up"]) for j in jobs)
        hid = [[sb(f"hid{i}_{c}", [P, TB]) for c in range(chunks)] for i in range(2)]
        sg = [sb(f"sg{i}", [P, TB]) for i in range(2)] if gated else None
        up_ps = [ps(f"up{i}", [P, TB]) for i in range(2)]
        gate_ps = [ps(f"gate{i}", [P, TB]) for i in range(2)] if gated else None
        down_ps = [ps(f"down{i}", [P, TT, D]) for i in range(2)]
        up_ready = sem("up_ready")
        sg_ready = sem("sg_ready")
        hid_ready = sem("hid_ready")
        down_ready = sem("down_ready")
        down_free = sem("down_free")

        with nc.Block() as block:
            @block.tensor
            def _(pe):
                def up(tb, n, k, item):
                    w, wg, _, width = item
                    pe.wait_ge(hid_ready, n + 1)
                    x = xnT[:, bass.ds(tb * TB, TB)]
                    ins = pe.matmul(up_ps[k % 2][0:width, :], w, x, start=True, stop=True)
                    if gated:
                        ins = pe.matmul(gate_ps[k % 2][0:width, :], wg, x, start=True, stop=True)
                    ins.then_inc(up_ready, 1)

                def down(job_i, job, d, m, t, hid_count):
                    ws, bias, _ = job["down"][d]
                    if t == 0:
                        pe.wait_ge(down_free, m + 1)
                        pe.wait_ge(hid_ready, hid_count + 2)
                    dst = down_ps[m_static[0] % 2][:, t, :]
                    for c, (w, item) in enumerate(zip(ws, job["up"])):
                        ins = pe.matmul(dst, hid[job_i % 2][c][0:item[3], t * P:(t + 1) * P], w,
                                        start=(c == 0), stop=(c == len(ws) - 1 and not bias))
                    for i, row in enumerate(bias):
                        ins = pe.matmul(dst, ones[0:1, 0:P], row, start=False, stop=(i == len(bias) - 1))
                    if t == TT - 1:
                        ins.then_inc(down_ready, 1)
                        m_static[0] += 1

                m_static = [0]
                with pe.Fori(0, NT // TT) as tb:
                    k = m = 0
                    todo = []
                    for j, job in enumerate(jobs):
                        per = -(-len(todo) // len(job["up"]))
                        for item in job["up"]:
                            up(tb, tb * items + k, k, item)
                            k += 1
                            for a in todo[:per]:
                                down(*a)
                            todo = todo[per:]
                        for d in range(len(job["down"])):
                            todo += [(j, job, d, tb * experts + m, t, tb * items + k) for t in range(TT)]
                            m += 1
                    for a in todo:
                        down(*a)

            @block.scalar
            def _(act):
                if not gated:
                    act.sem_inc(hid_ready, 2)
                with act.Fori(0, NT // TT) as tb:
                    k = 0
                    for j, job in enumerate(jobs):
                        for c, (_, _, bias, width) in enumerate(job["up"]):
                            act.wait_ge(up_ready, tb * items + k + 1)
                            if gated:
                                act.activation(sg[k % 2][0:width, :], gate_ps[k % 2][0:width, :], func).then_inc(sg_ready, 1)
                            else:
                                act.activation(hid[j % 2][c][0:width, :], up_ps[k % 2][0:width, :], func, bias=bias)\
                                   .then_inc(hid_ready, 1)
                            k += 1

            @block.vector
            def _(dve):
                dve.sem_inc(down_free, dbufs)
                if gated:
                    dve.sem_inc(hid_ready, 2)

                def combine(tb, d, m, weight):
                    dve.wait_ge(down_ready, m + 1)
                    dve.wait_ge(down_free, m + dbufs)
                    src = down_ps[d % 2]
                    if weight.shape[1] == 1:
                        x = x_res[:, bass.ds(tb * TT, TT), :]
                        ins = dve.scalar_tensor_tensor(x, src[:, :, :], weight, x, ALU.mult, ALU.add)
                    else:
                        for t in range(TT):
                            x = x_res[:, bass.ds(tb * TT + t, 1), :].rearrange("p a n -> p (a n)")
                            ins = dve.scalar_tensor_tensor(x, src[:, t, :], weight[:, bass.ds(tb * TT + t, 1)], x,
                                                           ALU.mult, ALU.add)
                    ins.then_inc(down_free, 1)

                with dve.Fori(0, NT // TT) as tb:
                    k = m = 0
                    due = []
                    for j, job in enumerate(jobs):
                        for c, (_, _, _, width) in enumerate(job["up"]):
                            if gated:
                                dve.wait_ge(sg_ready, tb * items + k + 1)
                                dve.tensor_tensor(hid[j % 2][c][0:width, :], up_ps[k % 2][0:width, :],
                                                  sg[k % 2][0:width, :], ALU.mult).then_inc(hid_ready, 1)
                            k += 1
                        for a in due:
                            combine(*a)
                        due = []
                        for _, _, weight in job["down"]:
                            due.append((tb, m, tb * experts + m, weight))
                            m += 1
                    for a in due:
                        combine(*a)


def butterfly_step(eng, y, t0, t1, w, stage, transposed, chain, count):
    n = 2 ** stage
    v = y.rearrange("p (b a s) -> p b a s", a=2, s=n)
    a, b = v[:, :, 0, :], v[:, :, 1, :]
    wv = w.rearrange("p (b s o i) -> p b s o i", s=n, o=2, i=2)
    w01, w10 = wv[:, :, :, 0, 1], wv[:, :, :, 1, 0]
    if transposed:
        w01, w10 = w10, w01
    t0, t1, t2, t3 = (t.rearrange("p (b s) -> p b s", s=n) for t in (t0[:, 0:256], t0[:, 256:512], t1[:, 0:256], t1[:, 256:512]))
    eng.tensor_tensor(t0, a, wv[:, :, :, 0, 0], ALU.mult)
    eng.tensor_tensor(t1, b, w01, ALU.mult)
    eng.tensor_tensor(t2, a, w10, ALU.mult)
    eng.tensor_tensor(t3, b, wv[:, :, :, 1, 1], ALU.mult).then_inc(chain, 1)
    eng.wait_ge(chain, count + 1)
    eng.tensor_tensor(a, t0, t1, ALU.add)
    eng.tensor_tensor(b, t2, t3, ALU.add).then_inc(chain, 1)
    eng.wait_ge(chain, count + 2)


def butterfly_ffn(nc, name, x_res, gates, const, w):
    ident, _, _, _, ones, _ = const
    hidden, stages = 512, 9
    with ExitStack() as ctx:
        sb, ps, sem = alloc(nc, ctx, name)
        xn, xnT = sb("xn", [P, NT, D]), sb("xnT", [P, NT * P])
        w_exp, w_conT, b_exp = sb("w_exp", [P, hidden]), sb("w_conT", [P, hidden]), sb("b_exp", [1, hidden])
        up_bias = sb("up_bias", [1, hidden])
        w_con = sb("w_con", [P, 4, D])
        bias = sb("bias", [P, 4])
        rows = sb("rows", [1, 2, D])
        wup = [sb(f"wup{i}", [P, 1024]) for i in range(2)]
        wdn = [sb(f"wdn{i}", [P, 1024]) for i in range(2)]
        t0, t1, t2, t3 = (sb(f"t{i}", [P, hidden]) for i in range(4))
        t4, t5 = (sb(f"t{i}", [1, hidden]) for i in (4, 5))
        layernorm_all(nc, name, x_res, xn, xnT, const, [
            (w_exp[:, :], w["W_exp"]), (w_conT[:, :], w["W_conT"]), (b_exp[:, :], w["b_exp"].unsqueeze(0)),
            (up_bias[:, :], w["up_bias"].unsqueeze(0)), (rows[:, 0, :], w["b_con"].unsqueeze(0)),
            (rows[:, 1, :], w["down_bias"].unsqueeze(0))])
        with ExitStack() as c2:
            _, ps, sem = alloc(nc, c2, name + "b")
            turned, column = ps("turned", [P, 4, D]), ps("column", [P, 4])
            up_loaded = [sem(f"up_loaded{i}") for i in range(2)]
            down_loaded = [sem(f"down_loaded{i}") for i in range(2)]
            up_step = sem("up_step")
            down_step = sem("down_step")
            turned_ready = sem("turned_ready")
            done = sem("done")
            with nc.Block() as block:
                @block.sync
                def _(sp):
                    for n in range(stages):
                        if n >= 2:
                            sp.wait_ge(up_step, 4 * (n - 1))
                            sp.wait_ge(down_step, 2 * (n - 1))
                        sp.dma_start(wup[n % 2][:, :], w["up_weights"][n].rearrange("k o i -> (k o i)").partition_broadcast(P))\
                          .then_inc(up_loaded[n % 2], 16)
                        sp.dma_start(wdn[n % 2][:, :],
                                     w["down_weights"][stages - 1 - n].rearrange("k o i -> (k o i)").partition_broadcast(P))\
                          .then_inc(down_loaded[n % 2], 16)

                @block.vector
                def _(dve):
                    for n in range(stages):
                        dve.wait_ge(up_loaded[n % 2], 16 * (n // 2 + 1))
                        butterfly_step(dve, w_exp[:, :], t0, t1, wup[n % 2][:, :], n, False, up_step, 4 * n)
                        butterfly_step(dve, b_exp[:, :], t4, t5, wup[n % 2][0:1, :], n, False, up_step, 4 * n + 2)
                    dve.wait_ge(turned_ready, 1)
                    dve.tensor_copy(w_con[:, :, :], turned[:, :, :])
                    dve.tensor_copy(bias[:, :], column[:, :])

                @block.gpsimd
                def _(pool):
                    for n in range(stages):
                        pool.wait_ge(down_loaded[n % 2], 16 * (n // 2 + 1))
                        butterfly_step(pool, w_conT[:, :], t2, t3, wdn[n % 2][:, :], stages - 1 - n, True, down_step, 2 * n)

                @block.tensor
                def _(pe):
                    pe.wait_ge(up_step, 4 * stages)
                    for c in range(4):
                        pe.matmul(column[:, c:c + 1], b_exp[0:1, c * P:(c + 1) * P], ones[0:1, 0:1], start=True, stop=False)
                        pe.matmul(column[:, c:c + 1], up_bias[0:1, c * P:(c + 1) * P], ones[0:1, 0:1], start=False, stop=True)
                    pe.wait_ge(down_step, 2 * stages)
                    for c in range(4):
                        ins = pe.transpose(turned[:, c, :], w_conT[:, c * P:(c + 1) * P], ident[:, :])
                    ins.then_inc(turned_ready, 1)
        mlp(nc, name, x_res, xnT, ones, ACT.Gelu, [{
            "up": [(w_exp[:, c * P:(c + 1) * P], None, bias[:, c:c + 1], P) for c in range(4)],
            "down": [([w_con[:, c, :] for c in range(4)], [rows[0:1, 0, :], rows[0:1, 1, :]], gates[:, 4:5])]}])


def expert_ffn(nc, name, x_res, gates, const, io, w):
    ones = const[4]
    hidden, routed = 512, 7
    with ExitStack() as ctx:
        sb, ps, sem = alloc(nc, ctx, name)
        xn, xnT = sb("xn", [P, NT, D]), sb("xnT", [P, NT * P])
        wu, wg = sb("wu", [P, routed + 1, hidden]), sb("wg", [P, routed + 1, hidden])
        wd = sb("wd", [P, routed + 1, 4, D])
        wr, iota = sb("wr", [P, 8]), sb("iota", [P, 8])
        weight = sb("weight", [P, 8, NT])
        layernorm_all(nc, name, x_res, xn, xnT, const, [
            (wr[:, :], w["w_router"]), (iota[:, :], io["c_iota8"]),
            (wu[:, 0:routed, :], w["w_up"].rearrange("e p n -> p e n")), (wu[:, routed, :], w["ws_up"]),
            (wg[:, 0:routed, :], w["w_gate"].rearrange("e p n -> p e n")), (wg[:, routed, :], w["ws_gate"]),
            (wd[:, routed, :, :], w["ws_down"].rearrange("(c p) n -> p c n", p=P))]
            + [(wd[:, e, :, :], w["w_down"][e].rearrange("(c p) n -> p c n", p=P)) for e in range(routed)])
        with ExitStack() as c2:
            sb2, ps, sem = alloc(nc, c2, name + "r")
            logits = ps("logits", [P, NT, 8])
            top, p_top, first = sb2("top", [P, NT]), sb2("p_top", [P, NT]), sb2("first", [P, NT])
            z, e, eq, at = (sb2(n, [P, NT, 8]) for n in ("z", "e", "eq", "at"))
            logits_ready, e_ready, step = sem("logits_ready"), sem("e_ready"), sem("step")
            with nc.Block() as block:
                @block.tensor
                def _(pe):
                    for t in range(NT):
                        ins = pe.matmul(logits[:, t, :], xnT[:, t * P:(t + 1) * P], wr[:, :], start=True, stop=True)
                    ins.then_inc(logits_ready, 1)

                @block.scalar
                def _(act):
                    act.wait_ge(step, 2)
                    act.activation(e[:, :, :], z[:, :, :], ACT.Exp).then_inc(e_ready, 1)

                @block.vector
                def _(dve):
                    def over(a):
                        return a[:, :].unsqueeze(2).broadcast_to([P, NT, 8])
                    dve.wait_ge(logits_ready, 1)
                    dve.tensor_reduce(top[:, :], logits[:, :, :], AXX, ALU.max).then_inc(step, 1)
                    dve.wait_ge(step, 1)
                    dve.tensor_tensor(z[:, :, :], logits[:, :, :], over(top), ALU.subtract).then_inc(step, 1)
                    dve.wait_ge(e_ready, 1)
                    dve.reduce_sum(p_top[:, :], e[:, :, :], AXX).then_inc(step, 1)
                    dve.tensor_tensor(eq[:, :, :], logits[:, :, :], over(top), ALU.is_equal).then_inc(step, 1)
                    dve.wait_ge(step, 4)
                    dve.scalar_tensor_tensor(at[:, :, :], eq[:, :, :], -100.0,
                                             iota[:, :].unsqueeze(1).broadcast_to([P, NT, 8]), ALU.mult, ALU.add).then_inc(step, 1)
                    dve.wait_ge(step, 5)
                    dve.tensor_reduce(first[:, :], at[:, :, :], AXX, ALU.min).then_inc(step, 1)
                    dve.reciprocal(top[:, :], p_top[:, :]).then_inc(step, 1)
                    dve.wait_ge(step, 7)
                    dve.tensor_tensor(eq[:, :, :], at[:, :, :], over(first), ALU.is_equal).then_inc(step, 1)
                    dve.tensor_scalar(p_top[:, :], top[:, :], gates[:, 5:6], 2.0, ALU.mult, ALU.mult).then_inc(step, 1)
                    dve.wait_ge(step, 9)
                    dve.tensor_tensor(weight[:, :, :].rearrange("p e t -> p t e"), eq[:, :, :], over(p_top), ALU.mult)
        jobs = []
        for e in range(routed + 1):
            up = [(wu[:, e, c * P:(c + 1) * P], wg[:, e, c * P:(c + 1) * P], None, P) for c in range(4)]
            col = weight[:, e, :] if e < routed else gates[:, 5:6]
            jobs.append({"up": up, "down": [([wd[:, e, c, :] for c in range(4)], [], col)]})
        mlp(nc, name, x_res, xnT, ones, ACT.Silu, jobs)


def column_ffn(nc, name, x_res, gates, const, io, w):
    ident, _, _, _, ones, eps = const
    cols, neurons, gate_dim = 16, 32, 64
    hidden = cols * neurons
    with ExitStack() as ctx:
        sb, ps, sem = alloc(nc, ctx, name)
        xn, xnT = sb("xn", [P, NT, D]), sb("xnT", [P, NT * P])
        col_emb, ceT = sb("col_emb", [cols, D]), sb("ceT", [P, cols])
        w1, b1, w2, b2 = sb("w1", [P, gate_dim]), sb("b1", [gate_dim, 1]), sb("w2", [gate_dim, cols]), sb("b2", [1, cols])
        w_cols, b_cols = sb("w_cols", [P, cols, neurons]), sb("b_cols", [1, hidden])
        proj_w, proj_b = sb("proj_w", [P, 4, D]), sb("proj_b", [1, D])
        ln_g, ln_b = sb("ln_g", [P, D]), sb("ln_b", [P, D])
        iota = sb("iota", [P, cols])
        weight = sb("weight", [P, NT, cols])
        layernorm_all(nc, name, x_res, xn, xnT, const, [
            (col_emb[:, :], w["col_emb"]), (w1[:, :], w["gate_w1"]), (b1[:, :], w["gate_b1"].unsqueeze(1)),
            (w2[:, :], w["gate_w2"]), (b2[:, :], w["gate_b2"].unsqueeze(0)),
            (w_cols[:, :, :], w["W_cols"].rearrange("c p n -> p c n")),
            (b_cols[:, :], w["b_cols"].rearrange("(a c) n -> a (c n)", a=1)),
            (proj_w[:, :, :], w["proj_w"].rearrange("(c p) n -> p c n", p=P)), (proj_b[:, :], w["proj_b"].unsqueeze(0)),
            (ln_g[:, :], w["ln_g"].partition_broadcast(P)), (ln_b[:, :], w["ln_b"].partition_broadcast(P)),
            (iota[:, :], io["c_iota16"])])

        with ExitStack() as c2:
            sb2, ps, sem = alloc(nc, c2, name + "r")
            hg = sb2("hg", [gate_dim, NT * P])
            sq, norm, n2 = sb2("sq", [P, NT, D]), sb2("norm", [P, NT]), sb2("n2", [P, NT])
            ce2, ce_n, ce_s = sb2("ce2", [cols, D]), sb2("ce_n", [cols, 1]), sb2("ce_s", [cols, D])
            sig, lg, z, e, eq, at = (sb2(n, [P, NT, cols]) for n in ("sig", "lg", "z", "e", "eq", "at"))
            top, total, first, p_top = (sb2(n, [P, NT]) for n in ("top", "total", "first", "p_top"))
            hg_ps = [ps(f"hg_ps{i}", [gate_dim, 512]) for i in range(2)]
            gate_ps, sim_ps, ce_ps = ps("gate_ps", [P, NT, cols]), ps("sim_ps", [P, NT, cols]), ps("ce_ps", [P, cols])
            step, reci = sem("step"), sem("reci")
            act_step = sem("act_step")
            hg_ready, hg_done = sem("hg_ready"), sem("hg_done")
            gate_ready, ce_ready, sim_ready = sem("gate_ready"), sem("ce_ready"), sem("sim_ready")
            with nc.Block() as block:
                @block.tensor
                def _(pe):
                    for k in range(4):
                        if k >= 2:
                            pe.wait_ge(hg_done, k - 1)
                        pe.matmul(hg_ps[k % 2][:, :], w1[:, :], xnT[:, k * 512:(k + 1) * 512], start=True, stop=True)\
                          .then_inc(hg_ready, 1)
                    for t in range(NT):
                        if t % 4 == 0:
                            pe.wait_ge(hg_done, t // 4 + 1)
                        pe.matmul(gate_ps[:, t, :], hg[:, t * P:(t + 1) * P], w2[:, :], start=True, stop=False)
                        ins = pe.matmul(gate_ps[:, t, :], ones[0:1, 0:P], b2[:, :], start=False, stop=True)
                    ins.then_inc(gate_ready, 1)
                    pe.wait_ge(step, 6)
                    pe.transpose(ce_ps[:, :], ce_s[:, :], ident[0:cols, 0:cols]).then_inc(ce_ready, 1)
                    pe.wait_ge(step, 7)
                    for t in range(NT):
                        ins = pe.matmul(sim_ps[:, t, :], xnT[:, t * P:(t + 1) * P], ceT[:, :], start=True, stop=True)
                    ins.then_inc(sim_ready, 1)

                @block.scalar
                def _(act):
                    act.wait_ge(step, 4)
                    act.activation(norm[:, :], n2[:, :], ACT.Sqrt)
                    act.activation(ce_n[:, :], ce_n[:, :], ACT.Sqrt).then_inc(act_step, 1)
                    for k in range(4):
                        act.wait_ge(hg_ready, k + 1)
                        act.activation(hg[:, k * 512:(k + 1) * 512], hg_ps[k % 2][:, :], ACT.Gelu, bias=b1[:, 0:1])\
                           .then_inc(hg_done, 1)
                    act.wait_ge(gate_ready, 1)
                    act.activation(sig[:, :, :], gate_ps[:, :, :], ACT.Sigmoid).then_inc(act_step, 1)
                    act.wait_ge(step, 11)
                    act.activation(e[:, :, :], z[:, :, :], ACT.Exp).then_inc(act_step, 1)

                @block.vector
                def _(dve):
                    def over(a):
                        return a[:, :].unsqueeze(2).broadcast_to([P, NT, cols])
                    dve.tensor_tensor(sq[:, :, :], xn[:, :, :], xn[:, :, :], ALU.mult).then_inc(step, 1)
                    dve.tensor_tensor(ce2[:, :], col_emb[:, :], col_emb[:, :], ALU.mult).then_inc(step, 1)
                    dve.wait_ge(step, 2)
                    dve.reduce_sum(n2[:, :], sq[:, :, :], AXX).then_inc(step, 1)
                    dve.reduce_sum(ce_n[:, :], ce2[:, :], AXX).then_inc(step, 1)
                    dve.wait_ge(act_step, 1)
                    dve.tensor_scalar(ce_n[:, :], ce_n[:, :], 1e-12, None, ALU.max)
                    dve.tensor_scalar(norm[:, :], norm[:, :], 1e-12, None, ALU.max).then_inc(step, 1)
                    dve.wait_ge(step, 5)
                    dve.reciprocal(ce2[:, 0:1], ce_n[:, :])
                    dve.reciprocal(n2[:, :], norm[:, :]).then_inc(reci, 1)
                    dve.wait_ge(reci, 1)
                    dve.tensor_scalar(ce_s[:, :], col_emb[:, :], ce2[:, 0:1], None, ALU.mult).then_inc(step, 1)
                    dve.wait_ge(ce_ready, 1)
                    dve.tensor_copy(ceT[:, :], ce_ps[:, :]).then_inc(step, 1)
                    dve.wait_ge(sim_ready, 1)
                    dve.tensor_tensor(lg[:, :, :], sim_ps[:, :, :], over(n2), ALU.mult).then_inc(step, 1)
                    dve.wait_ge(act_step, 2)
                    dve.wait_ge(step, 8)
                    dve.tensor_tensor(z[:, :, :], lg[:, :, :], sig[:, :, :], ALU.add).then_inc(step, 1)
                    dve.wait_ge(step, 9)
                    dve.tensor_reduce(top[:, :], z[:, :, :], AXX, ALU.max).then_inc(step, 1)
                    dve.wait_ge(step, 10)
                    dve.tensor_tensor(eq[:, :, :], z[:, :, :], over(top), ALU.is_equal)
                    dve.tensor_tensor(z[:, :, :], z[:, :, :], over(top), ALU.subtract).then_inc(step, 1)
                    dve.wait_ge(step, 11)
                    dve.scalar_tensor_tensor(at[:, :, :], eq[:, :, :], -100.0,
                                             iota[:, :].unsqueeze(1).broadcast_to([P, NT, cols]), ALU.mult, ALU.add)\
                       .then_inc(step, 1)
                    dve.wait_ge(step, 12)
                    dve.tensor_reduce(first[:, :], at[:, :, :], AXX, ALU.min).then_inc(step, 1)
                    dve.wait_ge(act_step, 3)
                    dve.reduce_sum(total[:, :], e[:, :, :], AXX).then_inc(step, 1)
                    dve.wait_ge(step, 14)
                    dve.reciprocal(p_top[:, :], total[:, :])
                    dve.tensor_tensor(eq[:, :, :], at[:, :, :], over(first), ALU.is_equal).then_inc(step, 1)
                    dve.wait_ge(step, 15)
                    dve.tensor_tensor(weight[:, :, :], eq[:, :, :], over(p_top), ALU.mult)

        with ExitStack() as c2:
            sb2, ps, sem = alloc(nc, c2, name + "c")
            hc = [sb2(f"hc{i}", [P, cols, neurons]) for i in range(2)]
            hw = [sb2(f"hw{i}", [P, hidden]) for i in range(2)]
            hT = [sb2(f"hT{i}", [P, 4, P]) for i in range(2)]
            y, yn = sb2("y", [P, NT, D]), sb2("yn", [P, NT, D])
            stats, mv = sb2("stats", [P, NT, 6]), sb2("mv", [P, NT, 2])
            lnv, rstd = sb2("lnv", [P, NT]), sb2("rstd", [P, NT])
            up_ps = [ps(f"up{i}", [P, hidden]) for i in range(2)]
            t_ps = [ps(f"t{i}", [P, 4, P]) for i in range(2)]
            y_ps = [ps(f"y{i}", [P, D]) for i in range(2)]
            up_ready = sem("up_ready")
            hc_ready = sem("hc_ready")
            hw_ready = sem("hw_ready")
            t_ready = sem("t_ready")
            hT_ready = sem("hT_ready")
            y_ready = sem("y_ready")
            y_done = sem("y_done")
            step, rstd_ready = sem("step"), sem("rstd_ready")
            with nc.Block() as block:
                @block.tensor
                def _(pe):
                    def up(t, i):
                        if i >= 2:
                            pe.wait_ge(hc_ready, t - 1)
                        pe.matmul(up_ps[i % 2][:, :], xnT_tile(t), w_cols[:, :, :].rearrange("p c n -> p (c n)"),
                                  start=True, stop=False)
                        pe.matmul(up_ps[i % 2][:, :], ones[0:1, 0:P], b_cols[:, :], start=False, stop=True)\
                          .then_inc(up_ready, 1)

                    def xnT_tile(t):
                        return xnT[:, t * P:(t + 1) * P]

                    for t in range(NT + 1):
                        if t < NT:
                            up(t, t)
                        if t >= 1:
                            n = t - 1
                            pe.wait_ge(hw_ready, n + 1)
                            if n >= 2:
                                pe.wait_ge(hT_ready, n - 1)
                            for c in range(4):
                                ins = pe.transpose(t_ps[n % 2][:, c, :], hw[n % 2][:, c * P:(c + 1) * P], ident[:, :])
                            ins.then_inc(t_ready, 1)
                            if n >= 2:
                                pe.wait_ge(y_done, n - 1)
                            pe.wait_ge(hT_ready, n + 1)
                            for c in range(4):
                                pe.matmul(y_ps[n % 2][:, :], hT[n % 2][:, c, :], proj_w[:, c, :], start=(c == 0), stop=False)
                            pe.matmul(y_ps[n % 2][:, :], ones[0:1, 0:P], proj_b[:, :], start=False, stop=True)\
                              .then_inc(y_ready, 1)

                @block.scalar
                def _(act):
                    def hidden_values(t):
                        act.wait_ge(up_ready, t + 1)
                        act.activation(hc[t % 2][:, :, :], up_ps[t % 2][:, :].rearrange("p (c n) -> p c n", c=cols), ACT.Gelu)\
                           .then_inc(hc_ready, 1)
                    hidden_values(0)
                    for t in range(NT):
                        if t + 1 < NT:
                            if t >= 1:
                                act.wait_ge(hw_ready, t)
                            hidden_values(t + 1)
                        act.wait_ge(t_ready, t + 1)
                        act.copy(hT[t % 2][:, :, :], t_ps[t % 2][:, :, :]).then_inc(hT_ready, 1)
                    act.wait_ge(step, 2)
                    act.activation(lnv[:, :], mv[:, :, 1], ACT.Ln, bias=eps[:, 0:1]).then_inc(rstd_ready, 1)
                    act.wait_ge(rstd_ready, 1)
                    act.activation(rstd[:, :], lnv[:, :], ACT.Exp, scale=-0.5).then_inc(rstd_ready, 1)

                @block.vector
                def _(dve):
                    for t in range(NT + 1):
                        if t < NT:
                            dve.wait_ge(hc_ready, t + 1)
                            if t >= 2:
                                dve.wait_ge(t_ready, t - 1)
                            dve.tensor_tensor(hw[t % 2][:, :].rearrange("p (c n) -> p c n", c=cols), hc[t % 2][:, :, :],
                                              weight[:, t, :].unsqueeze(2).broadcast_to([P, cols, neurons]), ALU.mult)\
                               .then_inc(hw_ready, 1)
                        if t >= 1:
                            n = t - 1
                            dve.wait_ge(y_ready, n + 1)
                            dve.tensor_tensor(y[:, n, :], y_ps[n % 2][:, :], xn[:, n, :], ALU.add).then_inc(y_done, 1)
                    dve.wait_ge(y_done, NT)
                    for t in range(NT):
                        ins = dve.bn_stats(stats[:, t, :], y[:, t, :])
                    ins.then_inc(step, 1)
                    dve.wait_ge(step, 1)
                    for t in range(NT):
                        ins = dve.bn_aggr(mv[:, t, :], stats[:, t, :])
                    ins.then_inc(step, 1)
                    dve.wait_ge(rstd_ready, 2)
                    for t in range(NT):
                        ins = dve.tensor_scalar(yn[:, t, :], y[:, t, :], mv[:, t, 0:1], rstd[:, t:t + 1],
                                                ALU.subtract, ALU.mult)
                    ins.then_inc(step, 1)
                    dve.wait_ge(step, 3)
                    every = [P, NT, D]
                    dve.tensor_tensor(y[:, :, :], yn[:, :, :], ln_g[:, :].unsqueeze(1).broadcast_to(every), ALU.mult)\
                       .then_inc(step, 1)
                    dve.wait_ge(step, 4)
                    dve.tensor_tensor(yn[:, :, :], y[:, :, :], ln_b[:, :].unsqueeze(1).broadcast_to(every), ALU.add)\
                       .then_inc(step, 1)
                    dve.wait_ge(step, 5)
                    dve.scalar_tensor_tensor(x_res[:, :, :], yn[:, :, :], gates[:, 6:7], x_res[:, :, :], ALU.mult, ALU.add)


def choice_ffn(nc, name, x_res, gates, const, io, w):
    ident, _, _, _, ones, _ = const
    experts, groups, width = 8, 4, 341
    chosen = NT * P // experts
    bits = 30
    spans = [(0, P), (P, P), (2 * P, width - 2 * P)]
    with ExitStack() as ctx:
        sb, ps, sem = alloc(nc, ctx, name)
        xn, xnT = sb("xn", [P, NT, D]), sb("xnT", [P, NT * P])
        wr, br = sb("wr", [P, experts]), sb("br", [1, experts])
        wu, bu = sb("wu", [P, groups, width]), sb("bu", [P, 3, groups])
        wd, bd = sb("wd", [P, experts, 3, D]), sb("bd", [1, experts, D])
        same, before, masks = sb("same", [P, P]), sb("before", [P, P]), sb("masks", [P, bits], U32)
        weight = sb("weight", [P, experts, NT])
        loads = [(wr[:, :], w["Wr"]), (br[:, :], w["br"].unsqueeze(0)), (wu[:, :, :], w["W_up"].rearrange("g p f -> p g f")),
                 (bd[:, :, :], w["b_down"].unsqueeze(0)), (same[:, :], io["c_same"]), (before[:, :], io["c_before"]),
                 (masks[:, :], io["c_masks"])]
        for c, (at, n) in enumerate(spans):
            loads.append((bu[0:n, c, :], w["b_upT"][at:at + n, :]))
            loads.append((wd[0:n, :, c, :], w["W_down"][:, at:at + n, :].rearrange("e f n -> f e n")))
        layernorm_all(nc, name, x_res, xn, xnT, const, loads)
        with ExitStack() as c2:
            sb2, ps, sem = alloc(nc, c2, name + "r")
            logits, turned = ps("logits", [P, NT, experts]), ps("turned", [P, P])
            count_ps, back_ps = ps("count", [P, 4]), ps("back", [P, P])
            top, total, z, e, probs = (sb2(n, s) for n, s in (
                ("top", [P, NT]), ("total", [P, NT]), ("z", [P, NT, experts]), ("e", [P, NT, experts]),
                ("probs", [P, NT, experts])))
            p, over_it, gt, eq, rank, chosen_p = (sb2(n, [P, P]) for n in ("p", "over_it", "gt", "eq", "rank", "chosen_p"))
            least, trial, cnt, kept = sb2("least", [P, 1], U32), sb2("trial", [P, 1], U32), sb2("cnt", [P, 1]), sb2("kept", [P, 1])
            n_gt, n_eq, room = sb2("n_gt", [P, 1]), sb2("n_eq", [P, 1]), sb2("room", [P, 1])
            least_f, trial_f = least[:, :].bitcast(F32), trial[:, :].bitcast(F32)
            step, e_ready, late = sem("step"), sem("e_ready"), sem("late")
            pe_step = sem("pe_step")
            trial_ready, counted, summed, judged, settled = (
                sem(n) for n in ("trial_ready", "counted", "summed", "judged", "settled"))
            with nc.Block() as block:
                @block.tensor
                def _(pe):
                    for t in range(NT):
                        pe.matmul(logits[:, t, :], xnT[:, t * P:(t + 1) * P], wr[:, :], start=True, stop=False)
                        ins = pe.matmul(logits[:, t, :], ones[0:1, 0:P], br[:, :], start=False, stop=True)
                    ins.then_inc(pe_step, 1)
                    pe.wait_ge(step, 5)
                    pe.transpose(turned[:, :], probs[:, :, :].rearrange("p t e -> p (t e)"), ident[:, :]).then_inc(pe_step, 1)
                    with pe.Fori(0, bits) as i:
                        pe.wait_ge(counted, i + 1)
                        pe.matmul(count_ps[:, 0:1], same[:, :], cnt[:, :], start=True, stop=True).then_inc(summed, 1)
                    pe.wait_ge(step, 7)
                    pe.matmul(count_ps[:, 1:2], same[:, :], n_gt[:, :], start=True, stop=True)
                    pe.matmul(count_ps[:, 2:3], before[:, :], n_eq[:, :], start=True, stop=True).then_inc(pe_step, 1)
                    pe.wait_ge(step, 12)
                    pe.transpose(back_ps[:, :], chosen_p[:, :], ident[:, :]).then_inc(pe_step, 1)

                @block.scalar
                def _(act):
                    act.wait_ge(step, 2)
                    act.activation(e[:, :, :], z[:, :, :], ACT.Exp).then_inc(e_ready, 1)

                @block.vector
                def _(dve):
                    def over(a):
                        return a[:, :].unsqueeze(2).broadcast_to([P, NT, experts])
                    dve.wait_ge(pe_step, 1)
                    dve.tensor_reduce(top[:, :], logits[:, :, :], AXX, ALU.max).then_inc(step, 1)
                    dve.wait_ge(step, 1)
                    dve.tensor_tensor(z[:, :, :], logits[:, :, :], over(top), ALU.subtract).then_inc(step, 1)
                    dve.wait_ge(e_ready, 1)
                    dve.reduce_sum(total[:, :], e[:, :, :], AXX).then_inc(step, 1)
                    dve.wait_ge(step, 3)
                    dve.reciprocal(top[:, :], total[:, :]).then_inc(step, 1)
                    dve.wait_ge(step, 4)
                    dve.tensor_tensor(probs[:, :, :], e[:, :, :], over(top), ALU.mult).then_inc(step, 1)
                    dve.wait_ge(pe_step, 2)
                    dve.tensor_copy(p[:, :], turned[:, :])
                    dve.memset(least[:, :], 0).then_inc(settled, 1)
                    with dve.Fori(0, bits) as i:
                        dve.wait_ge(settled, i + 1)
                        dve.tensor_tensor(trial[:, :], least[:, :], masks[:, bass.ds(i, 1)], ALU.bitwise_or)\
                           .then_inc(trial_ready, 1)
                        dve.wait_ge(trial_ready, i + 1)
                        dve.tensor_scalar(over_it[:, :], p[:, :], trial_f, None, ALU.is_ge, ALU.add, accum_out=cnt[:, :])\
                           .then_inc(counted, 1)
                        dve.wait_ge(summed, i + 1)
                        dve.tensor_scalar(kept[:, :], count_ps[:, 0:1], chosen - 0.5, trial_f, ALU.is_gt, ALU.mult)\
                           .then_inc(judged, 1)
                        dve.wait_ge(judged, i + 1)
                        dve.tensor_tensor(least_f, least_f, kept[:, :], ALU.max).then_inc(settled, 1)
                    dve.wait_ge(settled, bits + 1)
                    dve.tensor_scalar(gt[:, :], p[:, :], least_f, None, ALU.is_gt, ALU.add, accum_out=n_gt[:, :]).then_inc(step, 1)
                    dve.tensor_scalar(eq[:, :], p[:, :], least_f, None, ALU.is_equal, ALU.add, accum_out=n_eq[:, :]).then_inc(step, 1)
                    dve.wait_ge(step, 7)
                    dve.tensor_tensor_scan(rank[:, :], ones[:, 0:P], eq[:, :], 0.0, ALU.mult, ALU.add).then_inc(step, 1)
                    dve.wait_ge(pe_step, 3)
                    dve.tensor_scalar(kept[:, :], count_ps[:, 1:2], -1.0, float(chosen), ALU.mult, ALU.add).then_inc(step, 1)
                    dve.wait_ge(step, 9)
                    dve.tensor_tensor(room[:, :], kept[:, :], count_ps[:, 2:3], ALU.subtract).then_inc(step, 1)
                    dve.wait_ge(step, 10)
                    dve.scalar_tensor_tensor(over_it[:, :], rank[:, :], room[:, 0:1], eq[:, :], ALU.is_le, ALU.mult)\
                       .then_inc(step, 1)
                    dve.wait_ge(step, 11)
                    dve.tensor_tensor(rank[:, :], over_it[:, :], gt[:, :], ALU.add).then_inc(late, 1)
                    dve.wait_ge(late, 1)
                    dve.tensor_tensor(chosen_p[:, :], rank[:, :], p[:, :], ALU.mult).then_inc(step, 1)
                    dve.wait_ge(pe_step, 4)
                    dve.tensor_scalar(weight[:, :, :].rearrange("p e t -> p t e"),
                                      back_ps[:, :].rearrange("p (t e) -> p t e", e=experts), gates[:, 7:8], None, ALU.mult)
        jobs = []
        for g in range(groups):
            up = [(wu[:, g, at:at + n], None, bu[0:n, c, g:g + 1], n) for c, (at, n) in enumerate(spans)]
            jobs.append({"up": up, "down": [([wd[0:n, e, c, :] for c, (_, n) in enumerate(spans)], [bd[0:1, e, :]],
                                             weight[:, e, :]) for e in (2 * g, 2 * g + 1)]})
        mlp(nc, name, x_res, xnT, ones, ACT.Silu, jobs)


def program(nc, io, layers):
    SEMAPHORES.clear()
    with ExitStack() as ctx:
        sb, ps, sem = alloc(nc, ctx, "top")
        x_res = sb("x_res", [P, NT, D])
        gates = sb("gates", [P, 8])
        gates_in = sb("gates_in", [P, 8])
        ident, bsel, ones = sb("ident", [P, P]), sb("bsel", [P, P]), sb("ones", [P, SK])
        identb, identh = sb("identb", [P, P], BF16), sb("identh", [P, P], F16)
        cvec, eps = sb("cvec", [P, 3]), sb("eps", [P, 1])
        mask_in, mask_f = sb("mask_in", [B, SK], U8), sb("mask_f", [B, SK])
        loaded, ready, stored = sem("loaded"), sem("ready"), sem("stored")
        mask_rows = io["scratch_mask"]

        with nc.Block() as block:
            @block.sync
            def _(sp):
                for dst, src in ((x_res[:, :, :], io["x"].rearrange("b (t p) d -> p (b t) d", p=P)),
                                 (gates_in[:, 0:4], io["g_xattn"].partition_broadcast(P)),
                                 (gates_in[:, 4:8], io["g_ffn"].partition_broadcast(P)),
                                 (ident[:, :], io["c_ident"]), (identh[:, :], io["c_identh"]),
                                 (bsel[:, :], io["c_bsel"]), (cvec[:, :], io["c_vec"]),
                                 (mask_in[:, :], io["mask_BxS2_bf1"])):
                    sp.dma_start(dst, src).then_inc(loaded, 16)
                sp.wait_ge(ready, 4)
                sp.dma_start(mask_rows, mask_f[:, :]).then_inc(stored, 16)
                sp.wait_ge(stored, 16)

            @block.scalar
            def _(act):
                act.wait_ge(loaded, 8 * 16)
                act.activation(gates[:, :], gates_in[:, :], ACT.Tanh).then_inc(ready, 1)

            @block.vector
            def _(dve):
                dve.memset(ones[:, :], 1.0)
                dve.memset(eps[:, :], EPS)
                dve.wait_ge(loaded, 8 * 16)
                dve.tensor_copy(identb[:, :], identh[:, :])
                dve.tensor_copy(mask_f[:, :], mask_in[:, :]).then_inc(ready, 1)
                dve.wait_ge(ready, 2)
                dve.tensor_scalar(mask_f[:, :], mask_f[:, :], 1.0, MASK_K, ALU.subtract, ALU.mult).then_inc(ready, 2)

        const = (ident, identb, cvec, bsel, ones, eps)

        def weights(prefix, names):
            return {n: io[f"{prefix}_{n}"] for n in names}

        shared = {"ctxT": io["ctxT"], "sel": io["c_sel"], "identh": identh}
        if 0 in layers:
            attention(nc, Shape("L0x", wide=False, clip=True, bias=True, gate=0),
                      shared | {"ones_row": io["c_ones"]} | weights("L0_xattn", "Wq bq Wk bk Wv bv Wo bo".split()),
                      (x_res, gates), const)
        if 1 in layers:
            butterfly_ffn(nc, "L0f", x_res, gates, const, weights("L0_ffn", "W_exp b_exp up_weights up_bias down_weights "
                                                                  "W_conT b_con down_bias".split()))
        if 2 in layers:
            attention(nc, Shape("L1x", wide=True, ipa=True, gate=1),
                      shared | weights("L1_xattn", "Wq Wk Wv Wo bo q_downT q_up q_alpha k_downT k_up k_alpha v_downT v_up "
                                       "v_alpha o_downT o_up o_alpha Wk_ipa Wv_ipa".split()), (x_res, gates), const)
        if 3 in layers:
            expert_ffn(nc, "L1f", x_res, gates, const, io,
                       weights("L1_ffn", "w_router w_up w_gate w_down ws_up ws_gate ws_down".split()))
        nc.clear_and_free_semaphores(SEMAPHORES)
        SEMAPHORES.clear()
        nc.all_engine_barrier()
        stored = sem("stored_out")
        if 4 in layers:
            attention(nc, Shape("L2x", wide=True, gate=2),
                      shared | weights("L2_xattn", "Wq Wk Wv Wo bo".split()), (x_res, gates), const)
        if 5 in layers:
            column_ffn(nc, "L2f", x_res, gates, const, io, weights("L2_ffn", "col_emb gate_w1 gate_b1 gate_w2 gate_b2 W_cols "
                                                                   "b_cols proj_w proj_b ln_g ln_b".split()))
        if 6 in layers:
            attention(nc, Shape("L3x", wide=False, mask=True, out_bias=False, gate=3),
                      shared | {"mask_row": mask_rows.unsqueeze(1), "mask_q_row": io["c_mask_q"],
                                "mask_k_row": io["c_mask_k"],
                                "shift_k_row": io["c_shift_k"], "ones_row": io["c_ones"]} | weights("L3_xattn", "Wq Wk Wv Wo".split()),
                      (x_res, gates), const)
        if 7 in layers:
            choice_ffn(nc, "L3f", x_res, gates, const, io,
                       weights("L3_ffn", "Wr br W_up b_upT W_down b_down".split()))

        with nc.Block() as block:
            @block.sync
            def _(sp):
                sp.dma_start(io["out"].rearrange("b (t p) d -> p (b t) d", p=P), x_res[:, :, :]).then_inc(stored, 16)
                sp.wait_ge(stored, 16)


def constants():
    row = np.arange(P)
    sel = np.zeros((32, HG, 2, P), np.float16)
    for h in range(HG):
        for part in range(3):
            sel[part * HG + h, h] = 1.0
    sel[12, :, 1, P - IPA:] = HIDE_KEY
    slot = (row % 32) // 8
    vec = np.zeros((P, 3), np.float32)
    vec[:, 0] = slot == 1
    vec[:, 1] = slot == 2
    vec[:, 2] = row >= 64
    bsel = np.zeros((P, P), np.float32)
    bsel[(row // 32) * 32 + 8, row] = 1.0
    mask_q, mask_k = np.zeros((1, NG, P), np.float32), np.zeros((1, NG, P), np.float32)
    mask_q[:, :, 24::32] = MASK_Q
    mask_k[:, :, 24::32] = 1.0
    shift_k = np.zeros((1, NG, P), np.float32)
    for part in range(3):
        shift_k[:, :, 25 + part::32] = MASK_K
    return {"c_sel": sel, "c_vec": vec, "c_bsel": bsel, "c_mask_q": mask_q, "c_mask_k": mask_k,
            "c_ident": np.eye(P, dtype=np.float32),
            "c_iota8": np.tile(np.arange(8, dtype=np.float32), (P, 1)),
            "c_iota16": np.tile(np.arange(16, dtype=np.float32), (P, 1)),
            "c_identh": np.eye(P, dtype=np.float16), "c_shift_k": shift_k,
            "c_same": (row[:, None] % 8 == row % 8).astype(np.float32),
            "c_before": ((row[:, None] % 8 == row % 8) & (row[:, None] < row)).astype(np.float32),
            "c_masks": np.tile(np.uint32(1) << np.arange(29, -1, -1, dtype=np.uint32), (P, 1)),
            "c_ones": np.ones((1, SK), np.float32)}


LAYERS = (0, 1, 2, 3, 4, 5, 6, 7)


def kernel(**inputs):
    import concourse.bacc as bacc
    from concourse.bass_utils import run_bass_kernel_spmd

    nc = bacc.Bacc("TRN2", target_bir_lowering=False, num_devices=1)
    arrays = {n: np.ascontiguousarray(a) for n, a in inputs.items() if n != "ctx_768"}
    arrays["mask_BxS2_bf1"] = arrays["mask_BxS2_bf1"].view(np.uint8)
    arrays["ctxT"] = np.ascontiguousarray(np.asarray(inputs["ctx_768"]).transpose(0, 2, 1))
    for n in "qkvo":
        arrays[f"L1_xattn_{n}_downT"] = np.ascontiguousarray(np.asarray(arrays.pop(f"L1_xattn_{n}_down")).T)
    arrays["L0_ffn_W_conT"] = np.ascontiguousarray(np.asarray(arrays.pop("L0_ffn_W_con")).T)
    arrays["L3_ffn_b_upT"] = np.ascontiguousarray(np.asarray(arrays.pop("L3_ffn_b_up")).T)
    arrays |= constants()
    io = {n: nc.dram_tensor(f"in_{n}", a.shape, mybir.dt.from_np(a.dtype), kind="ExternalInput").ap()
          for n, a in arrays.items()}
    io["scratch_mask"] = nc.dram_tensor("scratch_mask", (B, SK), F32).ap()
    io["out"] = nc.dram_tensor("out_x", (B, SQ, D), F32, kind="ExternalOutput").ap()
    program(nc, io, LAYERS)
    result = run_bass_kernel_spmd(nc, [{f"in_{n}": a for n, a in arrays.items()}], core_ids=[0])
    return result.results[0]["out_x"]
```

```python
from contextlib import ExitStack

import numpy as np

import concourse.bass as bass
from concourse import mybir

ALU = mybir.AluOpType
ACT = mybir.ActivationFunctionType
AXX = mybir.AxisListType.X
F32 = mybir.dt.float32
F16 = mybir.dt.float16
BF16 = mybir.dt.bfloat16
U8 = mybir.dt.uint8
U32 = mybir.dt.uint32
I32 = mybir.dt.int32

P = 128
B, SQ, D = 8, 256, 128
SK, DC = 512, 96
QT = SQ // P
KC = SK // P
NT = B * QT
HEADS = 16
HG = 4
NG = HEADS // HG
EPS = 1e-5
CLAMP = 10000.0
IPA = 4
RANK = 32
HIDE_ROW, HIDE_KEY = 30000.0, -30000.0
SHIFT_K = 64.0
MASK_Q, MASK_K = 60000.0, 60000.0


SEMAPHORES = []


def alloc(nc, ctx, name):
    def sb(n, shape, dt=F32):
        return ctx.enter_context(nc.sbuf_tensor(f"{name}_{n}", shape, dt))

    def ps(n, shape, dt=F32):
        return ctx.enter_context(nc.psum_tensor(f"{name}_{n}", shape, dt))

    def sem(n):
        SEMAPHORES.append(nc.alloc_semaphore(f"{name}_{n}"))
        return SEMAPHORES[-1]
    return sb, ps, sem


def wait(eng, sem, value):
    if not isinstance(value, int) or value > 0:
        eng.wait_ge(sem, value)


def at_batch(ap, b):
    return ap[b] if isinstance(b, int) else ap[bass.ds(b, 1)].rearrange("a p n -> (a p) n")


class Shape:

    def __init__(self, name, wide, clip=False, ipa=False, bias=False, mask=False, out_bias=True, gate=0):
        self.name, self.wide, self.clip, self.ipa = name, wide, clip, ipa
        self.bias, self.mask, self.out_bias, self.gate = bias, mask, out_bias, gate
        self.dh = 64 if wide else D // HEADS
        self.scale = self.dh ** -0.5
        self.pairs = 2
        self.parts = 2 if wide else 1
        self.shift_row = 0 if wide else 25
        self.shift_k = MASK_K if mask else SHIFT_K
        self.keys = SK - IPA if ipa else SK
        if wide:
            self.pieces = [[("V", 0)], [("Q", 0)], [("Q", 1)], [("V", 1)]]
        else:
            self.pieces = [[("V", 0)], [("K", 0)], [("Q", 0)], []]

    def slots(self, kind):
        out = []
        for g in range(NG):
            for s in range(HG):
                pcs = self.pieces[s] if not (kind == "last" and g >= NG - 2) else []
                tail = []
                more = not (kind == "last" and g == NG - 1)
                if s == 2 and more:
                    tail.append(("MT",))
                if s == 3 and more and self.clip:
                    tail += [("NB", 0), ("NB", 1)]
                if (g, s) == (0, HG - 1) and kind != "first":
                    tail.append(("OP",))
                if self.ipa:
                    tail += {(0, 1): [("MI",)], (0, 2): [("VI",)], (1, 0): [("SI",)], (1, 1): [("G",)],
                             (3, 1): [("PT",)]}.get((g, s), [])
                if (g, s) == (2, 0) and kind != "last":
                    tail.append(("XT",))
                out.append((g, s, pcs[0] if pcs else None, pcs[1] if len(pcs) > 1 else None, more and s < 2, tail))
        return out

    def opening(self):
        first = [p for ps_ in self.pieces for p in ps_]
        return ([("XT",)] + [(0,) + p for p in first] + [(1,) + p for p in first]
                + [("MT",)] + [("NB", i) for i in range(2)] * self.clip)

    def order(self, kind):
        out = []
        for g, s, p1, p2, _, tail in self.slots(kind):
            out += [(g, s) + p for p in (p1, p2) if p] + [(g, s) + t for t in tail]
        return out

    def turn(self, kind, b, key):
        n0 = len(self.opening())
        if kind == "opening":
            return self.opening().index(key)
        pos = self.order(kind).index(key)
        nf, nm = len(self.order("first")), len(self.order("mid"))
        if kind == "first":
            return n0 + pos
        if kind == "last":
            return n0 + nf + (B - 2) * nm + pos
        return (b - 1) * nm + (n0 + nf + pos)

    def place(self, kind, key):
        n0, nf, nm = len(self.opening()), len(self.order("first")), len(self.order("mid"))
        if key is None:
            at = self.end_turn()
        elif kind == "mid":
            at = n0 + nf + (self.par == 0) * nm + self.order(kind).index(key)
            return at % 2, self.round * nm + at // 2
        else:
            at = self.turn(kind, 0, key)
        return at % 2, at // 2

    def shift_place(self, kind, g):
        if g:
            return self.place(kind, (g - 1, 2, "MT"))
        if kind == "first":
            return self.place("opening", ("MT",))
        n0, nf, nm = len(self.opening()), len(self.order("first")), len(self.order("mid"))
        back = nm - self.order("mid").index((NG - 1, 2, "MT"))
        if kind == "mid":
            at = n0 + nf + (self.par == 0) * nm - back
            return at % 2, self.round * nm + at // 2
        at = n0 + nf + (B - 2) * nm - back
        return at % 2, at // 2

    def end_turn(self):
        return len(self.opening()) + len(self.order("first")) + (B - 2) * len(self.order("mid")) + len(self.order("last"))


def attention(nc, sh, dram, res, const):
    wide, clip, ipa = sh.wide, sh.clip, sh.ipa
    x_res, gates = res
    ident, identb, cvec, bsel, ones, eps = const
    with ExitStack() as ctx:
        sb, ps, sem = alloc(nc, ctx, sh.name)
        rows = DC if wide else DC + 2

        if wide:
            inner = HEADS * sh.dh
            wq, wk, wv = (sb(n, [P, inner]) for n in ("wq", "wk", "wv"))
            wo = sb("wo", [P, inner // P, D])
            wqT = sb("wqT", [P, HEADS // 2, D])
            wkT = sb("wkT", [P, HEADS // 2, DC])
            wqk = sb("wqk", [P, HEADS, DC])
            if ipa:
                wkiT = sb("wkiT", [P, HEADS // 2, DC])
                wkq_i = sb("wkq_i", [P, HEADS, D])
                sel_w = sb("sel_w", [P, HEADS * IPA])
                wki, wvi = sb("wki", [P, inner]), sb("wvi", [P, inner])
                lora_up = {n: sb(f"{n}_up", [RANK, inner]) for n in "qkv"}
                lora_dn = {n: sb(f"{n}_dn", [RANK, D]) for n in "qkv"}
                o_dn, o_up = sb("o_dn", [RANK, inner]), sb("o_up", [RANK, D])
                alpha = sb("alpha", [P, 4])
            v_ipa = sb("v_ipa", [P, HEADS // 2, 64]) if ipa else None
            g_ipa = sb("g_ipa", [64, D]) if ipa else None
            s_ipa = sb("s_ipa", [P, QT, HEADS, IPA]) if ipa else None
            e_ipa = sb("e_ipa", [P, QT * HEADS, IPA]) if ipa else None
            m_ipa = sb("m_ipa", [P, QT * HEADS]) if ipa else None
            r_ipa = sb("r_ipa", [P, QT * HEADS]) if ipa else None
            p_ipa = sb("p_ipa", [P, QT * HEADS, IPA]) if ipa else None
            pt_ipa = sb("pt_ipa", [64, SQ]) if ipa else None
        else:
            wq_in, wk_in = sb("wq_in", [P, D]), sb("wk_in", [P, D])
            wv = sb("wv", [P, D])
            wq, wk = sb("wq", [P, NG, P]), sb("wk", [P, NG, P])
            wo = sb("wo", [P, NG, D])
            q_row = sb("q_row", [1, NG, P])
        bo = sb("bo", [1, D]) if sh.out_bias else None
        keyrow = None if wide else sb("keyrow", [P, HG, P], F16)

        ctxb = [sb(f"ctxb{i}", [P, SK]) for i in range(2)]
        stats = sb("stats", [P, QT, 6])
        mv = sb("mv", [P, QT, 2])
        lnv = sb("lnv", [P, QT])
        rstd = sb("rstd", [P, QT])
        xn = sb("xn", [P, QT, D])
        xnT = sb("xnT", [P, SQ])
        if wide:
            ctx_hi = [sb(f"ctx_hi{i}", [P, SK], F16) for i in range(2)]
            ctx_lo = [sb(f"ctx_lo{i}", [P, SK], F16) for i in range(2)]
            q_hi = [sb(f"q_hi{i}", [P, HG, SQ], F16) for i in range(4)]
            q_lo = [sb(f"q_lo{i}", [P, HG, SQ], F16) for i in range(4)]
        else:
            chi_k, chi_q = sb("chi_k", [P, SK], F16), sb("chi_q", [P, SQ], F16)
            kst = [sb(f"kst{i}", [P, SK], F16) for i in range(4)]
            qst = [sb(f"qst{i}", [P, SQ], F16) for i in range(4)]
        vst = [sb(f"vst{i}", [P, KC, HG * 64] if wide else [P, KC, HG, 32]) for i in range(4)]
        neg_max = sb("neg_max", [P, HG, QT])
        rest = sb("rest", [P, HG, QT])
        shift_parts = sb("shift_parts", [P, QT, HG, 32], F16)
        probs = [sb(f"probs{i}", [P, KC, SQ]) for i in range(2 * HG)]
        attn = sb("attn", [P, HEADS * (64 if wide else 32) // P, SQ])
        r_sum = sb("r_sum", [P, SQ])
        if wide:
            fold = sb("fold", [P, 2, SQ])
            folded = [sb(f"folded{i}", [P, SQ]) for i in range(2 * HG)]
        else:
            u_sb = sb("u_sb", [P, SQ])
        if clip:
            floor = [sb(f"floor{i}", [P, HG, SQ]) for i in range(2)]
            minus_clamp = sb("minus_clamp", [P, 1])

        rowmax_ps = ps("rowmax_ps", [P, QT, SK])
        st_ps = [ps(f"st_ps{i}", [P, KC // 2, SQ]) for i in range(3)]
        u_ps = ps("u_ps", [P, 2, SQ])
        banks = [ps(f"bank{i}", [P, 512]) for i in range(2)]

        loaded = sem("loaded")
        weights_ok = sem("weights_ok")
        preset = sem("preset")
        lora_ready = sem("lora_ready")
        ctx_loaded = sem("ctx_loaded")
        ctx_ready = sem("ctx_ready")
        stats_ready = sem("stats_ready")
        rstd_ready = sem("rstd_ready")
        xn_ready = sem("xn_ready")
        bank_full = sem("bank_full")
        bank_free = [sem(f"bank_free{i}") for i in range(2)]
        hi_ready = sem("hi_ready")
        rows_ready = sem("rows_ready")
        max_ready = sem("max_ready")
        parts_step = sem("parts_step")
        parts_ready = sem("parts_ready")
        capped = sem("capped")
        setup_pe = sem("setup_pe")
        setup_sb = sem("setup_sb")
        st_ready = sem("st_ready")
        exp_ready = sem("exp_ready")
        hi_step = sem("hi_step")
        fold_step = sem("fold_step")
        pool_ready = sem("pool_ready")
        pv_ready = sem("pv_ready")
        u_ready = sem("u_ready")
        div_ready = sem("div_ready")
        rsum_ready = sem("rsum_ready")
        attn_ready = sem("attn_ready")
        passed = sem("passed")
        pool_passed = sem("pool_passed")
        pe_passed = sem("pe_passed")
        ipa_step = sem("ipa_step")
        ipa_exp = sem("ipa_exp")

        def batches(body, eng):
            body("first", 0, 0)
            with eng.Fori(0, (B - 2) // 2) as i:
                for par in (1, 0):
                    sh.round, sh.par = i, par
                    body("mid", i * 2 + (2 - par), par)
            body("last", B - 1, (B - 1) % 2)

        def shared(kind, key):
            p, _ = sh.place(kind, key)
            return banks[p], bank_free[p]

        def been_read(eng, kind, key, upto=1):
            p, n = sh.place(kind, key)
            wait(eng, bank_free[p], n + upto)

        def floor_place(kind, g):
            if g:
                p, n = sh.place(kind, (g - 1, 3, "NB", 1))
                return p, n + 1
            p, n = sh.place(kind, ("NB", 1)) if kind == "opening" else sh.shift_place(kind, 0)
            return p, n + 2

        def shifted(eng, kind, g):
            p, n = sh.shift_place(kind, g)
            eng.wait_ge(bank_free[p], n + 1)

        def lora_ps(i):
            if i < 3:
                return st_ps[i][:, :, :].rearrange("p c q -> p (c q)")
            if i < 5:
                return rowmax_ps[:, i - 3, :]
            return u_ps[:, :, :].rearrange("p a q -> p (a q)") if i == 5 else banks[i - 6][:, :]

        def cap(dve, g, s):
            pr = probs[(g % 2) * HG + s][:, :, :]
            return dve.scalar_tensor_tensor(pr, pr, 1.0, floor[g % 2][:, s:s + 1, :].broadcast_to([P, KC, SQ]),
                                            ALU.min, ALU.max)

        def stats_of(dve, b):
            x = x_of(b)
            for t in range(QT):
                ins = dve.bn_stats(stats[:, t, :], x[:, t, :])
            ins.then_inc(stats_ready, 1)
            dve.wait_ge(stats_ready, 2 * b + 1)
            dve.sem_inc(passed, 1)
            for t in range(QT):
                ins = dve.bn_aggr(mv[:, t, :], stats[:, t, :])
            ins.then_inc(stats_ready, 1)

        def x_of(b):
            return x_res[:, b * QT:(b + 1) * QT, :] if isinstance(b, int) else x_res[:, bass.ds(b * QT, QT), :]

        turned = [(wq, D), (wk, DC)] if wide else []
        if ipa:
            turned.append((wki, DC))
        block = ctx.enter_context(nc.Block())

        n_loads = 0

        @block.sync
        def _(sp):
            nonlocal n_loads

            def load(dst, src):
                nonlocal n_loads
                n_loads += 1
                sp.dma_start(dst, src).then_inc(loaded, 16)

            def load_ctx(b, par):
                sp.dma_start(ctxb[par][0:DC, :], at_batch(dram["ctxT"], b)).then_inc(ctx_loaded, 16)
                if sh.mask:
                    sp.dma_start(ctxb[par][DC:DC + 1, :], at_batch(dram["mask_row"], b)).then_inc(ctx_loaded, 16)

            if sh.mask:
                sp.wait_ge(preset, 2)
            load_ctx(0, 0)
            if wide:
                for hi in ctx_hi:
                    load(hi[DC:P, :], dram["ctx_tail"])
                load(wq[:, :], dram["Wq"])
                load(wk[0:DC, :], dram["Wk"])
                load(wv[0:DC, :], dram["Wv"])
                load(wo[:, :, :], dram["Wo"].rearrange("(i p) n -> p i n", p=P))
                if ipa:
                    load(wki[0:DC, :], dram["Wk_ipa"])
                    load(wvi[0:DC, :], dram["Wv_ipa"])
                    for n in "qkv":
                        load(lora_up[n][:, :], dram[f"{n}_up"])
                        load(lora_dn[n][:, 0:D if n == "q" else DC], dram[f"{n}_downT"])
                    load(o_up[:, :], dram["o_up"])
                    load(o_dn[:, :], dram["o_downT"])
                    for i, n in enumerate("qkvo"):
                        load(alpha[:, i:i + 1], dram[f"{n}_alpha"].partition_broadcast(P))
            else:
                load(wq_in[:, :], dram["Wq"])
                load(wk_in[0:DC, :], dram["Wk"])
                load(wv[0:DC, :], dram["Wv"])
                if sh.bias:
                    load(wk_in[DC:DC + 1, :], dram["bk"].unsqueeze(0))
                    load(wv[DC:DC + 1, :], dram["bv"].unsqueeze(0))
                if not sh.mask:
                    sp.wait_ge(preset, 2)
                for j in range(HG):
                    load(wo[32 * j:32 * j + sh.dh, :, :],
                         dram["Wo"].rearrange("(g j d) n -> j d g n", g=NG, j=HG)[j])
                if sh.bias:
                    qv = q_row[:, :, :].rearrange("a g (j s d) -> a g j s d", j=HG, s=4)
                    for s in range(3):
                        for g in range(NG):
                            load(qv[:, g, :, s, :], dram["bq"].rearrange("(a g j d) -> a g j d", a=1, g=NG, j=HG)[:, g])
                else:
                    load(q_row[:, :, :], dram["mask_q_row"])
                if sh.mask:
                    load(wk[DC:DC + 1, :, :], dram["mask_k_row"])
                load(wk[DC + 1:DC + 2, :, :], dram["shift_k_row"])
                if clip:
                    load(keyrow[:, :, :], dram["keyrow"])
            if sh.out_bias:
                load(bo[:, :], dram["bo"].unsqueeze(0))

            def body(kind, b, par):
                if kind != "last":
                    sp.wait_ge(bank_full, sh.turn(kind, b, sh.order(kind)[0]))
                    load_ctx(b + 1, 1 - par)
            batches(body, sp)

        n_loads = sum([6 * wide, ipa * (2 + 6 + 2 + 4), (not wide) * (4 + HG + 2 * sh.bias), sh.bias * 12,
                       (not wide and not sh.bias) * 1, sh.mask * 1, clip * 1, sh.out_bias * 1])
        ctx_dmas = 16 * (1 + sh.mask)

        @block.gpsimd
        def _(pool):
            def context_pair(b, par):
                pool.wait_ge(ctx_loaded, (b + 1) * ctx_dmas)
                pool.sem_inc(pool_passed, 1)
                pool.tensor_copy(ctx_hi[par][0:DC, :], ctxb[par][0:DC, :]).then_inc(hi_step, 1)
                pool.wait_ge(hi_step, b + 1)
                pool.tensor_tensor(ctx_lo[par][0:DC, :], ctxb[par][0:DC, :], ctx_hi[par][0:DC, :],
                                   ALU.subtract).then_inc(ctx_ready, 1)

            if wide:
                context_pair(0, 0)

            def body(kind, b, par):
                for g, s, *_ in sh.slots(kind):
                    n = (b * NG + g) * HG + s
                    pr = probs[(g % 2) * HG + s]
                    pool.wait_ge(exp_ready, n * 2 + 2)
                    wait(pool, pool_ready, n)
                    pool.tensor_tensor(fold[:, :, :], pr[:, 0:2, :], pr[:, 2:4, :], ALU.add).then_inc(fold_step, 1)
                    pool.wait_ge(fold_step, n + 1)
                    pool.tensor_tensor(folded[(g % 2) * HG + s][:, :], fold[:, 0, :], fold[:, 1, :],
                                       ALU.add).then_inc(pool_ready, 1)
                    if (g, s) == (1, HG - 1) and kind != "last":
                        context_pair(b + 1, 1 - par)
            if wide:
                batches(body, pool)

        @block.scalar
        def _(act):
            def ln_rstd(b):
                act.wait_ge(stats_ready, 2 * (b + 1))
                act.activation(lnv[:, :], mv[:, :, 1], ACT.Ln, bias=eps[:, 0:1]).then_inc(rstd_ready, 1)
                act.wait_ge(rstd_ready, 2 * b + 1)
                act.activation(rstd[:, :], lnv[:, :], ACT.Exp, scale=-0.5).then_inc(rstd_ready, 1)

            def evacuate(kind, b, key, u, what):
                turn = sh.turn(kind, b, key)
                name = what[0]
                if name in ("MT", "OP", "SI"):
                    return
                act.wait_ge(bank_full, turn + 1)
                bank, free = shared(kind, key)
                ub = u % 4 if isinstance(u, int) else what[-1]
                if name == "V":
                    i = what[1]
                    if wide:
                        act.copy(vst[ub][:, 2 * i:2 * i + 2, :], bank[:, :].rearrange("p (c n) -> p c n", c=2))\
                           .then_inc(free, 1)
                    else:
                        act.copy(vst[ub][:, :, :, 0:sh.dh],
                                 bank[:, 0:KC * 32].rearrange("p (c h d) -> p c h d", c=KC, h=HG)).then_inc(free, 1)
                elif name == "K":
                    act.activation(chi_k[:, :], bank[:, :], ACT.Copy, scale=cvec[:, 0:1]).then_inc(hi_ready, 1)
                elif name == "Q" and wide:
                    i = what[1]
                    act.copy(q_hi[ub][0:DC, 2 * i:2 * i + 2, :],
                             bank[0:DC, :].rearrange("p (h q) -> p h q", h=2)).then_inc(hi_ready, 1)
                elif name == "Q":
                    act.activation(chi_q[:, :], bank[:, 0:SQ], ACT.Copy, scale=cvec[:, 1:2]).then_inc(hi_ready, 1)
                elif name == "XT":
                    act.copy(xnT[:, :], bank[:, 0:SQ]).then_inc(free, 1)
                elif name == "NB":
                    i = what[1]
                    act.activation(floor[what[-1] % 2][:, 2 * i:2 * i + 2, :],
                                   bank[:, :].rearrange("p (h q) -> p h q", h=2), ACT.Exp,
                                   bias=minus_clamp[:, 0:1], scale=sh.scale).then_inc(free, 1)
                elif name == "MI":
                    act.copy(sel_w[:, :], bank[:, 0:HEADS * IPA]).then_inc(free, 1)
                elif name == "VI":
                    src = bank[:, 0:HEADS // 2 * IPA].rearrange("p (i t) -> p i t", t=IPA)
                    flat = v_ipa[:, :, :].rearrange("p i n -> p (i n)")
                    for hh in range(2):
                        for i in range(HEADS // 2):
                            at = i * 64 + (2 * i + hh) * IPA
                            ins = act.copy(flat[64 * hh:64 * hh + 64, at:at + IPA], src[64 * hh:64 * hh + 64, i, :])
                    ins.then_inc(free, 1)
                elif name == "G":
                    act.copy(g_ipa[:, :], bank[0:64, 0:D]).then_inc(free, 1)
                elif name == "PT":
                    act.copy(pt_ipa[:, :], bank[0:64, 0:SQ]).then_inc(free, 1)

            ln_rstd(0)
            for key in sh.opening():
                if key[0] in (0, 1):
                    evacuate("opening", 0, key, key[0], key[1:])
                else:
                    evacuate("opening", 0, key, 0, key + (0,))

            def body(kind, b, par):
                for g, s, p1, p2, more, tail in sh.slots(kind):
                    n = (b * NG + g) * HG + s
                    if p1:
                        evacuate(kind, b, (g, s) + p1, None, p1 + ((g + 2) % 4,))
                    for half in range(2):
                        act.wait_ge(st_ready, n * 2 + (half + 1))
                        act.activation(probs[(g % 2) * HG + s][:, 2 * half:2 * half + 2, :],
                                       st_ps[(2 * s + half) % 3][:, :, :], ACT.Exp, scale=sh.scale).then_inc(exp_ready, 1)
                    if p2:
                        evacuate(kind, b, (g, s) + p2, None, p2 + ((g + 2) % 4,))
                    if not wide and s == 1 and not (kind == "first" and g == 0):
                        act.wait_ge(pv_ready, b * NG + g)
                        act.copy(u_sb[:, :], u_ps[:, 0, :]).then_inc(u_ready, 1)
                    for t in tail:
                        evacuate(kind, b, (g, s) + t, None, t + ((g + 1) % 4,))
                    if (g, s) == (0, HG - 1) and kind != "last":
                        ln_rstd(b + 1)
                    if ipa and (g, s) == (2, HG - 1):
                        been_read(act, kind, (1, 0, "SI"))
                        act.activation(e_ipa[:, :, :], s_ipa[:, :, :, :].rearrange("p a h t -> p (a h) t"), ACT.Exp,
                                       scale=sh.scale).then_inc(ipa_exp, 1)
            batches(body, act)
            if not wide:
                act.wait_ge(pv_ready, B * NG)
                act.copy(u_sb[:, :], u_ps[:, 0, :]).then_inc(u_ready, 1)

        @block.tensor
        def _(pe):
            def use(kind, b, key, u, what, par):
                name = what[0]
                been_read(pe, kind, key, upto=0)
                if name == "Q" and (kind == "opening" or (key[0], what[1]) == (2, 0)):
                    been_read(pe, kind, ("XT",) if kind == "opening" else (2, 0, "XT"))
                if what == ("NB", 0):
                    been_read(pe, kind, ("MT",) if kind == "opening" else (key[0], 2, "MT"))
                bank, _ = shared(kind, key)
                if name == "V":
                    i = what[1]
                    if wide:
                        for c in range(2):
                            at = (2 * i + c) * P
                            ins = pe.matmul(bank[:, c * 256:(c + 1) * 256], ctxb[par][0:DC, at:at + P],
                                            wv[0:DC, u * 256:(u + 1) * 256], start=True, stop=True)
                    else:
                        r = DC + 1 if sh.bias else DC
                        for c in range(KC):
                            ins = pe.matmul(bank[:, c * 32:(c + 1) * 32], ctxb[par][0:r, c * P:(c + 1) * P],
                                            wv[0:r, u * 32:(u + 1) * 32], start=True, stop=True)
                elif name == "K":
                    ins = pe.matmul(bank[:, :], wk[0:rows, u, :], ctxb[par][0:rows, :], start=True, stop=True)
                elif name == "Q":
                    if wide:
                        for j in range(2):
                            ins = pe.matmul(bank[0:DC, j * SQ:(j + 1) * SQ], wqk[:, u * HG + 2 * what[1] + j, :],
                                            xnT[:, :], start=True, stop=True)
                    else:
                        pe.matmul(bank[:, 0:SQ], wq[:, u, :], xnT[:, :], start=True, stop=False)
                        ins = pe.matmul(bank[:, 0:SQ], q_row[0:1, u, :], ones[0:1, 0:SQ], start=False, stop=True)
                elif name == "XT":
                    pe.wait_ge(xn_ready, b_next(kind, b))
                    for t in range(QT):
                        ins = pe.transpose(bank[:, t * P:(t + 1) * P], xn[:, t, :], ident[:, :])
                elif name == "MT":
                    pe.wait_ge(parts_ready, unit_next(kind, b, key) + 1)
                    view = bank[:, :].bitcast(F16)
                    for t in range(QT):
                        for h in range(HG if wide else 1):
                            if wide:
                                ins = pe.transpose(view[DC:P, h * SQ + t * P:h * SQ + (t + 1) * P],
                                                   shift_parts[:, t, h, :], dram["identh"][:, :])
                            else:
                                ins = pe.transpose(view[:, t * P:(t + 1) * P],
                                                   shift_parts[:, t, :, :].rearrange("p h k -> p (h k)"),
                                                   dram["identh"][:, :])
                elif name == "NB":
                    g1 = (key[0] + 1) % 4 if kind != "opening" else 0
                    for j in range(2):
                        ins = pe.matmul(bank[:, j * SQ:(j + 1) * SQ], keyrow[:, 2 * what[1] + j, :], qst[g1][:, :],
                                        start=True, stop=True)
                elif name == "MI":
                    for h in range(HEADS):
                        ins = pe.matmul(bank[:, h * IPA:(h + 1) * IPA], wkq_i[0:DC, h, :], ctxb[par][0:DC, sh.keys:SK],
                                        start=True, stop=True)
                elif name == "SI":
                    for t in range(QT):
                        ins = pe.matmul(bank[:, t * 64:(t + 1) * 64], xnT[:, t * P:(t + 1) * P], sel_w[:, :],
                                        start=True, stop=True)
                elif name == "VI":
                    for i in range(HEADS // 2):
                        ins = pe.matmul(bank[:, i * IPA:(i + 1) * IPA], wvi[0:DC, i * P:(i + 1) * P],
                                        ctxb[par][0:DC, sh.keys:SK], start=True, stop=True)
                elif name == "G":
                    for i in range(HEADS // 2):
                        ins = pe.matmul(bank[0:64, 0:D], v_ipa[:, i, :], wo[:, i, :],
                                        start=(i == 0), stop=(i == HEADS // 2 - 1))
                elif name == "PT":
                    pe.wait_ge(ipa_step, 4 * b + 4)
                    pe.sem_inc(pe_passed, 1)
                    for t in range(QT):
                        ins = pe.transpose(bank[0:64, t * P:(t + 1) * P],
                                           p_ipa[:, t * HEADS:(t + 1) * HEADS, :].rearrange("p h t -> p (h t)"),
                                           ident[:, :])
                elif name == "OP":
                    ins = out_projection(bank, b * NG * sh.parts)
                ins.then_inc(bank_full, 1)

            def b_next(kind, b):
                return 1 if kind == "opening" else b + 2

            def unit_next(kind, b, key):
                return 0 if kind == "opening" else b * NG + key[0] + 1

            def out_projection(bank, parts_before):
                pe.wait_ge(attn_ready, parts_before)
                chunks = attn.shape[1]
                for t in range(QT):
                    dst = bank[:, t * D:(t + 1) * D]
                    rest_ = (1 if ipa else 0) + (1 if bo is not None else 0)
                    for i in range(chunks):
                        ins = pe.matmul(dst, attn[:, i, t * P:(t + 1) * P], wo[:, i, :],
                                        start=(i == 0), stop=(i == chunks - 1 and rest_ == 0))
                    if ipa:
                        ins = pe.matmul(dst, pt_ipa[:, t * P:(t + 1) * P], g_ipa[:, :], start=False, stop=(bo is None))
                    if bo is not None:
                        ins = pe.matmul(dst, ones[0:1, 0:P], bo[0:1, :], start=False, stop=True)
                return ins

            def row_scores(ub, u, h, t, par):
                wait(pe, max_ready, u * (HG * QT) + (h * QT + t - 1))
                if wide:
                    ins = pe.matmul(rowmax_ps[:, t, :], q_hi[ub][0:DC, h, t * P:(t + 1) * P],
                                    ctx_hi[par][0:DC, :], start=True, stop=True)
                else:
                    r = slice(32 * h, 32 * h + 32)
                    ins = pe.matmul(rowmax_ps[:, t, :], qst[ub][r, t * P:(t + 1) * P], kst[ub][r, :],
                                    start=True, stop=True)
                ins.then_inc(rows_ready, 1)

            def key_scores(ub, u, h, half, par):
                j = 2 * h + half
                wait(pe, exp_ready, u * 2 * HG + (j - 2 if j >= 3 else (-1, 0, -2)[j]))
                for c in range(2 * half, 2 * half + 2):
                    dst = st_ps[j % 3][:, c % 2, :]
                    k = slice(c * P, (c + 1) * P)
                    if wide:
                        pe.matmul(dst, ctx_hi[par][0:DC, k], q_lo[ub][0:DC, h, :], start=True, stop=False)
                        pe.matmul(dst, ctx_lo[par][0:DC, k], q_hi[ub][0:DC, h, :], start=False, stop=False)
                        ins = pe.matmul(dst, ctx_hi[par][:, k], q_hi[ub][:, h, :], start=False, stop=True)
                    else:
                        r = slice(32 * h, 32 * h + 32)
                        ins = pe.matmul(dst, kst[ub][r, k], qst[ub][r, :], start=True, stop=True)
                ins.then_inc(st_ready, 1)

            def values(ub, u, part):
                wait(pe, attn_ready, sh.parts * u + part)
                heads = range(2 * part, 2 * part + 2) if wide else range(HG)
                w = 64 if wide else 32
                if clip or wide:
                    pe.wait_ge(capped if clip else pool_ready, u * HG + heads[-1] + 1)
                else:
                    pe.wait_ge(exp_ready, u * 2 * HG + 2 * HG)
                for c in range(KC):
                    for n, h in enumerate(heads):
                        lhs = vst[ub][:, c, h * 64:(h + 1) * 64] if wide else vst[ub][:, c, h, :]
                        ins = pe.matmul(u_ps[w * n:w * n + w, 0, :], lhs, probs[(ub % 2) * HG + h][:, c, :],
                                        start=(c == 0), stop=(c == KC - 1), skip_group_check=True)
                if wide:
                    for n, h in enumerate(heads):
                        ins = pe.matmul(u_ps[w * n:w * n + w, 1, :], ones[:, 0:64], folded[(ub % 2) * HG + h][:, :],
                                        start=True, stop=True)
                ins.then_inc(pv_ready, 1)

            def divisors(u):
                pe.wait_ge(u_ready, u + 1)
                pe.matmul(u_ps[:, 1, :], bsel[:, :], u_sb[:, :], start=True, stop=True).then_inc(div_ready, 1)

            pe.wait_ge(loaded, 16 * n_loads)
            if ipa:
                for i, n in enumerate("qkv"):
                    r = D if n == "q" else DC
                    for half in range(2):
                        pe.matmul(lora_ps(2 * i + half)[0:r, :], lora_dn[n][:, 0:r],
                                  lora_up[n][:, half * 512:(half + 1) * 512], start=True, stop=True)
                for i in range(HEADS // 2):
                    ins = pe.matmul(lora_ps(6 + i // 4)[:, (i % 4) * D:(i % 4 + 1) * D],
                                    o_dn[:, i * P:(i + 1) * P], o_up[:, :], start=True, stop=True)
                ins.then_inc(lora_ready, 1)
            if ipa or not wide:
                pe.wait_ge(weights_ok, 1)
            if wide:
                banks = [[lora_ps(0), lora_ps(1)], [lora_ps(2), lora_ps(3)], [lora_ps(4), lora_ps(5)]]
                for k, (w, r) in enumerate(turned):
                    for i in range(HEADS // 2):
                        at = (i % 4) * r
                        ins = pe.transpose(banks[k][i // 4][:, at:at + r], w[0:r, i * P:(i + 1) * P], ident[0:r, 0:r])
                ins.then_inc(setup_pe, 1)
                pe.wait_ge(setup_sb, 1)
                for i in range(HEADS // 2):
                    for j in range(2):
                        rows_j = slice(64 * j, 64 * j + 64)
                        ins = pe.matmul(lora_ps(2 * j + i // 4)[:, (i % 4) * DC:(i % 4 + 1) * DC], wqT[rows_j, i, :],
                                        wkT[rows_j, i, :], start=True, stop=True)
                ins.then_inc(setup_pe, 1)
                if ipa:
                    for i in range(HEADS // 2):
                        for j in range(2):
                            rows_j = slice(64 * j, 64 * j + 64)
                            ins = pe.matmul(lora_ps(4 + 2 * j + i // 4)[0:DC, (i % 4) * D:(i % 4 + 1) * D],
                                            wkiT[rows_j, i, :], wqT[rows_j, i, :], start=True, stop=True)
                    ins.then_inc(setup_pe, 1)
                pe.wait_ge(setup_sb, 3 if ipa else 2)
            pe.wait_ge(ctx_loaded, ctx_dmas)
            if wide:
                pe.wait_ge(ctx_ready, 1)
            for key in sh.opening():
                if key[0] == "MT":
                    for before in sh.opening()[-2 - len(sh.opening()) + sh.opening().index(key):][:2]:
                        been_read(pe, "opening", before)
                    for h in range(HG):
                        for t in range(QT):
                            row_scores(0, 0, h, t, 0)
                use("opening", 0, key, key[0] if key[0] in (0, 1) else 0, key[1:] if key[0] in (0, 1) else key,
                    0)

            def body(kind, b, par):
                for g, s, p1, p2, more, tail in sh.slots(kind):
                    u = b * NG + g
                    par1 = par if g < NG - 1 else 1 - par
                    g2 = (g + 2) % 4
                    par2 = par if g < NG - 2 else 1 - par
                    if (g, s) == (2, 0) and kind != "last":
                        pe.wait_ge(ctx_loaded, (b + 2) * ctx_dmas)
                    if wide and (g, s) == (3, 0) and kind != "last":
                        pe.wait_ge(ctx_ready, b + 2)
                    if p1:
                        use(kind, b, (g, s) + p1, g2, p1, par2)
                    if s == 0:
                        shifted(pe, kind, g)
                    for half in range(2):
                        if more:
                            row_scores((g + 1) % 4, u + 1, 2 * s, half, par1)
                        key_scores(g, u, s, half, par)
                    if more:
                        row_scores((g + 1) % 4, u + 1, 2 * s + 1, 0, par1)
                    if p2:
                        use(kind, b, (g, s) + p2, g2, p2, par2)
                    if more:
                        row_scores((g + 1) % 4, u + 1, 2 * s + 1, 1, par1)
                    if ("MT",) in tail:
                        use(kind, b, (g, s, "MT"), None, ("MT",), par)
                    if not (kind == "first" and g == 0):
                        if wide and s in (0, 3):
                            values((g - 1) % 4, u - 1, s // 3)
                        if not wide and s == 1:
                            values((g - 1) % 4, u - 1, 0)
                        if not wide and s == 2:
                            divisors(u - 1)
                    for t in tail:
                        if t[0] == "MT":
                            continue
                        use(kind, b, (g, s) + t, None, t, par)
            batches(body, pe)
            for part in range(sh.parts):
                values(3, B * NG - 1, part)
            if not wide:
                divisors(B * NG - 1)
            been_read(pe, "last", None, upto=0)
            out_projection(shared("last", None)[0], B * NG * sh.parts).then_inc(bank_full, 1)

        @block.vector
        def _(dve):
            dve.memset(shift_parts[:, :, :, :], 0.0).then_inc(preset, 1)
            dve.wait_ge(preset, 1)
            ins = dve.memset(shift_parts[:, :, :, 3] if wide else minus_clamp[:, :] if clip else shift_parts[:, :, :, 31],
                             HIDE_ROW if wide else -CLAMP if clip else 0.0)
            if ipa:
                ins = dve.memset(v_ipa[:, :, :], 0.0)
            if not wide:
                for c in ctxb:
                    dve.memset(c[DC:DC + 2, :], 1.0)
                for w in [wq, wk, wo, q_row] + vst:
                    ins = dve.memset(w[tuple(slice(None) for _ in w.shape)], 0.0)
            ins.then_inc(preset, 1)
            if not wide:
                dve.wait_ge(preset, 2)
                for v in vst:
                    ins = dve.memset(v[:, :, :, sh.dh:sh.dh + 1], 1.0)
                ins.then_inc(preset, 1)
            stats_of(dve, 0)
            dve.wait_ge(loaded, 16 * n_loads)
            if ipa:
                dve.tensor_scalar(alpha[:, :], alpha[:, :], 1.0 / RANK, None, ALU.mult).then_inc(preset, 1)
                dve.wait_ge(preset, 3)
                dve.wait_ge(lora_ready, 1)
                for i, (w, r) in enumerate(((wq, D), (wk, DC), (wv, DC))):
                    for half in range(2):
                        cols = w[0:r, half * 512:(half + 1) * 512]
                        dve.scalar_tensor_tensor(cols, lora_ps(2 * i + half)[0:r, :], alpha[0:r, i:i + 1], cols,
                                                 ALU.mult, ALU.add)
                for i in range(2):
                    four = wo[:, 4 * i:4 * i + 4, :].rearrange("p i n -> p (i n)")
                    ins = dve.scalar_tensor_tensor(four, lora_ps(6 + i), alpha[:, 3:4], four, ALU.mult, ALU.add)
            elif not wide:
                for w, w_in, r in ((wq, wq_in, P), (wk, wk_in, DC + 1 if sh.bias else DC)):
                    dst = w[0:r, :, :].rearrange("p g (j s d) -> p (g j) s d", j=HG, s=4)
                    src = w_in[0:r, :].rearrange("p (h d) -> p h d", d=sh.dh)
                    for s in range(3):
                        ins = dve.tensor_copy(dst[:, :, s, :], src)
            if ipa or not wide:
                ins.then_inc(weights_ok, 1)
            if wide:
                def halves(k, n):
                    return [lora_ps(k + i)[:, 0:4 * n].rearrange("p (i n) -> p i n", i=4) for i in range(2)]
                dve.wait_ge(setup_pe, 1)
                for k, (dst, (_, r)) in enumerate(zip((wqT, wkT, wkiT if ipa else None), turned)):
                    for i, src in enumerate(halves(2 * k, r)):
                        ins = dve.tensor_copy(dst[:, 4 * i:4 * i + 4, :], src)
                ins.then_inc(setup_sb, 1)
                dve.wait_ge(setup_pe, 2)
                heads = wqk[:, :, :].rearrange("p (i j) n -> p i j n", j=2)
                for j in range(2):
                    for i, src in enumerate(halves(2 * j, DC)):
                        ins = dve.tensor_copy(heads[:, 4 * i:4 * i + 4, j, :], src)
                ins.then_inc(setup_sb, 1)
                if ipa:
                    dve.wait_ge(setup_pe, 3)
                    heads = wkq_i[:, :, :].rearrange("p (i j) n -> p i j n", j=2)
                    for j in range(2):
                        for i, src in enumerate(halves(4 + 2 * j, D)):
                            ins = dve.tensor_copy(heads[0:DC, 4 * i:4 * i + 4, j, :], src[0:DC])
                    ins.then_inc(setup_sb, 1)

            def pair(kind, b, key, what, unit):
                name, i = what
                idx = i if wide else int(name == "Q")
                ub = (key[0] + 2) % 4 if kind != "opening" else key[0]
                dve.wait_ge(bank_full, sh.turn(kind, b, key) + 1)
                dve.wait_ge(hi_ready, sh.pairs * unit + idx + 1)
                bank, free = shared(kind, key)
                if wide:
                    src = bank[0:DC, :].rearrange("p (h q) -> p h q", h=2)
                    dst, hi = (q[ub][0:DC, 2 * i:2 * i + 2, :] for q in (q_lo, q_hi))
                elif name == "K":
                    src, hi, dst = bank[:, :], chi_k[:, :], kst[ub][:, :]
                else:
                    src, hi, dst = bank[:, 0:SQ], chi_q[:, :], qst[ub][:, :]
                dve.tensor_tensor(dst, src, hi, ALU.subtract).then_inc(free, 1)

            def normalise(b):
                dve.wait_ge(rstd_ready, 2 * (b + 1))
                x = x_of(b)
                for t in range(QT):
                    ins = dve.tensor_scalar(xn[:, t, :], x[:, t, :], mv[:, t, 0:1], rstd[:, t:t + 1],
                                            ALU.subtract, ALU.mult)
                ins.then_inc(xn_ready, 1)

            def row_max(g1, u1, h):
                for t in range(QT):
                    dve.wait_ge(rows_ready, u1 * (HG * QT) + (h * QT + t + 1))
                    dve.tensor_reduce(neg_max[:, h, t:t + 1], rowmax_ps[:, t, 0:sh.keys], AXX, ALU.max, negate=True)\
                       .then_inc(max_ready, 1)

            def split_max(u1):
                steps = 5 if clip else 4
                at = 1
                dve.wait_ge(max_ready, u1 * (HG * QT) + HG * QT)
                if clip:
                    bound = CLAMP / sh.scale
                    dve.tensor_scalar(neg_max[:, :, :], neg_max[:, :, :], -bound, bound, ALU.max, ALU.min)\
                       .then_inc(parts_step, 1)
                    at = 2
                    dve.wait_ge(parts_step, u1 * steps + 1)
                dve.tensor_scalar(neg_max[:, :, :], neg_max[:, :, :], 1.0 / sh.shift_k, None, ALU.mult)\
                   .then_inc(parts_step, 1)
                dve.wait_ge(parts_step, u1 * steps + at)
                part = [shift_parts[:, :, :, sh.shift_row + k] for k in range(3)]
                negated = neg_max[:, :, :].rearrange("p h t -> p t h")
                left = rest[:, :, :].rearrange("p h t -> p t h")
                dve.tensor_copy(part[0], negated).then_inc(parts_step, 1)
                dve.wait_ge(parts_step, u1 * steps + at + 1)
                dve.tensor_tensor(left, negated, part[0], ALU.subtract).then_inc(parts_step, 1)
                dve.wait_ge(parts_step, u1 * steps + at + 2)
                dve.tensor_copy(part[1], left).then_inc(parts_step, 1)
                dve.wait_ge(parts_step, u1 * steps + at + 3)
                dve.tensor_tensor(part[2], left, part[1], ALU.subtract)\
                   .then_inc(parts_ready, 1)

            def divide(g, u, part):
                n = u * sh.parts + part
                dve.wait_ge(pv_ready if wide else div_ready, n + 1)
                dve.reciprocal(r_sum[:, :], u_ps[:, 1, :]).then_inc(rsum_ready, 1)
                dve.wait_ge(rsum_ready, n + 1)
                dve.tensor_tensor(attn[:, g * sh.parts + part, :], u_ps[:, 0, :] if wide else u_sb[:, :], r_sum[:, :],
                                  ALU.mult).then_inc(attn_ready, 1)

            def take_maxima(kind, b, key, g1):
                dve.wait_ge(bank_full, (sh.end_turn() if key is None else sh.turn(kind, b, key)) + 1)
                bank, free = shared(kind, key)
                if wide:
                    dve.tensor_copy(q_hi[g1][DC:P, :, :],
                                    bank[:, :].bitcast(F16)[DC:P, :].rearrange("p (h q) -> p h q", h=HG))\
                       .then_inc(free, 1)
                else:
                    dve.tensor_tensor(qst[g1][:, :], bank[:, :].bitcast(F16)[:, 0:SQ], qst[g1][:, :], ALU.add)\
                       .then_inc(free, 1)

            def add_residual(kind, b, key, b_of):
                dve.wait_ge(bank_full, (sh.end_turn() if key is None else sh.turn(kind, b, key)) + 1)
                bank, free = shared(kind, key)
                x = x_of(b_of)
                dve.scalar_tensor_tensor(x, bank[:, 0:QT * D].rearrange("p (t n) -> p t n", t=QT),
                                         gates[:, sh.gate:sh.gate + 1], x, ALU.mult, ALU.add).then_inc(free, 1)

            def small_softmax_scores(kind, b, key):
                dve.wait_ge(bank_full, (sh.end_turn() if key is None else sh.turn(kind, b, key)) + 1)
                bank, free = shared(kind, key)
                flat = bank[:, 0:QT * HEADS * IPA].rearrange("p (a t) -> p a t", t=IPA)
                dve.tensor_reduce(m_ipa[:, :], flat, AXX, ALU.max).then_inc(ipa_step, 1)
                dve.wait_ge(ipa_step, 4 * b + 1)
                dve.tensor_tensor(s_ipa[:, :, :, :].rearrange("p a h t -> p (a h) t"), flat,
                                  m_ipa[:, :].unsqueeze(2).broadcast_to([P, QT * HEADS, IPA]),
                                  ALU.subtract).then_inc(free, 1)

            def small_softmax(b):
                dve.wait_ge(ipa_exp, b + 1)
                dve.reduce_sum(r_ipa[:, :], e_ipa[:, :, :], AXX).then_inc(ipa_step, 1)
                dve.wait_ge(ipa_step, 4 * b + 2)
                dve.reciprocal(m_ipa[:, :], r_ipa[:, :]).then_inc(ipa_step, 1)
                dve.wait_ge(ipa_step, 4 * b + 3)
                dve.tensor_tensor(p_ipa[:, :, :], e_ipa[:, :, :],
                                  m_ipa[:, :].unsqueeze(2).broadcast_to([P, QT * HEADS, IPA]), ALU.mult)\
                   .then_inc(ipa_step, 1)

            normalise(0)
            for key in sh.opening():
                if key[0] in (0, 1) and key[1] != "V":
                    pair("opening", 0, key, key[1:], key[0])
                elif key[0] == "MT":
                    for h in range(HG):
                        row_max(0, 0, h)
                    split_max(0)
                    take_maxima("opening", 0, key, 0)

            def body(kind, b, par):
                for g, s, p1, p2, more, tail in sh.slots(kind):
                    u = b * NG + g
                    g1 = (g + 1) % 4
                    if p1 and p1[0] != "V":
                        pair(kind, b, (g, s) + p1, p1, u + 2)
                    if (g, s) == (1, 0) and kind != "last":
                        normalise(b + 1)
                    if ipa and (g, s) == (3, 0):
                        small_softmax(b)
                    if more:
                        row_max(g1, u + 1, 2 * s)
                    if p2 and p2[0] != "V":
                        pair(kind, b, (g, s) + p2, p2, u + 2)
                    if more:
                        row_max(g1, u + 1, 2 * s + 1)
                    if more and s == 1:
                        split_max(u + 1)
                    if ("MT",) in tail:
                        take_maxima(kind, b, (g, s, "MT"), g1)
                    if not (kind == "first" and g == 0):
                        if wide and s in (2, 3):
                            divide((g - 1) % 4, u - 1, s - 2)
                        if not wide and s == 2:
                            divide((g - 1) % 4, u - 1, 0)
                    for t in tail:
                        if t[0] == "OP":
                            add_residual(kind, b, (g, s) + t, b - 1)
                        if t[0] == "SI":
                            small_softmax_scores(kind, b, (g, s) + t)
                    if clip:
                        dve.wait_ge(exp_ready, u * 2 * HG + (2 * s + 2))
                        if s == 0:
                            p, at = floor_place(kind, g)
                            dve.wait_ge(bank_free[p], at)
                        cap(dve, g, s).then_inc(capped, 1)
                    if (g, s) == (0, HG - 1) and kind != "last":
                        stats_of(dve, b + 1)
            batches(body, dve)
            for part in range(sh.parts):
                divide(3, B * NG - 1, part)
            add_residual("last", B - 1, None, B - 1)


def layernorm_all(nc, name, x_res, xn, xnT, const, loads):
    ident, _, _, _, _, eps = const
    with ExitStack() as ctx:
        sb, ps, sem = alloc(nc, ctx, name + "n")
        stats, mv = sb("stats", [P, NT, 6]), sb("mv", [P, NT, 2])
        lnv, rstd = sb("lnv", [P, NT]), sb("rstd", [P, NT])
        turned = [ps(f"turned{i}", [P, 4, P]) for i in range(2)]
        loaded = sem("loaded")
        stats_ready = sem("stats_ready")
        rstd_ready = sem("rstd_ready")
        xn_ready = sem("xn_ready")
        turned_ready = sem("turned_ready")
        xnT_ready = sem("xnT_ready")
        with nc.Block() as block:
            @block.sync
            def _(sp):
                for dst, src in loads:
                    sp.dma_start(dst, src).then_inc(loaded, 16)
                if loads:
                    sp.wait_ge(loaded, 16 * len(loads))

            @block.vector
            def _(dve):
                for t in range(NT):
                    ins = dve.bn_stats(stats[:, t, :], x_res[:, t, :])
                ins.then_inc(stats_ready, 1)
                dve.wait_ge(stats_ready, 1)
                for t in range(NT):
                    ins = dve.bn_aggr(mv[:, t, :], stats[:, t, :])
                ins.then_inc(stats_ready, 1)
                dve.wait_ge(rstd_ready, 2)
                for t in range(NT):
                    ins = dve.tensor_scalar(xn[:, t, :], x_res[:, t, :], mv[:, t, 0:1], rstd[:, t:t + 1],
                                            ALU.subtract, ALU.mult)
                    if t % 4 == 3:
                        ins.then_inc(xn_ready, 1)

            @block.scalar
            def _(act):
                act.wait_ge(stats_ready, 2)
                act.activation(lnv[:, :], mv[:, :, 1], ACT.Ln, bias=eps[:, 0:1]).then_inc(rstd_ready, 1)
                act.wait_ge(rstd_ready, 1)
                act.activation(rstd[:, :], lnv[:, :], ACT.Exp, scale=-0.5).then_inc(rstd_ready, 1)
                for k in range(NT // 4):
                    act.wait_ge(turned_ready, k + 1)
                    act.copy(xnT[:, k * 512:(k + 1) * 512], turned[k % 2][:, :, :].rearrange("p t n -> p (t n)"))\
                       .then_inc(xnT_ready, 1)

            @block.tensor
            def _(pe):
                for k in range(NT // 4):
                    pe.wait_ge(xn_ready, k + 1)
                    if k >= 2:
                        pe.wait_ge(xnT_ready, k - 1)
                    for t in range(4):
                        ins = pe.transpose(turned[k % 2][:, t, :], xn[:, 4 * k + t, :], ident[:, :])
                    ins.then_inc(turned_ready, 1)


TB = 512
TT = TB // P


def mlp(nc, name, x_res, xnT, ones, func, jobs):
    gated = jobs[0]["up"][0][1] is not None
    items = sum(len(j["up"]) for j in jobs)
    experts = sum(len(j["down"]) for j in jobs)
    dbufs = min(2, experts)
    with ExitStack() as ctx:
        sb, ps, sem = alloc(nc, ctx, name + "m")
        chunks = max(len(j["up"]) for j in jobs)
        hid = [[sb(f"hid{i}_{c}", [P, TB]) for c in range(chunks)] for i in range(2)]
        sg = [sb(f"sg{i}", [P, TB]) for i in range(2)] if gated else None
        up_ps = [ps(f"up{i}", [P, TB]) for i in range(2)]
        gate_ps = [ps(f"gate{i}", [P, TB]) for i in range(2)] if gated else None
        down_ps = [ps(f"down{i}", [P, TT, D]) for i in range(2)]
        up_ready = sem("up_ready")
        sg_ready = sem("sg_ready")
        hid_ready = sem("hid_ready")
        down_ready = sem("down_ready")
        down_free = sem("down_free")

        with nc.Block() as block:
            @block.tensor
            def _(pe):
                def up(tb, n, k, item):
                    w, wg, _, width = item
                    pe.wait_ge(hid_ready, n + 1)
                    x = xnT[:, bass.ds(tb * TB, TB)]
                    ins = pe.matmul(up_ps[k % 2][0:width, :], w, x, start=True, stop=True)
                    if gated:
                        ins = pe.matmul(gate_ps[k % 2][0:width, :], wg, x, start=True, stop=True)
                    ins.then_inc(up_ready, 1)

                def down(job_i, job, d, m, t, hid_count):
                    ws, bias, _ = job["down"][d]
                    if t == 0:
                        pe.wait_ge(down_free, m + 1)
                        pe.wait_ge(hid_ready, hid_count + 2)
                    dst = down_ps[m_static[0] % 2][:, t, :]
                    for c, (w, item) in enumerate(zip(ws, job["up"])):
                        ins = pe.matmul(dst, hid[job_i % 2][c][0:item[3], t * P:(t + 1) * P], w,
                                        start=(c == 0), stop=(c == len(ws) - 1 and not bias))
                    for i, row in enumerate(bias):
                        ins = pe.matmul(dst, ones[0:1, 0:P], row, start=False, stop=(i == len(bias) - 1))
                    if t == TT - 1:
                        ins.then_inc(down_ready, 1)
                        m_static[0] += 1

                m_static = [0]
                with pe.Fori(0, NT // TT) as tb:
                    k = m = 0
                    todo = []
                    for j, job in enumerate(jobs):
                        per = -(-len(todo) // len(job["up"]))
                        for item in job["up"]:
                            up(tb, tb * items + k, k, item)
                            k += 1
                            for a in todo[:per]:
                                down(*a)
                            todo = todo[per:]
                        for d in range(len(job["down"])):
                            todo += [(j, job, d, tb * experts + m, t, tb * items + k) for t in range(TT)]
                            m += 1
                    for a in todo:
                        down(*a)

            @block.scalar
            def _(act):
                if not gated:
                    act.sem_inc(hid_ready, 2)
                with act.Fori(0, NT // TT) as tb:
                    k = 0
                    for j, job in enumerate(jobs):
                        for c, (_, _, bias, width) in enumerate(job["up"]):
                            act.wait_ge(up_ready, tb * items + k + 1)
                            if gated:
                                act.activation(sg[k % 2][0:width, :], gate_ps[k % 2][0:width, :], func).then_inc(sg_ready, 1)
                            else:
                                act.activation(hid[j % 2][c][0:width, :], up_ps[k % 2][0:width, :], func, bias=bias)\
                                   .then_inc(hid_ready, 1)
                            k += 1

            @block.vector
            def _(dve):
                dve.sem_inc(down_free, dbufs)
                if gated:
                    dve.sem_inc(hid_ready, 2)

                def combine(tb, d, m, weight):
                    dve.wait_ge(down_ready, m + 1)
                    dve.wait_ge(down_free, m + dbufs)
                    src = down_ps[d % 2]
                    if weight.shape[1] == 1:
                        x = x_res[:, bass.ds(tb * TT, TT), :]
                        ins = dve.scalar_tensor_tensor(x, src[:, :, :], weight, x, ALU.mult, ALU.add)
                    else:
                        for t in range(TT):
                            x = x_res[:, bass.ds(tb * TT + t, 1), :].rearrange("p a n -> p (a n)")
                            ins = dve.scalar_tensor_tensor(x, src[:, t, :], weight[:, bass.ds(tb * TT + t, 1)], x,
                                                           ALU.mult, ALU.add)
                    ins.then_inc(down_free, 1)

                with dve.Fori(0, NT // TT) as tb:
                    k = m = 0
                    due = []
                    for j, job in enumerate(jobs):
                        for c, (_, _, _, width) in enumerate(job["up"]):
                            if gated:
                                dve.wait_ge(sg_ready, tb * items + k + 1)
                                dve.tensor_tensor(hid[j % 2][c][0:width, :], up_ps[k % 2][0:width, :],
                                                  sg[k % 2][0:width, :], ALU.mult).then_inc(hid_ready, 1)
                            k += 1
                        for a in due:
                            combine(*a)
                        due = []
                        for _, _, weight in job["down"]:
                            due.append((tb, m, tb * experts + m, weight))
                            m += 1
                    for a in due:
                        combine(*a)


def butterfly_step(eng, y, t0, t1, w, stage, transposed, chain, count):
    n = 2 ** stage
    v = y.rearrange("p (b a s) -> p b a s", a=2, s=n)
    a, b = v[:, :, 0, :], v[:, :, 1, :]
    wv = w.rearrange("p (b s o i) -> p b s o i", s=n, o=2, i=2)
    w01, w10 = wv[:, :, :, 0, 1], wv[:, :, :, 1, 0]
    if transposed:
        w01, w10 = w10, w01
    t0, t1, t2, t3 = (t.rearrange("p (b s) -> p b s", s=n) for t in (t0[:, 0:256], t0[:, 256:512], t1[:, 0:256], t1[:, 256:512]))
    eng.tensor_tensor(t0, a, wv[:, :, :, 0, 0], ALU.mult)
    eng.tensor_tensor(t1, b, w01, ALU.mult)
    eng.tensor_tensor(t2, a, w10, ALU.mult)
    eng.tensor_tensor(t3, b, wv[:, :, :, 1, 1], ALU.mult).then_inc(chain, 1)
    eng.wait_ge(chain, count + 1)
    eng.tensor_tensor(a, t0, t1, ALU.add)
    eng.tensor_tensor(b, t2, t3, ALU.add).then_inc(chain, 1)
    eng.wait_ge(chain, count + 2)


def butterfly_ffn(nc, name, x_res, gates, const, w):
    ident, _, _, _, ones, _ = const
    hidden, stages = 512, 9
    with ExitStack() as ctx:
        sb, ps, sem = alloc(nc, ctx, name)
        xn, xnT = sb("xn", [P, NT, D]), sb("xnT", [P, NT * P])
        w_exp, w_conT, b_exp = sb("w_exp", [P, hidden]), sb("w_conT", [P, hidden]), sb("b_exp", [1, hidden])
        up_bias = sb("up_bias", [1, hidden])
        w_con = sb("w_con", [P, 4, D])
        bias = sb("bias", [P, 4])
        rows = sb("rows", [1, 2, D])
        wup = [sb(f"wup{i}", [P, 1024]) for i in range(2)]
        wdn = [sb(f"wdn{i}", [P, 1024]) for i in range(2)]
        t0, t1, t2, t3 = (sb(f"t{i}", [P, hidden]) for i in range(4))
        t4, t5 = (sb(f"t{i}", [1, hidden]) for i in (4, 5))
        layernorm_all(nc, name, x_res, xn, xnT, const, [
            (w_exp[:, :], w["W_exp"]), (w_conT[:, :], w["W_conT"]), (b_exp[:, :], w["b_exp"].unsqueeze(0)),
            (up_bias[:, :], w["up_bias"].unsqueeze(0)), (rows[:, 0, :], w["b_con"].unsqueeze(0)),
            (rows[:, 1, :], w["down_bias"].unsqueeze(0))])
        with ExitStack() as c2:
            _, ps, sem = alloc(nc, c2, name + "b")
            turned, column = ps("turned", [P, 4, D]), ps("column", [P, 4])
            up_loaded = [sem(f"up_loaded{i}") for i in range(2)]
            down_loaded = [sem(f"down_loaded{i}") for i in range(2)]
            up_step = sem("up_step")
            down_step = sem("down_step")
            turned_ready = sem("turned_ready")
            done = sem("done")
            with nc.Block() as block:
                @block.sync
                def _(sp):
                    for n in range(stages):
                        if n >= 2:
                            sp.wait_ge(up_step, 4 * (n - 1))
                            sp.wait_ge(down_step, 2 * (n - 1))
                        sp.dma_start(wup[n % 2][:, :], w["up_weights"][n].rearrange("k o i -> (k o i)").partition_broadcast(P))\
                          .then_inc(up_loaded[n % 2], 16)
                        sp.dma_start(wdn[n % 2][:, :],
                                     w["down_weights"][stages - 1 - n].rearrange("k o i -> (k o i)").partition_broadcast(P))\
                          .then_inc(down_loaded[n % 2], 16)

                @block.vector
                def _(dve):
                    for n in range(stages):
                        dve.wait_ge(up_loaded[n % 2], 16 * (n // 2 + 1))
                        butterfly_step(dve, w_exp[:, :], t0, t1, wup[n % 2][:, :], n, False, up_step, 4 * n)
                        butterfly_step(dve, b_exp[:, :], t4, t5, wup[n % 2][0:1, :], n, False, up_step, 4 * n + 2)
                    dve.wait_ge(turned_ready, 1)
                    dve.tensor_copy(w_con[:, :, :], turned[:, :, :])
                    dve.tensor_copy(bias[:, :], column[:, :])

                @block.gpsimd
                def _(pool):
                    for n in range(stages):
                        pool.wait_ge(down_loaded[n % 2], 16 * (n // 2 + 1))
                        butterfly_step(pool, w_conT[:, :], t2, t3, wdn[n % 2][:, :], stages - 1 - n, True, down_step, 2 * n)

                @block.tensor
                def _(pe):
                    pe.wait_ge(up_step, 4 * stages)
                    for c in range(4):
                        pe.matmul(column[:, c:c + 1], b_exp[0:1, c * P:(c + 1) * P], ones[0:1, 0:1], start=True, stop=False)
                        pe.matmul(column[:, c:c + 1], up_bias[0:1, c * P:(c + 1) * P], ones[0:1, 0:1], start=False, stop=True)
                    pe.wait_ge(down_step, 2 * stages)
                    for c in range(4):
                        ins = pe.transpose(turned[:, c, :], w_conT[:, c * P:(c + 1) * P], ident[:, :])
                    ins.then_inc(turned_ready, 1)
        mlp(nc, name, x_res, xnT, ones, ACT.Gelu, [{
            "up": [(w_exp[:, c * P:(c + 1) * P], None, bias[:, c:c + 1], P) for c in range(4)],
            "down": [([w_con[:, c, :] for c in range(4)], [rows[0:1, 0, :], rows[0:1, 1, :]], gates[:, 4:5])]}])


def expert_ffn(nc, name, x_res, gates, const, io, w):
    ones = const[4]
    hidden, routed = 512, 7
    with ExitStack() as ctx:
        sb, ps, sem = alloc(nc, ctx, name)
        xn, xnT = sb("xn", [P, NT, D]), sb("xnT", [P, NT * P])
        wu, wg = sb("wu", [P, routed + 1, hidden]), sb("wg", [P, routed + 1, hidden])
        wd = sb("wd", [P, routed + 1, 4, D])
        wr, iota = sb("wr", [P, 8]), sb("iota", [P, 8])
        weight = sb("weight", [P, 8, NT])
        layernorm_all(nc, name, x_res, xn, xnT, const, [
            (wr[:, :], w["w_router"]), (iota[:, :], io["c_iota8"]),
            (wu[:, 0:routed, :], w["w_up"].rearrange("e p n -> p e n")), (wu[:, routed, :], w["ws_up"]),
            (wg[:, 0:routed, :], w["w_gate"].rearrange("e p n -> p e n")), (wg[:, routed, :], w["ws_gate"]),
            (wd[:, routed, :, :], w["ws_down"].rearrange("(c p) n -> p c n", p=P))]
            + [(wd[:, e, :, :], w["w_down"][e].rearrange("(c p) n -> p c n", p=P)) for e in range(routed)])
        with ExitStack() as c2:
            sb2, ps, sem = alloc(nc, c2, name + "r")
            logits = ps("logits", [P, NT, 8])
            top, p_top, first = sb2("top", [P, NT]), sb2("p_top", [P, NT]), sb2("first", [P, NT])
            z, e, eq, at = (sb2(n, [P, NT, 8]) for n in ("z", "e", "eq", "at"))
            logits_ready, e_ready, step = sem("logits_ready"), sem("e_ready"), sem("step")
            with nc.Block() as block:
                @block.tensor
                def _(pe):
                    for t in range(NT):
                        ins = pe.matmul(logits[:, t, :], xnT[:, t * P:(t + 1) * P], wr[:, :], start=True, stop=True)
                    ins.then_inc(logits_ready, 1)

                @block.scalar
                def _(act):
                    act.wait_ge(step, 2)
                    act.activation(e[:, :, :], z[:, :, :], ACT.Exp).then_inc(e_ready, 1)

                @block.vector
                def _(dve):
                    def over(a):
                        return a[:, :].unsqueeze(2).broadcast_to([P, NT, 8])
                    dve.wait_ge(logits_ready, 1)
                    dve.tensor_reduce(top[:, :], logits[:, :, :], AXX, ALU.max).then_inc(step, 1)
                    dve.wait_ge(step, 1)
                    dve.tensor_tensor(z[:, :, :], logits[:, :, :], over(top), ALU.subtract).then_inc(step, 1)
                    dve.wait_ge(e_ready, 1)
                    dve.reduce_sum(p_top[:, :], e[:, :, :], AXX).then_inc(step, 1)
                    dve.tensor_tensor(eq[:, :, :], logits[:, :, :], over(top), ALU.is_equal).then_inc(step, 1)
                    dve.wait_ge(step, 4)
                    dve.scalar_tensor_tensor(at[:, :, :], eq[:, :, :], -100.0,
                                             iota[:, :].unsqueeze(1).broadcast_to([P, NT, 8]), ALU.mult, ALU.add).then_inc(step, 1)
                    dve.wait_ge(step, 5)
                    dve.tensor_reduce(first[:, :], at[:, :, :], AXX, ALU.min).then_inc(step, 1)
                    dve.reciprocal(top[:, :], p_top[:, :]).then_inc(step, 1)
                    dve.wait_ge(step, 7)
                    dve.tensor_tensor(eq[:, :, :], at[:, :, :], over(first), ALU.is_equal).then_inc(step, 1)
                    dve.tensor_scalar(p_top[:, :], top[:, :], gates[:, 5:6], 2.0, ALU.mult, ALU.mult).then_inc(step, 1)
                    dve.wait_ge(step, 9)
                    dve.tensor_tensor(weight[:, :, :].rearrange("p e t -> p t e"), eq[:, :, :], over(p_top), ALU.mult)
        jobs = []
        for e in range(routed + 1):
            up = [(wu[:, e, c * P:(c + 1) * P], wg[:, e, c * P:(c + 1) * P], None, P) for c in range(4)]
            col = weight[:, e, :] if e < routed else gates[:, 5:6]
            jobs.append({"up": up, "down": [([wd[:, e, c, :] for c in range(4)], [], col)]})
        mlp(nc, name, x_res, xnT, ones, ACT.Silu, jobs)


def column_ffn(nc, name, x_res, gates, const, io, w):
    ident, _, _, _, ones, eps = const
    cols, neurons, gate_dim = 16, 32, 64
    hidden = cols * neurons
    with ExitStack() as ctx:
        sb, ps, sem = alloc(nc, ctx, name)
        xn, xnT = sb("xn", [P, NT, D]), sb("xnT", [P, NT * P])
        col_emb, ceT = sb("col_emb", [cols, D]), sb("ceT", [P, cols])
        w1, b1, w2, b2 = sb("w1", [P, gate_dim]), sb("b1", [gate_dim, 1]), sb("w2", [gate_dim, cols]), sb("b2", [1, cols])
        w_cols, b_cols = sb("w_cols", [P, cols, neurons]), sb("b_cols", [1, hidden])
        proj_w, proj_b = sb("proj_w", [P, 4, D]), sb("proj_b", [1, D])
        ln_g, ln_b = sb("ln_g", [P, D]), sb("ln_b", [P, D])
        iota = sb("iota", [P, cols])
        weight = sb("weight", [P, NT, cols])
        layernorm_all(nc, name, x_res, xn, xnT, const, [
            (col_emb[:, :], w["col_emb"]), (w1[:, :], w["gate_w1"]), (b1[:, :], w["gate_b1"].unsqueeze(1)),
            (w2[:, :], w["gate_w2"]), (b2[:, :], w["gate_b2"].unsqueeze(0)),
            (w_cols[:, :, :], w["W_cols"].rearrange("c p n -> p c n")),
            (b_cols[:, :], w["b_cols"].rearrange("(a c) n -> a (c n)", a=1)),
            (proj_w[:, :, :], w["proj_w"].rearrange("(c p) n -> p c n", p=P)), (proj_b[:, :], w["proj_b"].unsqueeze(0)),
            (ln_g[:, :], w["ln_g"].partition_broadcast(P)), (ln_b[:, :], w["ln_b"].partition_broadcast(P)),
            (iota[:, :], io["c_iota16"])])

        with ExitStack() as c2:
            sb2, ps, sem = alloc(nc, c2, name + "r")
            hg = sb2("hg", [gate_dim, NT * P])
            sq, norm, n2 = sb2("sq", [P, NT, D]), sb2("norm", [P, NT]), sb2("n2", [P, NT])
            ce2, ce_n, ce_s = sb2("ce2", [cols, D]), sb2("ce_n", [cols, 1]), sb2("ce_s", [cols, D])
            sig, lg, z, e, eq, at = (sb2(n, [P, NT, cols]) for n in ("sig", "lg", "z", "e", "eq", "at"))
            top, total, first, p_top = (sb2(n, [P, NT]) for n in ("top", "total", "first", "p_top"))
            hg_ps = [ps(f"hg_ps{i}", [gate_dim, 512]) for i in range(2)]
            gate_ps, sim_ps, ce_ps = ps("gate_ps", [P, NT, cols]), ps("sim_ps", [P, NT, cols]), ps("ce_ps", [P, cols])
            step, reci = sem("step"), sem("reci")
            act_step = sem("act_step")
            hg_ready, hg_done = sem("hg_ready"), sem("hg_done")
            gate_ready, ce_ready, sim_ready = sem("gate_ready"), sem("ce_ready"), sem("sim_ready")
            with nc.Block() as block:
                @block.tensor
                def _(pe):
                    for k in range(4):
                        if k >= 2:
                            pe.wait_ge(hg_done, k - 1)
                        pe.matmul(hg_ps[k % 2][:, :], w1[:, :], xnT[:, k * 512:(k + 1) * 512], start=True, stop=True)\
                          .then_inc(hg_ready, 1)
                    for t in range(NT):
                        if t % 4 == 0:
                            pe.wait_ge(hg_done, t // 4 + 1)
                        pe.matmul(gate_ps[:, t, :], hg[:, t * P:(t + 1) * P], w2[:, :], start=True, stop=False)
                        ins = pe.matmul(gate_ps[:, t, :], ones[0:1, 0:P], b2[:, :], start=False, stop=True)
                    ins.then_inc(gate_ready, 1)
                    pe.wait_ge(step, 6)
                    pe.transpose(ce_ps[:, :], ce_s[:, :], ident[0:cols, 0:cols]).then_inc(ce_ready, 1)
                    pe.wait_ge(step, 7)
                    for t in range(NT):
                        ins = pe.matmul(sim_ps[:, t, :], xnT[:, t * P:(t + 1) * P], ceT[:, :], start=True, stop=True)
                    ins.then_inc(sim_ready, 1)

                @block.scalar
                def _(act):
                    act.wait_ge(step, 4)
                    act.activation(norm[:, :], n2[:, :], ACT.Sqrt)
                    act.activation(ce_n[:, :], ce_n[:, :], ACT.Sqrt).then_inc(act_step, 1)
                    for k in range(4):
                        act.wait_ge(hg_ready, k + 1)
                        act.activation(hg[:, k * 512:(k + 1) * 512], hg_ps[k % 2][:, :], ACT.Gelu, bias=b1[:, 0:1])\
                           .then_inc(hg_done, 1)
                    act.wait_ge(gate_ready, 1)
                    act.activation(sig[:, :, :], gate_ps[:, :, :], ACT.Sigmoid).then_inc(act_step, 1)
                    act.wait_ge(step, 11)
                    act.activation(e[:, :, :], z[:, :, :], ACT.Exp).then_inc(act_step, 1)

                @block.vector
                def _(dve):
                    def over(a):
                        return a[:, :].unsqueeze(2).broadcast_to([P, NT, cols])
                    dve.tensor_tensor(sq[:, :, :], xn[:, :, :], xn[:, :, :], ALU.mult).then_inc(step, 1)
                    dve.tensor_tensor(ce2[:, :], col_emb[:, :], col_emb[:, :], ALU.mult).then_inc(step, 1)
                    dve.wait_ge(step, 2)
                    dve.reduce_sum(n2[:, :], sq[:, :, :], AXX).then_inc(step, 1)
                    dve.reduce_sum(ce_n[:, :], ce2[:, :], AXX).then_inc(step, 1)
                    dve.wait_ge(act_step, 1)
                    dve.tensor_scalar(ce_n[:, :], ce_n[:, :], 1e-12, None, ALU.max)
                    dve.tensor_scalar(norm[:, :], norm[:, :], 1e-12, None, ALU.max).then_inc(step, 1)
                    dve.wait_ge(step, 5)
                    dve.reciprocal(ce2[:, 0:1], ce_n[:, :])
                    dve.reciprocal(n2[:, :], norm[:, :]).then_inc(reci, 1)
                    dve.wait_ge(reci, 1)
                    dve.tensor_scalar(ce_s[:, :], col_emb[:, :], ce2[:, 0:1], None, ALU.mult).then_inc(step, 1)
                    dve.wait_ge(ce_ready, 1)
                    dve.tensor_copy(ceT[:, :], ce_ps[:, :]).then_inc(step, 1)
                    dve.wait_ge(sim_ready, 1)
                    dve.tensor_tensor(lg[:, :, :], sim_ps[:, :, :], over(n2), ALU.mult).then_inc(step, 1)
                    dve.wait_ge(act_step, 2)
                    dve.wait_ge(step, 8)
                    dve.tensor_tensor(z[:, :, :], lg[:, :, :], sig[:, :, :], ALU.add).then_inc(step, 1)
                    dve.wait_ge(step, 9)
                    dve.tensor_reduce(top[:, :], z[:, :, :], AXX, ALU.max).then_inc(step, 1)
                    dve.wait_ge(step, 10)
                    dve.tensor_tensor(eq[:, :, :], z[:, :, :], over(top), ALU.is_equal)
                    dve.tensor_tensor(z[:, :, :], z[:, :, :], over(top), ALU.subtract).then_inc(step, 1)
                    dve.wait_ge(step, 11)
                    dve.scalar_tensor_tensor(at[:, :, :], eq[:, :, :], -100.0,
                                             iota[:, :].unsqueeze(1).broadcast_to([P, NT, cols]), ALU.mult, ALU.add)\
                       .then_inc(step, 1)
                    dve.wait_ge(step, 12)
                    dve.tensor_reduce(first[:, :], at[:, :, :], AXX, ALU.min).then_inc(step, 1)
                    dve.wait_ge(act_step, 3)
                    dve.reduce_sum(total[:, :], e[:, :, :], AXX).then_inc(step, 1)
                    dve.wait_ge(step, 14)
                    dve.reciprocal(p_top[:, :], total[:, :])
                    dve.tensor_tensor(eq[:, :, :], at[:, :, :], over(first), ALU.is_equal).then_inc(step, 1)
                    dve.wait_ge(step, 15)
                    dve.tensor_tensor(weight[:, :, :], eq[:, :, :], over(p_top), ALU.mult)

        with ExitStack() as c2:
            sb2, ps, sem = alloc(nc, c2, name + "c")
            hc = [sb2(f"hc{i}", [P, cols, neurons]) for i in range(2)]
            hw = [sb2(f"hw{i}", [P, hidden]) for i in range(2)]
            hT = [sb2(f"hT{i}", [P, 4, P]) for i in range(2)]
            y, yn = sb2("y", [P, NT, D]), sb2("yn", [P, NT, D])
            stats, mv = sb2("stats", [P, NT, 6]), sb2("mv", [P, NT, 2])
            lnv, rstd = sb2("lnv", [P, NT]), sb2("rstd", [P, NT])
            up_ps = [ps(f"up{i}", [P, hidden]) for i in range(2)]
            t_ps = [ps(f"t{i}", [P, 4, P]) for i in range(2)]
            y_ps = [ps(f"y{i}", [P, D]) for i in range(2)]
            up_ready = sem("up_ready")
            hc_ready = sem("hc_ready")
            hw_ready = sem("hw_ready")
            t_ready = sem("t_ready")
            hT_ready = sem("hT_ready")
            y_ready = sem("y_ready")
            y_done = sem("y_done")
            step, rstd_ready = sem("step"), sem("rstd_ready")
            with nc.Block() as block:
                @block.tensor
                def _(pe):
                    def up(t, i):
                        if i >= 2:
                            pe.wait_ge(hc_ready, t - 1)
                        pe.matmul(up_ps[i % 2][:, :], xnT_tile(t), w_cols[:, :, :].rearrange("p c n -> p (c n)"),
                                  start=True, stop=False)
                        pe.matmul(up_ps[i % 2][:, :], ones[0:1, 0:P], b_cols[:, :], start=False, stop=True)\
                          .then_inc(up_ready, 1)

                    def xnT_tile(t):
                        return xnT[:, t * P:(t + 1) * P]

                    for t in range(NT + 1):
                        if t < NT:
                            up(t, t)
                        if t >= 1:
                            n = t - 1
                            pe.wait_ge(hw_ready, n + 1)
                            if n >= 2:
                                pe.wait_ge(hT_ready, n - 1)
                            for c in range(4):
                                ins = pe.transpose(t_ps[n % 2][:, c, :], hw[n % 2][:, c * P:(c + 1) * P], ident[:, :])
                            ins.then_inc(t_ready, 1)
                            if n >= 2:
                                pe.wait_ge(y_done, n - 1)
                            pe.wait_ge(hT_ready, n + 1)
                            for c in range(4):
                                pe.matmul(y_ps[n % 2][:, :], hT[n % 2][:, c, :], proj_w[:, c, :], start=(c == 0), stop=False)
                            pe.matmul(y_ps[n % 2][:, :], ones[0:1, 0:P], proj_b[:, :], start=False, stop=True)\
                              .then_inc(y_ready, 1)

                @block.scalar
                def _(act):
                    def hidden_values(t):
                        act.wait_ge(up_ready, t + 1)
                        act.activation(hc[t % 2][:, :, :], up_ps[t % 2][:, :].rearrange("p (c n) -> p c n", c=cols), ACT.Gelu)\
                           .then_inc(hc_ready, 1)
                    hidden_values(0)
                    for t in range(NT):
                        if t + 1 < NT:
                            if t >= 1:
                                act.wait_ge(hw_ready, t)
                            hidden_values(t + 1)
                        act.wait_ge(t_ready, t + 1)
                        act.copy(hT[t % 2][:, :, :], t_ps[t % 2][:, :, :]).then_inc(hT_ready, 1)
                    act.wait_ge(step, 2)
                    act.activation(lnv[:, :], mv[:, :, 1], ACT.Ln, bias=eps[:, 0:1]).then_inc(rstd_ready, 1)
                    act.wait_ge(rstd_ready, 1)
                    act.activation(rstd[:, :], lnv[:, :], ACT.Exp, scale=-0.5).then_inc(rstd_ready, 1)

                @block.vector
                def _(dve):
                    for t in range(NT + 1):
                        if t < NT:
                            dve.wait_ge(hc_ready, t + 1)
                            if t >= 2:
                                dve.wait_ge(t_ready, t - 1)
                            dve.tensor_tensor(hw[t % 2][:, :].rearrange("p (c n) -> p c n", c=cols), hc[t % 2][:, :, :],
                                              weight[:, t, :].unsqueeze(2).broadcast_to([P, cols, neurons]), ALU.mult)\
                               .then_inc(hw_ready, 1)
                        if t >= 1:
                            n = t - 1
                            dve.wait_ge(y_ready, n + 1)
                            dve.tensor_tensor(y[:, n, :], y_ps[n % 2][:, :], xn[:, n, :], ALU.add).then_inc(y_done, 1)
                    dve.wait_ge(y_done, NT)
                    for t in range(NT):
                        ins = dve.bn_stats(stats[:, t, :], y[:, t, :])
                    ins.then_inc(step, 1)
                    dve.wait_ge(step, 1)
                    for t in range(NT):
                        ins = dve.bn_aggr(mv[:, t, :], stats[:, t, :])
                    ins.then_inc(step, 1)
                    dve.wait_ge(rstd_ready, 2)
                    for t in range(NT):
                        ins = dve.tensor_scalar(yn[:, t, :], y[:, t, :], mv[:, t, 0:1], rstd[:, t:t + 1],
                                                ALU.subtract, ALU.mult)
                    ins.then_inc(step, 1)
                    dve.wait_ge(step, 3)
                    every = [P, NT, D]
                    dve.tensor_tensor(y[:, :, :], yn[:, :, :], ln_g[:, :].unsqueeze(1).broadcast_to(every), ALU.mult)\
                       .then_inc(step, 1)
                    dve.wait_ge(step, 4)
                    dve.tensor_tensor(yn[:, :, :], y[:, :, :], ln_b[:, :].unsqueeze(1).broadcast_to(every), ALU.add)\
                       .then_inc(step, 1)
                    dve.wait_ge(step, 5)
                    dve.scalar_tensor_tensor(x_res[:, :, :], yn[:, :, :], gates[:, 6:7], x_res[:, :, :], ALU.mult, ALU.add)


def choice_ffn(nc, name, x_res, gates, const, io, w):
    ident, _, _, _, ones, _ = const
    experts, groups, width = 8, 4, 341
    chosen = NT * P // experts
    bits = 30
    spans = [(0, P), (P, P), (2 * P, width - 2 * P)]
    with ExitStack() as ctx:
        sb, ps, sem = alloc(nc, ctx, name)
        xn, xnT = sb("xn", [P, NT, D]), sb("xnT", [P, NT * P])
        wr, br = sb("wr", [P, experts]), sb("br", [1, experts])
        wu, bu = sb("wu", [P, groups, width]), sb("bu", [P, 3, groups])
        wd, bd = sb("wd", [P, experts, 3, D]), sb("bd", [1, experts, D])
        same, before, masks = sb("same", [P, P]), sb("before", [P, P]), sb("masks", [P, bits], U32)
        weight = sb("weight", [P, experts, NT])
        loads = [(wr[:, :], w["Wr"]), (br[:, :], w["br"].unsqueeze(0)), (wu[:, :, :], w["W_up"].rearrange("g p f -> p g f")),
                 (bd[:, :, :], w["b_down"].unsqueeze(0)), (same[:, :], io["c_same"]), (before[:, :], io["c_before"]),
                 (masks[:, :], io["c_masks"])]
        for c, (at, n) in enumerate(spans):
            loads.append((bu[0:n, c, :], w["b_upT"][at:at + n, :]))
            loads.append((wd[0:n, :, c, :], w["W_down"][:, at:at + n, :].rearrange("e f n -> f e n")))
        layernorm_all(nc, name, x_res, xn, xnT, const, loads)
        with ExitStack() as c2:
            sb2, ps, sem = alloc(nc, c2, name + "r")
            logits, turned = ps("logits", [P, NT, experts]), ps("turned", [P, P])
            count_ps, back_ps = ps("count", [P, 4]), ps("back", [P, P])
            top, total, z, e, probs = (sb2(n, s) for n, s in (
                ("top", [P, NT]), ("total", [P, NT]), ("z", [P, NT, experts]), ("e", [P, NT, experts]),
                ("probs", [P, NT, experts])))
            p, over_it, gt, eq, rank, chosen_p = (sb2(n, [P, P]) for n in ("p", "over_it", "gt", "eq", "rank", "chosen_p"))
            least, trial, cnt, kept = sb2("least", [P, 1], U32), sb2("trial", [P, 1], U32), sb2("cnt", [P, 1]), sb2("kept", [P, 1])
            n_gt, n_eq, room = sb2("n_gt", [P, 1]), sb2("n_eq", [P, 1]), sb2("room", [P, 1])
            least_f, trial_f = least[:, :].bitcast(F32), trial[:, :].bitcast(F32)
            step, e_ready, late = sem("step"), sem("e_ready"), sem("late")
            pe_step = sem("pe_step")
            trial_ready, counted, summed, judged, settled = (
                sem(n) for n in ("trial_ready", "counted", "summed", "judged", "settled"))
            with nc.Block() as block:
                @block.tensor
                def _(pe):
                    for t in range(NT):
                        pe.matmul(logits[:, t, :], xnT[:, t * P:(t + 1) * P], wr[:, :], start=True, stop=False)
                        ins = pe.matmul(logits[:, t, :], ones[0:1, 0:P], br[:, :], start=False, stop=True)
                    ins.then_inc(pe_step, 1)
                    pe.wait_ge(step, 5)
                    pe.transpose(turned[:, :], probs[:, :, :].rearrange("p t e -> p (t e)"), ident[:, :]).then_inc(pe_step, 1)
                    with pe.Fori(0, bits) as i:
                        pe.wait_ge(counted, i + 1)
                        pe.matmul(count_ps[:, 0:1], same[:, :], cnt[:, :], start=True, stop=True).then_inc(summed, 1)
                    pe.wait_ge(step, 7)
                    pe.matmul(count_ps[:, 1:2], same[:, :], n_gt[:, :], start=True, stop=True)
                    pe.matmul(count_ps[:, 2:3], before[:, :], n_eq[:, :], start=True, stop=True).then_inc(pe_step, 1)
                    pe.wait_ge(step, 12)
                    pe.transpose(back_ps[:, :], chosen_p[:, :], ident[:, :]).then_inc(pe_step, 1)

                @block.scalar
                def _(act):
                    act.wait_ge(step, 2)
                    act.activation(e[:, :, :], z[:, :, :], ACT.Exp).then_inc(e_ready, 1)

                @block.vector
                def _(dve):
                    def over(a):
                        return a[:, :].unsqueeze(2).broadcast_to([P, NT, experts])
                    dve.wait_ge(pe_step, 1)
                    dve.tensor_reduce(top[:, :], logits[:, :, :], AXX, ALU.max).then_inc(step, 1)
                    dve.wait_ge(step, 1)
                    dve.tensor_tensor(z[:, :, :], logits[:, :, :], over(top), ALU.subtract).then_inc(step, 1)
                    dve.wait_ge(e_ready, 1)
                    dve.reduce_sum(total[:, :], e[:, :, :], AXX).then_inc(step, 1)
                    dve.wait_ge(step, 3)
                    dve.reciprocal(top[:, :], total[:, :]).then_inc(step, 1)
                    dve.wait_ge(step, 4)
                    dve.tensor_tensor(probs[:, :, :], e[:, :, :], over(top), ALU.mult).then_inc(step, 1)
                    dve.wait_ge(pe_step, 2)
                    dve.tensor_copy(p[:, :], turned[:, :])
                    dve.memset(least[:, :], 0).then_inc(settled, 1)
                    with dve.Fori(0, bits) as i:
                        dve.wait_ge(settled, i + 1)
                        dve.tensor_tensor(trial[:, :], least[:, :], masks[:, bass.ds(i, 1)], ALU.bitwise_or)\
                           .then_inc(trial_ready, 1)
                        dve.wait_ge(trial_ready, i + 1)
                        dve.tensor_scalar(over_it[:, :], p[:, :], trial_f, None, ALU.is_ge, ALU.add, accum_out=cnt[:, :])\
                           .then_inc(counted, 1)
                        dve.wait_ge(summed, i + 1)
                        dve.tensor_scalar(kept[:, :], count_ps[:, 0:1], chosen - 0.5, trial_f, ALU.is_gt, ALU.mult)\
                           .then_inc(judged, 1)
                        dve.wait_ge(judged, i + 1)
                        dve.tensor_tensor(least_f, least_f, kept[:, :], ALU.max).then_inc(settled, 1)
                    dve.wait_ge(settled, bits + 1)
                    dve.tensor_scalar(gt[:, :], p[:, :], least_f, None, ALU.is_gt, ALU.add, accum_out=n_gt[:, :]).then_inc(step, 1)
                    dve.tensor_scalar(eq[:, :], p[:, :], least_f, None, ALU.is_equal, ALU.add, accum_out=n_eq[:, :]).then_inc(step, 1)
                    dve.wait_ge(step, 7)
                    dve.tensor_tensor_scan(rank[:, :], ones[:, 0:P], eq[:, :], 0.0, ALU.mult, ALU.add).then_inc(step, 1)
                    dve.wait_ge(pe_step, 3)
                    dve.tensor_scalar(kept[:, :], count_ps[:, 1:2], -1.0, float(chosen), ALU.mult, ALU.add).then_inc(step, 1)
                    dve.wait_ge(step, 9)
                    dve.tensor_tensor(room[:, :], kept[:, :], count_ps[:, 2:3], ALU.subtract).then_inc(step, 1)
                    dve.wait_ge(step, 10)
                    dve.scalar_tensor_tensor(over_it[:, :], rank[:, :], room[:, 0:1], eq[:, :], ALU.is_le, ALU.mult)\
                       .then_inc(step, 1)
                    dve.wait_ge(step, 11)
                    dve.tensor_tensor(rank[:, :], over_it[:, :], gt[:, :], ALU.add).then_inc(late, 1)
                    dve.wait_ge(late, 1)
                    dve.tensor_tensor(chosen_p[:, :], rank[:, :], p[:, :], ALU.mult).then_inc(step, 1)
                    dve.wait_ge(pe_step, 4)
                    dve.tensor_scalar(weight[:, :, :].rearrange("p e t -> p t e"),
                                      back_ps[:, :].rearrange("p (t e) -> p t e", e=experts), gates[:, 7:8], None, ALU.mult)
        jobs = []
        for g in range(groups):
            up = [(wu[:, g, at:at + n], None, bu[0:n, c, g:g + 1], n) for c, (at, n) in enumerate(spans)]
            jobs.append({"up": up, "down": [([wd[0:n, e, c, :] for c, (_, n) in enumerate(spans)], [bd[0:1, e, :]],
                                             weight[:, e, :]) for e in (2 * g, 2 * g + 1)]})
        mlp(nc, name, x_res, xnT, ones, ACT.Silu, jobs)


def program(nc, io, layers):
    SEMAPHORES.clear()
    with ExitStack() as ctx:
        sb, ps, sem = alloc(nc, ctx, "top")
        x_res = sb("x_res", [P, NT, D])
        gates = sb("gates", [P, 8])
        gates_in = sb("gates_in", [P, 8])
        ident, bsel, ones = sb("ident", [P, P]), sb("bsel", [P, P]), sb("ones", [P, SK])
        identb, identh = sb("identb", [P, P], BF16), sb("identh", [P, P], F16)
        cvec, eps = sb("cvec", [P, 2]), sb("eps", [P, 1])
        mask_in, mask_f = sb("mask_in", [B, SK], U8), sb("mask_f", [B, SK])
        loaded, ready, stored = sem("loaded"), sem("ready"), sem("stored")
        mask_rows = io["scratch_mask"]

        with nc.Block() as block:
            @block.sync
            def _(sp):
                for dst, src in ((x_res[:, :, :], io["x"].rearrange("b (t p) d -> p (b t) d", p=P)),
                                 (gates_in[:, 0:4], io["g_xattn"].partition_broadcast(P)),
                                 (gates_in[:, 4:8], io["g_ffn"].partition_broadcast(P)),
                                 (ident[:, :], io["c_ident"]), (identh[:, :], io["c_identh"]),
                                 (bsel[:, :], io["c_bsel"]), (cvec[:, :], io["c_vec"]),
                                 (mask_in[:, :], io["mask_BxS2_bf1"])):
                    sp.dma_start(dst, src).then_inc(loaded, 16)
                sp.wait_ge(ready, 4)
                sp.dma_start(mask_rows, mask_f[:, :]).then_inc(stored, 16)
                sp.wait_ge(stored, 16)

            @block.scalar
            def _(act):
                act.wait_ge(loaded, 8 * 16)
                act.activation(gates[:, :], gates_in[:, :], ACT.Tanh).then_inc(ready, 1)

            @block.vector
            def _(dve):
                dve.memset(ones[:, :], 1.0)
                dve.memset(eps[:, :], EPS)
                dve.wait_ge(loaded, 8 * 16)
                dve.tensor_copy(identb[:, :], identh[:, :])
                dve.tensor_copy(mask_f[:, :], mask_in[:, :]).then_inc(ready, 1)
                dve.wait_ge(ready, 2)
                dve.tensor_scalar(mask_f[:, :], mask_f[:, :], 1.0, MASK_K, ALU.subtract, ALU.mult).then_inc(ready, 2)

        const = (ident, identb, cvec, bsel, ones, eps)

        def weights(prefix, names):
            return {n: io[f"{prefix}_{n}"] for n in names}

        shared = {"ctxT": io["ctxT"], "identh": identh, "ctx_tail": io["c_ctx_tail"],
                  "ones_row": io["c_ones"]}
        if 0 in layers:
            attention(nc, Shape("L0x", wide=False, clip=True, bias=True, gate=0),
                      shared | {"mask_q_row": io["c_mask_q"], "shift_k_row": io["c_shift_k"],
                                "keyrow": io["c_keyrow"]} | weights("L0_xattn", "Wq bq Wk bk Wv bv Wo bo".split()),
                      (x_res, gates), const)
        if 1 in layers:
            butterfly_ffn(nc, "L0f", x_res, gates, const, weights("L0_ffn", "W_exp b_exp up_weights up_bias down_weights "
                                                                  "W_conT b_con down_bias".split()))
        if 2 in layers:
            attention(nc, Shape("L1x", wide=True, ipa=True, gate=1),
                      shared | {"ctx_tail": io["c_ctx_tail_ipa"]} | weights("L1_xattn", "Wq Wk Wv Wo bo q_downT q_up q_alpha k_downT k_up k_alpha v_downT v_up "
                                       "v_alpha o_downT o_up o_alpha Wk_ipa Wv_ipa".split()), (x_res, gates), const)
        if 3 in layers:
            expert_ffn(nc, "L1f", x_res, gates, const, io,
                       weights("L1_ffn", "w_router w_up w_gate w_down ws_up ws_gate ws_down".split()))
        nc.clear_and_free_semaphores(SEMAPHORES)
        SEMAPHORES.clear()
        nc.all_engine_barrier()
        stored = sem("stored_out")
        if 4 in layers:
            attention(nc, Shape("L2x", wide=True, gate=2),
                      shared | weights("L2_xattn", "Wq Wk Wv Wo bo".split()), (x_res, gates), const)
        if 5 in layers:
            column_ffn(nc, "L2f", x_res, gates, const, io, weights("L2_ffn", "col_emb gate_w1 gate_b1 gate_w2 gate_b2 W_cols "
                                                                   "b_cols proj_w proj_b ln_g ln_b".split()))
        if 6 in layers:
            attention(nc, Shape("L3x", wide=False, mask=True, out_bias=False, gate=3),
                      shared | {"mask_row": mask_rows.unsqueeze(1), "mask_q_row": io["c_mask_q"],
                                "mask_k_row": io["c_mask_k"],
                                "shift_k_row": io["c_shift_k_mask"]} | weights("L3_xattn", "Wq Wk Wv Wo".split()),
                      (x_res, gates), const)
        if 7 in layers:
            choice_ffn(nc, "L3f", x_res, gates, const, io,
                       weights("L3_ffn", "Wr br W_up b_upT W_down b_down".split()))

        with nc.Block() as block:
            @block.sync
            def _(sp):
                sp.dma_start(io["out"].rearrange("b (t p) d -> p (b t) d", p=P), x_res[:, :, :]).then_inc(stored, 16)
                sp.wait_ge(stored, 16)


def constants():
    row = np.arange(P)
    ctx_tail = {}
    for n, hidden in (("", 0), ("_ipa", IPA)):
        ctx_tail[n] = np.zeros((P - DC, SK), np.float16)
        ctx_tail[n][0:3] = SHIFT_K
        ctx_tail[n][3, SK - hidden:] = HIDE_KEY
    slot = (row % 32) // 8
    vec = np.zeros((P, 2), np.float32)
    vec[:, 0] = slot == 1
    vec[:, 1] = slot == 2
    bsel = np.zeros((P, P), np.float32)
    bsel[(row // 32) * 32 + 8, row] = 1.0
    mask_q, mask_k = np.zeros((1, NG, P), np.float32), np.zeros((1, NG, P), np.float32)
    mask_q[:, :, 24::32] = MASK_Q
    mask_k[:, :, 24::32] = 1.0
    shift_k = np.zeros((1, NG, P), np.float32)
    for part in range(3):
        shift_k[:, :, 25 + part::32] = 1.0
    keyrow = np.zeros((P, HG, P), np.float16)
    for h in range(HG):
        keyrow[32 * h + 25:32 * h + 28, h] = SHIFT_K
    return {"c_ctx_tail": ctx_tail[""], "c_ctx_tail_ipa": ctx_tail["_ipa"], "c_keyrow": keyrow, "c_vec": vec, "c_bsel": bsel, "c_mask_q": mask_q, "c_mask_k": mask_k,
            "c_ident": np.eye(P, dtype=np.float32),
            "c_iota8": np.tile(np.arange(8, dtype=np.float32), (P, 1)),
            "c_iota16": np.tile(np.arange(16, dtype=np.float32), (P, 1)),
            "c_identh": np.eye(P, dtype=np.float16), "c_shift_k": shift_k * SHIFT_K,
            "c_shift_k_mask": shift_k * MASK_K,
            "c_same": (row[:, None] % 8 == row % 8).astype(np.float32),
            "c_before": ((row[:, None] % 8 == row % 8) & (row[:, None] < row)).astype(np.float32),
            "c_masks": np.tile(np.uint32(1) << np.arange(29, -1, -1, dtype=np.uint32), (P, 1)),
            "c_ones": np.ones((1, SK), np.float32)}


LAYERS = (0, 1, 2, 3, 4, 5, 6, 7)


def kernel(**inputs):
    import concourse.bacc as bacc
    from concourse.bass_utils import run_bass_kernel_spmd

    nc = bacc.Bacc("TRN2", target_bir_lowering=False, num_devices=1)
    arrays = {n: np.ascontiguousarray(a) for n, a in inputs.items() if n != "ctx_768"}
    arrays["mask_BxS2_bf1"] = arrays["mask_BxS2_bf1"].view(np.uint8)
    arrays["ctxT"] = np.ascontiguousarray(np.asarray(inputs["ctx_768"]).transpose(0, 2, 1))
    for n in "qkvo":
        arrays[f"L1_xattn_{n}_downT"] = np.ascontiguousarray(np.asarray(arrays.pop(f"L1_xattn_{n}_down")).T)
    arrays["L0_ffn_W_conT"] = np.ascontiguousarray(np.asarray(arrays.pop("L0_ffn_W_con")).T)
    arrays["L3_ffn_b_upT"] = np.ascontiguousarray(np.asarray(arrays.pop("L3_ffn_b_up")).T)
    arrays |= constants()
    io = {n: nc.dram_tensor(f"in_{n}", a.shape, mybir.dt.from_np(a.dtype), kind="ExternalInput").ap()
          for n, a in arrays.items()}
    io["scratch_mask"] = nc.dram_tensor("scratch_mask", (B, SK), F32).ap()
    io["out"] = nc.dram_tensor("out_x", (B, SQ, D), F32, kind="ExternalOutput").ap()
    program(nc, io, LAYERS)
    result = run_bass_kernel_spmd(nc, [{f"in_{n}": a for n, a in arrays.items()}], core_ids=[0])
    return result.results[0]["out_x"]
```

```python
from contextlib import ExitStack

import numpy as np

import concourse.bass as bass
from concourse import mybir

ALU = mybir.AluOpType
ACT = mybir.ActivationFunctionType
AXX = mybir.AxisListType.X
F32 = mybir.dt.float32
F16 = mybir.dt.float16
BF16 = mybir.dt.bfloat16
U8 = mybir.dt.uint8
U32 = mybir.dt.uint32
I32 = mybir.dt.int32

P = 128
B, SQ, D = 8, 256, 128
SK, DC = 512, 96
QT = SQ // P
KC = SK // P
NT = B * QT
HEADS = 16
HG = 4
NG = HEADS // HG
EPS = 1e-5
CLAMP = 10000.0
IPA = 4
RANK = 32
HIDE_ROW, HIDE_KEY = 30000.0, -30000.0
W_SCALE = 64.0
SHIFT_K = 64.0
MASK_Q, MASK_K = 60000.0, 60000.0


SEMAPHORES = []


def alloc(nc, ctx, name):
    def sb(n, shape, dt=F32):
        return ctx.enter_context(nc.sbuf_tensor(f"{name}_{n}", shape, dt))

    def ps(n, shape, dt=F32):
        return ctx.enter_context(nc.psum_tensor(f"{name}_{n}", shape, dt))

    def sem(n):
        SEMAPHORES.append(nc.alloc_semaphore(f"{name}_{n}"))
        return SEMAPHORES[-1]
    return sb, ps, sem


def wait(eng, sem, value):
    if not isinstance(value, int) or value > 0:
        eng.wait_ge(sem, value)


def at_batch(ap, b):
    return ap[b] if isinstance(b, int) else ap[bass.ds(b, 1)].rearrange("a p n -> (a p) n")


class Shape:

    def __init__(self, name, wide, clip=False, ipa=False, bias=False, mask=False, out_bias=True, gate=0):
        self.name, self.wide, self.clip, self.ipa = name, wide, clip, ipa
        self.bias, self.mask, self.out_bias, self.gate = bias, mask, out_bias, gate
        self.dh = 64 if wide else D // HEADS
        self.scale = self.dh ** -0.5
        self.pairs = 2
        self.parts = 2 if wide else 1
        self.shift_row = 0 if wide else 25
        self.shift_k = MASK_K if mask else SHIFT_K
        self.keys = SK - IPA if ipa else SK
        if wide:
            self.pieces = [[("V", 0)], [("Q", 0)], [("Q", 1)], [None, ("V", 1)]]
        else:
            self.pieces = [[("V", 0)], [("K", 0)], [("Q", 0)], []]
        self.rows_at = [[0], [1, 2], [3], []] if wide else [[0, 1], [2, 3], [], []]
        self.turn_step = 3 if wide else 2

    def slots(self, kind):
        out = []
        for g in range(NG):
            for s in range(HG):
                pcs = self.pieces[s] if not (kind == "last" and g >= NG - 2) else []
                if not self.wide and s == 0 and g != NG - 2:
                    pcs = []
                tail = []
                more = not (kind == "last" and g == NG - 1)
                if s == self.turn_step and more:
                    tail.append(("MT",))
                if s == 3 and more and self.clip:
                    tail += [("NB", 0), ("NB", 1)]
                if (g, s) == (1, 1) and kind != "first":
                    tail.append(("OP",))
                if self.ipa:
                    tail += {(0, 1): [("MI",)], (0, 2): [("VI",)], (1, 0): [("SI",)], (1, 1): [("G",)],
                             (3, 1): [("PT",)]}.get((g, s), [])
                if (g, s) == (1, 3) and kind != "last":
                    tail.append(("XT",))
                out.append((g, s, pcs[0] if pcs else None, pcs[1] if len(pcs) > 1 else None, [(h, t) for h in self.rows_at[s] for t in range(QT)] if more else [], tail))
        return out

    def opening(self):
        first = [p for ps_ in self.pieces for p in ps_ if p]
        return ([("XT",)] + [(0,) + p for p in first] + [(1,) + p for p in first if self.wide or p[0] != "V"]
                + [("MT",)] + [("NB", i) for i in range(2)] * self.clip)

    def order(self, kind):
        out = []
        for g, s, p1, p2, _, tail in self.slots(kind):
            out += [(g, s) + p for p in (p1, p2) if p] + [(g, s) + t for t in tail]
        return out

    def turn(self, kind, b, key):
        n0 = len(self.opening())
        if kind == "opening":
            return self.opening().index(key)
        pos = self.order(kind).index(key)
        nf, nm = len(self.order("first")), len(self.order("mid"))
        if kind == "first":
            return n0 + pos
        if kind == "last":
            return n0 + nf + (B - 2) * nm + pos
        return (b - 1) * nm + (n0 + nf + pos)

    def place(self, kind, key):
        n0, nf, nm = len(self.opening()), len(self.order("first")), len(self.order("mid"))
        if key is None:
            at = self.end_turn()
        elif kind == "mid":
            at = n0 + nf + (self.par == 0) * nm + self.order(kind).index(key)
            return at % 2, self.round * nm + at // 2
        else:
            at = self.turn(kind, 0, key)
        return at % 2, at // 2

    def shift_place(self, kind, g):
        if g:
            return self.place(kind, (g - 1, self.turn_step, "MT"))
        if kind == "first":
            return self.place("opening", ("MT",))
        n0, nf, nm = len(self.opening()), len(self.order("first")), len(self.order("mid"))
        back = nm - self.order("mid").index((NG - 1, self.turn_step, "MT"))
        if kind == "mid":
            at = n0 + nf + (self.par == 0) * nm - back
            return at % 2, self.round * nm + at // 2
        at = n0 + nf + (B - 2) * nm - back
        return at % 2, at // 2

    def end_turn(self):
        return len(self.opening()) + len(self.order("first")) + (B - 2) * len(self.order("mid")) + len(self.order("last"))


def attention(nc, sh, dram, res, const, beside=None):
    wide, clip, ipa = sh.wide, sh.clip, sh.ipa
    x_res, gates = res
    ident, identb, cvec, bsel, ones, eps = const
    with ExitStack() as ctx:
        sb, ps, sem = alloc(nc, ctx, sh.name)
        rows = DC if wide else DC + 2

        if wide:
            inner = HEADS * sh.dh
            wq, wk, wv = (sb(n, [P, inner]) for n in ("wq", "wk", "wv"))
            wo = sb("wo", [P, inner // P, D])
            wqT = sb("wqT", [P, HEADS // 2, D])
            wkT = sb("wkT", [P, HEADS // 2, DC])
            wqk = [sb(f"wqk_{part}", [P, HEADS, DC], F16) for part in ("hi", "lo")]
            wv_pair = [sb(f"wv_{part}", [P, inner], F16) for part in ("hi", "lo")]
            if ipa:
                wkiT = sb("wkiT", [P, HEADS // 2, DC])
                wkq_i = sb("wkq_i", [P, HEADS, D])
                sel_w = sb("sel_w", [P, HEADS * IPA])
                wki, wvi = sb("wki", [P, inner]), sb("wvi", [P, inner])
                lora_up = {n: sb(f"{n}_up", [RANK, inner]) for n in "qkv"}
                lora_dn = {n: sb(f"{n}_dn", [RANK, D]) for n in "qkv"}
                o_dn, o_up = sb("o_dn", [RANK, inner]), sb("o_up", [RANK, D])
                alpha = sb("alpha", [P, 4])
            v_ipa = sb("v_ipa", [P, HEADS // 2, 64]) if ipa else None
            g_ipa = sb("g_ipa", [64, D]) if ipa else None
            s_ipa = sb("s_ipa", [P, QT, HEADS, IPA]) if ipa else None
            e_ipa = sb("e_ipa", [P, QT * HEADS, IPA]) if ipa else None
            m_ipa = sb("m_ipa", [P, QT * HEADS]) if ipa else None
            r_ipa = sb("r_ipa", [P, QT * HEADS]) if ipa else None
            p_ipa = sb("p_ipa", [P, QT * HEADS, IPA]) if ipa else None
            pt_ipa = sb("pt_ipa", [64, SQ]) if ipa else None
        else:
            wq_in, wk_in = sb("wq_in", [P, D]), sb("wk_in", [P, D])
            wv = sb("wv", [P, D])
            wq, wk = sb("wq", [P, NG, P]), sb("wk", [P, NG, P])
            wo = sb("wo", [P, NG, D])
            q_add = sb("q_add", [P, NG])
            q_add_hi = sb("q_add_hi", [P, NG])
        bo = sb("bo", [1, D]) if sh.out_bias else None
        keyrow = None if wide else sb("keyrow", [P, HG, P], F16)

        ctxb = [sb(f"ctxb{i}", [P, SK]) for i in range(2)]
        stats = sb("stats", [P, NT, 6])
        mv = sb("mv", [P, NT, 2])
        lnv = sb("lnv", [P, NT])
        rstd = sb("rstd", [P, NT])
        xn = sb("xn", [P, QT, D])
        xnT = sb("xnT", [P, SQ])
        xnT_pair = [sb(f"xnT_{part}", [P, SQ], F16) for part in ("hi", "lo")] if wide else None
        if wide:
            ctx_hi = [sb(f"ctx_hi{i}", [P, SK], F16) for i in range(2)]
            ctx_lo = [sb(f"ctx_lo{i}", [P, SK], F16) for i in range(2)]
            q_hi = [sb(f"q_hi{i}", [P, HG, SQ], F16) for i in range(4)]
            q_lo = [sb(f"q_lo{i}", [P, HG, SQ], F16) for i in range(4)]
        else:
            chi_k, chi_q = sb("chi_k", [P, SK], F16), sb("chi_q", [P, SQ], F16)
            kst = [sb(f"kst{i}", [P, SK], F16) for i in range(4)]
            qst = [sb(f"qst{i}", [P, SQ], F16) for i in range(4)]
        vst = [sb(f"vst{i}", [P, KC, HG * 64] if wide else [P, KC, HEADS, 32]) for i in range(4 if wide else 2)]
        neg_max = sb("neg_max", [P, HG, QT])
        rest = sb("rest", [P, HG, QT])
        shift_parts = sb("shift_parts", [P, QT, HG, 32], F16)
        probs = [sb(f"probs{i}", [P, KC, SQ]) for i in range(2 * HG)]
        attn = sb("attn", [P, HEADS * (64 if wide else 32) // P, SQ])
        r_sum = sb("r_sum", [P, SQ])
        if wide:
            fold = sb("fold", [P, 2, SQ])
            folded = [sb(f"folded{i}", [P, SQ]) for i in range(2 * HG)]
        else:
            u_sb = sb("u_sb", [P, SQ])
        if clip:
            floor = [sb(f"floor{i}", [P, HG, SQ]) for i in range(2)]
            minus_clamp = sb("minus_clamp", [P, 1])

        rowmax_ps = ps("rowmax_ps", [P, QT, SK])
        st_ps = [ps(f"st_ps{i}", [P, KC // 2, SQ]) for i in range(3)]
        u_ps = ps("u_ps", [P, 2, SQ])
        banks = [ps(f"bank{i}", [P, 512]) for i in range(2)]

        loaded = sem("loaded")
        weights_ok = sem("weights_ok")
        preset = sem("preset")
        lora_ready = sem("lora_ready")
        ctx_loaded = sem("ctx_loaded")
        ctx_ready = sem("ctx_ready")
        stats_ready = sem("stats_ready")
        rstd_ready = sem("rstd_ready")
        xn_ready = sem("xn_ready")
        xnT_ready = sem("xnT_ready")
        bank_full = sem("bank_full")
        bank_free = [sem(f"bank_free{i}") for i in range(2)]
        hi_ready = sem("hi_ready")
        rows_ready = sem("rows_ready")
        max_ready = sem("max_ready")
        parts_step = sem("parts_step")
        parts_ready = sem("parts_ready")
        capped = sem("capped")
        setup_pe = sem("setup_pe")
        setup_sb = sem("setup_sb")
        pair_step = sem("pair_step")
        st_ready = sem("st_ready")
        exp_ready = sem("exp_ready")
        hi_step = sem("hi_step")
        fold_step = sem("fold_step")
        pool_ready = sem("pool_ready")
        pv_ready = sem("pv_ready")
        u_ready = sem("u_ready")
        div_ready = sem("div_ready")
        rsum_ready = sem("rsum_ready")
        attn_ready = sem("attn_ready")
        passed = sem("passed")
        pool_passed = sem("pool_passed")
        pe_passed = sem("pe_passed")
        ipa_step = sem("ipa_step")
        ipa_exp = sem("ipa_exp")

        def batches(body, eng):
            sh.par = 0
            body("first", 0, 0)
            with eng.Fori(0, (B - 2) // 2) as i:
                for par in (1, 0):
                    sh.round, sh.par = i, par
                    body("mid", i * 2 + (2 - par), par)
            sh.par = (B - 1) % 2
            body("last", B - 1, sh.par)

        def shared(kind, key):
            p, _ = sh.place(kind, key)
            return banks[p], bank_free[p]

        def been_read(eng, kind, key, upto=1):
            p, n = sh.place(kind, key)
            wait(eng, bank_free[p], n + upto)

        def floor_place(kind, g):
            if g:
                p, n = sh.place(kind, (g - 1, 3, "NB", 1))
                return p, n + 1
            p, n = sh.place(kind, ("NB", 1)) if kind == "opening" else sh.shift_place(kind, 0)
            return p, n + 2

        def shifted(eng, kind, g):
            p, n = sh.shift_place(kind, g)
            eng.wait_ge(bank_free[p], n + 1)

        def lora_ps(i):
            if i < 3:
                return st_ps[i][:, :, :].rearrange("p c q -> p (c q)")
            if i < 5:
                return rowmax_ps[:, i - 3, :]
            return u_ps[:, :, :].rearrange("p a q -> p (a q)") if i == 5 else banks[i - 6][:, :]

        def cap(dve, g, s):
            pr = probs[(g % 2) * HG + s][:, :, :]
            return dve.scalar_tensor_tensor(pr, pr, 1.0, floor[g % 2][:, s:s + 1, :].broadcast_to([P, KC, SQ]),
                                            ALU.min, ALU.max)

        def stats_of_all(dve):
            for t in range(NT):
                ins = dve.bn_stats(stats[:, t, :], x_res[:, t, :])
            ins.then_inc(stats_ready, 1)
            dve.wait_ge(stats_ready, 1)
            for t in range(NT):
                ins = dve.bn_aggr(mv[:, t, :], stats[:, t, :])
            ins.then_inc(stats_ready, 1)

        def x_of(b):
            return x_res[:, b * QT:(b + 1) * QT, :] if isinstance(b, int) else x_res[:, bass.ds(b * QT, QT), :]

        turned = [(wq, D), (wk, DC)] if wide else []
        if ipa:
            turned.append((wki, DC))
        block = ctx.enter_context(nc.Block())

        n_loads = 0

        @block.sync
        def _(sp):
            nonlocal n_loads

            def load(dst, src):
                nonlocal n_loads
                n_loads += 1
                sp.dma_start(dst, src).then_inc(loaded, 16)

            def load_ctx(b, par):
                sp.dma_start(ctxb[par][0:DC, :], at_batch(dram["ctxT"], b)).then_inc(ctx_loaded, 16)
                if sh.mask:
                    sp.dma_start(ctxb[par][DC:DC + 1, :], at_batch(dram["mask_row"], b)).then_inc(ctx_loaded, 16)

            if sh.mask:
                sp.wait_ge(preset, 2)
            load_ctx(0, 0)
            if wide:
                for hi in ctx_hi:
                    load(hi[DC:P, :], dram["ctx_tail"])
                load(wq[:, :], dram["Wq"])
                load(wk[0:DC, :], dram["Wk"])
                load(wv[0:DC, :], dram["Wv"])
                load(wo[:, :, :], dram["Wo"].rearrange("(i p) n -> p i n", p=P))
                if ipa:
                    load(wki[0:DC, :], dram["Wk_ipa"])
                    load(wvi[0:DC, :], dram["Wv_ipa"])
                    for n in "qkv":
                        load(lora_up[n][:, :], dram[f"{n}_up"])
                        load(lora_dn[n][:, 0:D if n == "q" else DC], dram[f"{n}_downT"])
                    load(o_up[:, :], dram["o_up"])
                    load(o_dn[:, :], dram["o_downT"])
                    for i, n in enumerate("qkvo"):
                        load(alpha[:, i:i + 1], dram[f"{n}_alpha"].partition_broadcast(P))
            else:
                load(wq_in[:, :], dram["Wq"])
                load(wk_in[0:DC, :], dram["Wk"])
                load(wv[0:DC, :], dram["Wv"])
                if sh.bias:
                    load(wk_in[DC:DC + 1, :], dram["bk"].unsqueeze(0))
                    load(wv[DC:DC + 1, :], dram["bv"].unsqueeze(0))
                if not sh.mask:
                    sp.wait_ge(preset, 2)
                for j in range(HG):
                    load(wo[32 * j:32 * j + sh.dh, :, :],
                         dram["Wo"].rearrange("(g j d) n -> j d g n", g=NG, j=HG)[j])
                if sh.bias:
                    for j in range(HG):
                        for i in range(3):
                            at = 32 * j + sh.dh * i
                            load(q_add[at:at + sh.dh, :], dram["bqT"][j])
                else:
                    load(q_add[:, :], dram["mask_q"])
                if sh.mask:
                    load(wk[DC:DC + 1, :, :], dram["mask_k_row"])
                load(wk[DC + 1:DC + 2, :, :], dram["shift_k_row"])
                if clip:
                    load(keyrow[:, :, :], dram["keyrow"])
            if sh.out_bias:
                load(bo[:, :], dram["bo"].unsqueeze(0))
            if beside:
                beside.load(sp)

            def body(kind, b, par):
                if kind != "last":
                    sp.wait_ge(bank_full, sh.turn(kind, b, sh.order(kind)[0]))
                    load_ctx(b + 1, 1 - par)
            batches(body, sp)

        n_loads = sum([6 * wide, ipa * (2 + 6 + 2 + 4), (not wide) * (4 + HG + 2 * sh.bias), sh.bias * 12,
                       (not wide and not sh.bias) * 1, sh.mask * 1, clip * 1, sh.out_bias * 1])
        ctx_dmas = 16 * (1 + sh.mask)

        @block.gpsimd
        def _(pool):
            def context_pair(b, par):
                pool.wait_ge(ctx_loaded, (b + 1) * ctx_dmas)
                pool.sem_inc(pool_passed, 1)
                pool.tensor_copy(ctx_hi[par][0:DC, :], ctxb[par][0:DC, :]).then_inc(hi_step, 1)
                pool.wait_ge(hi_step, b + 1)
                pool.tensor_tensor(ctx_lo[par][0:DC, :], ctxb[par][0:DC, :], ctx_hi[par][0:DC, :],
                                   ALU.subtract).then_inc(ctx_ready, 1)

            if wide:
                context_pair(0, 0)

            def body(kind, b, par):
                for g, s, *_ in sh.slots(kind):
                    n = (b * NG + g) * HG + s
                    pr = probs[(g % 2) * HG + s]
                    pool.wait_ge(exp_ready, n * 2 + 2)
                    wait(pool, pool_ready, n)
                    pool.tensor_tensor(fold[:, :, :], pr[:, 0:2, :], pr[:, 2:4, :], ALU.add).then_inc(fold_step, 1)
                    pool.wait_ge(fold_step, n + 1)
                    pool.tensor_tensor(folded[(g % 2) * HG + s][:, :], fold[:, 0, :], fold[:, 1, :],
                                       ALU.add).then_inc(pool_ready, 1)
                    if (g, s) == (0, HG - 1) and kind != "last":
                        context_pair(b + 1, 1 - par)
            if wide:
                batches(body, pool)
            if beside:
                beside.run(pool)

        @block.scalar
        def _(act):
            def evacuate(kind, b, key, u, what):
                turn = sh.turn(kind, b, key)
                name = what[0]
                if name in ("MT", "OP", "SI"):
                    return
                act.wait_ge(bank_full, turn + 1)
                bank, free = shared(kind, key)
                ub = u % 4 if isinstance(u, int) else what[-1]
                if name == "V":
                    i = what[1]
                    if wide:
                        act.activation(vst[ub][:, 2 * i:2 * i + 2, :], bank[:, :].rearrange("p (c n) -> p c n", c=2),
                                       ACT.Copy, scale=1.0 / W_SCALE).then_inc(free, 1)
                    else:
                        act.copy(vst[0 if kind == "opening" else 1 - sh.par][:, :, :, 0:sh.dh],
                                 bank[:, :].rearrange("p (c h d) -> p c h d", c=KC, h=HEADS)).then_inc(free, 1)
                elif name == "K":
                    act.activation(chi_k[:, :], bank[:, :], ACT.Copy, scale=cvec[:, 0:1]).then_inc(hi_ready, 1)
                elif name == "Q" and wide:
                    i = what[1]
                    act.activation(q_hi[ub][0:DC, 2 * i:2 * i + 2, :], bank[0:DC, :].rearrange("p (h q) -> p h q", h=2),
                                   ACT.Copy, scale=1.0 / W_SCALE).then_inc(hi_ready, 1)
                elif name == "Q":
                    act.activation(chi_q[:, :], bank[:, 0:SQ], ACT.Identity, scale=cvec[:, 1:2],
                                   bias=q_add_hi[:, ub:ub + 1]).then_inc(hi_ready, 1)
                elif name == "XT":
                    if wide:
                        act.copy(xnT_pair[0][:, :], bank[:, 0:SQ])
                    act.copy(xnT[:, :], bank[:, 0:SQ]).then_inc(free if not wide else xnT_ready, 1)
                elif name == "NB":
                    i = what[1]
                    act.activation(floor[what[-1] % 2][:, 2 * i:2 * i + 2, :],
                                   bank[:, :].rearrange("p (h q) -> p h q", h=2), ACT.Exp,
                                   bias=minus_clamp[:, 0:1], scale=sh.scale).then_inc(free, 1)
                elif name == "MI":
                    act.copy(sel_w[:, :], bank[:, 0:HEADS * IPA]).then_inc(free, 1)
                elif name == "VI":
                    src = bank[:, 0:HEADS // 2 * IPA].rearrange("p (i t) -> p i t", t=IPA)
                    flat = v_ipa[:, :, :].rearrange("p i n -> p (i n)")
                    for hh in range(2):
                        for i in range(HEADS // 2):
                            at = i * 64 + (2 * i + hh) * IPA
                            ins = act.copy(flat[64 * hh:64 * hh + 64, at:at + IPA], src[64 * hh:64 * hh + 64, i, :])
                    ins.then_inc(free, 1)
                elif name == "G":
                    act.copy(g_ipa[:, :], bank[0:64, 0:D]).then_inc(free, 1)
                elif name == "PT":
                    act.copy(pt_ipa[:, :], bank[0:64, 0:SQ]).then_inc(free, 1)

            act.wait_ge(stats_ready, 2)
            act.activation(lnv[:, :], mv[:, :, 1], ACT.Ln, bias=eps[:, 0:1]).then_inc(rstd_ready, 1)
            act.wait_ge(rstd_ready, 1)
            act.activation(rstd[:, :], lnv[:, :], ACT.Exp, scale=-0.5).then_inc(rstd_ready, 1)
            if not wide:
                act.wait_ge(weights_ok, 1)
            for key in sh.opening():
                if key[0] in (0, 1):
                    evacuate("opening", 0, key, key[0], key[1:])
                else:
                    evacuate("opening", 0, key, 0, key + (0,))

            def body(kind, b, par):
                for g, s, p1, p2, tiles, tail in sh.slots(kind):
                    n = (b * NG + g) * HG + s
                    if p1:
                        evacuate(kind, b, (g, s) + p1, None, p1 + ((g + 2) % 4,))
                    for half in range(2):
                        act.wait_ge(st_ready, n * 2 + (half + 1))
                        act.activation(probs[(g % 2) * HG + s][:, 2 * half:2 * half + 2, :],
                                       st_ps[(2 * s + half) % 3][:, :, :], ACT.Exp, scale=sh.scale).then_inc(exp_ready, 1)
                        if ("NB", half) in tail:
                            evacuate(kind, b, (g, s, "NB", half), None, ("NB", half, (g + 1) % 4))
                    if p2:
                        evacuate(kind, b, (g, s) + p2, None, p2 + ((g + 2) % 4,))
                    if not wide and s == 1 and not (kind == "first" and g == 0):
                        act.wait_ge(pv_ready, b * NG + g)
                        act.copy(u_sb[:, :], u_ps[:, 0, :]).then_inc(u_ready, 1)
                    for t in tail:
                        if t[0] != "NB":
                            evacuate(kind, b, (g, s) + t, None, t + ((g + 1) % 4,))
                    if ipa and (g, s) == (2, HG - 1):
                        been_read(act, kind, (1, 0, "SI"))
                        act.activation(e_ipa[:, :, :], s_ipa[:, :, :, :].rearrange("p a h t -> p (a h) t"), ACT.Exp,
                                       scale=sh.scale).then_inc(ipa_exp, 1)
            batches(body, act)
            if not wide:
                act.wait_ge(pv_ready, B * NG)
                act.copy(u_sb[:, :], u_ps[:, 0, :]).then_inc(u_ready, 1)

        @block.tensor
        def _(pe):
            def use(kind, b, key, u, what, par):
                name = what[0]
                been_read(pe, kind, key, upto=0)
                if name == "Q" and (kind == "opening" or (key[0], what[1]) == (2, 0)):
                    been_read(pe, kind, ("XT",) if kind == "opening" else (1, 3, "XT"))
                if what == ("NB", 0):
                    been_read(pe, kind, ("MT",) if kind == "opening" else (key[0], sh.turn_step, "MT"))
                bank, _ = shared(kind, key)
                if name == "V":
                    i = what[1]
                    if wide:
                        for c in range(2):
                            at = (2 * i + c) * P
                            cols = slice(u * 256, (u + 1) * 256)
                            for n, (ctx_part, w_part) in enumerate(((ctx_hi, 1), (ctx_lo, 0), (ctx_hi, 0))):
                                ins = pe.matmul(bank[:, c * 256:(c + 1) * 256], ctx_part[par][0:DC, at:at + P],
                                                wv_pair[w_part][0:DC, cols], start=(n == 0), stop=(n == 2))
                    else:
                        r = DC + 1 if sh.bias else DC
                        for c in range(KC):
                            ins = pe.matmul(bank[:, c * P:(c + 1) * P], ctxb[par][0:r, c * P:(c + 1) * P],
                                            wv[0:r, :], start=True, stop=True)
                elif name == "K":
                    ins = pe.matmul(bank[:, :], wk[0:rows, u, :], ctxb[par][0:rows, :], start=True, stop=True)
                elif name == "Q":
                    if wide:
                        for j in range(2):
                            h = u * HG + 2 * what[1] + j
                            for n, (w_part, x_part) in enumerate(((1, 0), (0, 1), (0, 0))):
                                ins = pe.matmul(bank[0:DC, j * SQ:(j + 1) * SQ], wqk[w_part][:, h, :],
                                                xnT_pair[x_part][:, :], start=(n == 0), stop=(n == 2))
                    else:
                        ins = pe.matmul(bank[:, 0:SQ], wq[:, u, :], xnT[:, :], start=True, stop=True)
                elif name == "XT":
                    pe.wait_ge(xn_ready, b_next(kind, b))
                    for t in range(QT):
                        ins = pe.transpose(bank[:, t * P:(t + 1) * P], xn[:, t, :], ident[:, :])
                elif name == "MT":
                    pe.wait_ge(parts_ready, unit_next(kind, b, key) + 1)
                    view = bank[:, :].bitcast(F16)
                    for t in range(QT):
                        for h in range(HG if wide else 1):
                            if wide:
                                ins = pe.transpose(view[DC:P, h * SQ + t * P:h * SQ + (t + 1) * P],
                                                   shift_parts[:, t, h, :], dram["identh"][:, :])
                            else:
                                ins = pe.transpose(view[:, t * P:(t + 1) * P],
                                                   shift_parts[:, t, :, :].rearrange("p h k -> p (h k)"),
                                                   dram["identh"][:, :])
                elif name == "NB":
                    g1 = (key[0] + 1) % 4 if kind != "opening" else 0
                    for j in range(2):
                        ins = pe.matmul(bank[:, j * SQ:(j + 1) * SQ], keyrow[:, 2 * what[1] + j, :], qst[g1][:, :],
                                        start=True, stop=True)
                elif name == "MI":
                    for h in range(HEADS):
                        ins = pe.matmul(bank[:, h * IPA:(h + 1) * IPA], wkq_i[0:DC, h, :], ctxb[par][0:DC, sh.keys:SK],
                                        start=True, stop=True)
                elif name == "SI":
                    for t in range(QT):
                        ins = pe.matmul(bank[:, t * 64:(t + 1) * 64], xnT[:, t * P:(t + 1) * P], sel_w[:, :],
                                        start=True, stop=True)
                elif name == "VI":
                    for i in range(HEADS // 2):
                        ins = pe.matmul(bank[:, i * IPA:(i + 1) * IPA], wvi[0:DC, i * P:(i + 1) * P],
                                        ctxb[par][0:DC, sh.keys:SK], start=True, stop=True)
                elif name == "G":
                    for i in range(HEADS // 2):
                        ins = pe.matmul(bank[0:64, 0:D], v_ipa[:, i, :], wo[:, i, :],
                                        start=(i == 0), stop=(i == HEADS // 2 - 1))
                elif name == "PT":
                    pe.wait_ge(ipa_step, 4 * b + 4)
                    pe.sem_inc(pe_passed, 1)
                    for t in range(QT):
                        ins = pe.transpose(bank[0:64, t * P:(t + 1) * P],
                                           p_ipa[:, t * HEADS:(t + 1) * HEADS, :].rearrange("p h t -> p (h t)"),
                                           ident[:, :])
                elif name == "OP":
                    ins = out_projection(bank, b * NG * sh.parts)
                ins.then_inc(bank_full, 1)

            def b_next(kind, b):
                return 1 if kind == "opening" else b + 2

            def unit_next(kind, b, key):
                return 0 if kind == "opening" else b * NG + key[0] + 1

            def out_projection(bank, parts_before):
                pe.wait_ge(attn_ready, parts_before)
                chunks = attn.shape[1]
                for t in range(QT):
                    dst = bank[:, t * D:(t + 1) * D]
                    rest_ = (1 if ipa else 0) + (1 if bo is not None else 0)
                    for i in range(chunks):
                        ins = pe.matmul(dst, attn[:, i, t * P:(t + 1) * P], wo[:, i, :],
                                        start=(i == 0), stop=(i == chunks - 1 and rest_ == 0))
                    if ipa:
                        ins = pe.matmul(dst, pt_ipa[:, t * P:(t + 1) * P], g_ipa[:, :], start=False, stop=(bo is None))
                    if bo is not None:
                        ins = pe.matmul(dst, ones[0:1, 0:P], bo[0:1, :], start=False, stop=True)
                return ins

            def row_scores(ub, u, h, t, par):
                wait(pe, max_ready, u * (HG * QT) + (h * QT + t - 1))
                if wide:
                    ins = pe.matmul(rowmax_ps[:, t, :], q_hi[ub][0:DC, h, t * P:(t + 1) * P],
                                    ctx_hi[par][0:DC, :], start=True, stop=True)
                else:
                    r = slice(32 * h, 32 * h + 32)
                    ins = pe.matmul(rowmax_ps[:, t, :], qst[ub][r, t * P:(t + 1) * P], kst[ub][r, :],
                                    start=True, stop=True)
                ins.then_inc(rows_ready, 1)

            def key_scores(ub, u, h, half, par):
                j = 2 * h + half
                wait(pe, exp_ready, u * 2 * HG + (j - 2 if j >= 3 else (-1, 0, -2)[j]))
                for c in range(2 * half, 2 * half + 2):
                    dst = st_ps[j % 3][:, c % 2, :]
                    k = slice(c * P, (c + 1) * P)
                    if wide:
                        pe.matmul(dst, ctx_hi[par][0:DC, k], q_lo[ub][0:DC, h, :], start=True, stop=False)
                        pe.matmul(dst, ctx_lo[par][0:DC, k], q_hi[ub][0:DC, h, :], start=False, stop=False)
                        ins = pe.matmul(dst, ctx_hi[par][:, k], q_hi[ub][:, h, :], start=False, stop=True)
                    else:
                        r = slice(32 * h, 32 * h + 32)
                        ins = pe.matmul(dst, kst[ub][r, k], qst[ub][r, :], start=True, stop=True)
                ins.then_inc(st_ready, 1)

            def values(ub, u, part, vpar):
                wait(pe, attn_ready, sh.parts * u + part)
                heads = range(2 * part, 2 * part + 2) if wide else range(HG)
                w = 64 if wide else 32
                if clip or wide:
                    pe.wait_ge(capped if clip else pool_ready, u * HG + heads[-1] + 1)
                else:
                    pe.wait_ge(exp_ready, u * 2 * HG + 2 * HG)
                for c in range(KC):
                    for n, h in enumerate(heads):
                        lhs = vst[ub][:, c, h * 64:(h + 1) * 64] if wide else vst[vpar][:, c, ub * HG + h, :]
                        ins = pe.matmul(u_ps[w * n:w * n + w, 0, :], lhs, probs[(ub % 2) * HG + h][:, c, :],
                                        start=(c == 0), stop=(c == KC - 1), skip_group_check=True)
                if wide:
                    for n, h in enumerate(heads):
                        ins = pe.matmul(u_ps[w * n:w * n + w, 1, :], ones[:, 0:64], folded[(ub % 2) * HG + h][:, :],
                                        start=True, stop=True)
                ins.then_inc(pv_ready, 1)

            def divisors(u):
                pe.wait_ge(u_ready, u + 1)
                pe.matmul(u_ps[:, 1, :], bsel[:, :], u_sb[:, :], start=True, stop=True).then_inc(div_ready, 1)

            pe.wait_ge(loaded, 16 * n_loads)
            if ipa:
                for i, n in enumerate("qkv"):
                    r = D if n == "q" else DC
                    for half in range(2):
                        pe.matmul(lora_ps(2 * i + half)[0:r, :], lora_dn[n][:, 0:r],
                                  lora_up[n][:, half * 512:(half + 1) * 512], start=True, stop=True)
                for i in range(HEADS // 2):
                    ins = pe.matmul(lora_ps(6 + i // 4)[:, (i % 4) * D:(i % 4 + 1) * D],
                                    o_dn[:, i * P:(i + 1) * P], o_up[:, :], start=True, stop=True)
                ins.then_inc(lora_ready, 1)
            if ipa or not wide:
                pe.wait_ge(weights_ok, 1)
            if wide:
                banks = [[lora_ps(0), lora_ps(1)], [lora_ps(2), lora_ps(3)], [lora_ps(4), lora_ps(5)]]
                for k, (w, r) in enumerate(turned):
                    for i in range(HEADS // 2):
                        at = (i % 4) * r
                        ins = pe.transpose(banks[k][i // 4][:, at:at + r], w[0:r, i * P:(i + 1) * P], ident[0:r, 0:r])
                ins.then_inc(setup_pe, 1)
                pe.wait_ge(setup_sb, 1)
                for i in range(HEADS // 2):
                    for j in range(2):
                        rows_j = slice(64 * j, 64 * j + 64)
                        ins = pe.matmul(lora_ps(2 * j + i // 4)[:, (i % 4) * DC:(i % 4 + 1) * DC], wqT[rows_j, i, :],
                                        wkT[rows_j, i, :], start=True, stop=True)
                ins.then_inc(setup_pe, 1)
                if ipa:
                    for i in range(HEADS // 2):
                        for j in range(2):
                            rows_j = slice(64 * j, 64 * j + 64)
                            ins = pe.matmul(lora_ps(4 + 2 * j + i // 4)[0:DC, (i % 4) * D:(i % 4 + 1) * D],
                                            wkiT[rows_j, i, :], wqT[rows_j, i, :], start=True, stop=True)
                    ins.then_inc(setup_pe, 1)
                pe.wait_ge(setup_sb, 3 if ipa else 2)
            pe.wait_ge(ctx_loaded, ctx_dmas)
            if wide:
                pe.wait_ge(ctx_ready, 1)
            for key in sh.opening():
                if key[0] == "MT":
                    for before in sh.opening()[-2 - len(sh.opening()) + sh.opening().index(key):][:2]:
                        been_read(pe, "opening", before)
                    for h in range(HG):
                        for t in range(QT):
                            row_scores(0, 0, h, t, 0)
                use("opening", 0, key, key[0] if key[0] in (0, 1) else 0, key[1:] if key[0] in (0, 1) else key,
                    0)

            def body(kind, b, par):
                for g, s, p1, p2, tiles, tail in sh.slots(kind):
                    u = b * NG + g
                    par1 = par if g < NG - 1 else 1 - par
                    g2 = (g + 2) % 4
                    par2 = par if g < NG - 2 else 1 - par
                    if (g, s) == (2, 0) and kind != "last":
                        pe.wait_ge(ctx_loaded, (b + 2) * ctx_dmas)
                    if wide and (g, s) == (2, 0) and kind != "last":
                        pe.wait_ge(ctx_ready, b + 2)
                    if p1:
                        use(kind, b, (g, s) + p1, g2, p1, par2)
                    if s == 0:
                        shifted(pe, kind, g)
                    for half in range(2):
                        if half < len(tiles):
                            row_scores((g + 1) % 4, u + 1, *tiles[half], par1)
                        key_scores(g, u, s, half, par)
                        if ("NB", half) in tail:
                            use(kind, b, (g, s, "NB", half), None, ("NB", half), par)
                    if p2:
                        use(kind, b, (g, s) + p2, g2, p2, par2)
                    if not (kind == "first" and g == 0):
                        if wide and s in (1, 3):
                            values((g - 1) % 4, u - 1, s // 2, None)
                    for tile in tiles[2:]:
                        row_scores((g + 1) % 4, u + 1, *tile, par1)
                    if not wide and s == 1 and not (kind == "first" and g == 0):
                        values((g - 1) % 4, u - 1, 0, par if g else 1 - par)
                    if ("MT",) in tail and s == 2:
                        use(kind, b, (g, s, "MT"), None, ("MT",), par)
                    if not (kind == "first" and g == 0):
                        if not wide and s == 2:
                            divisors(u - 1)
                    for t in tail:
                        if t[0] == "NB" or t[0] == "MT" and s == 2:
                            continue
                        use(kind, b, (g, s) + t, None, t, par)
            batches(body, pe)
            for part in range(sh.parts):
                values(3, B * NG - 1, part, (B - 1) % 2)
            if not wide:
                divisors(B * NG - 1)
            been_read(pe, "last", None, upto=0)
            out_projection(shared("last", None)[0], B * NG * sh.parts).then_inc(bank_full, 1)

        @block.vector
        def _(dve):
            dve.memset(shift_parts[:, :, :, :], 0.0).then_inc(preset, 1)
            dve.wait_ge(preset, 1)
            ins = dve.memset(shift_parts[:, :, :, 3] if wide else minus_clamp[:, :] if clip else shift_parts[:, :, :, 31],
                             HIDE_ROW if wide else -CLAMP if clip else 0.0)
            if ipa:
                ins = dve.memset(v_ipa[:, :, :], 0.0)
            if not wide:
                for c in ctxb:
                    dve.memset(c[DC:DC + 2, :], 1.0)
                for w in [wq, wk, wo, q_add] + vst:
                    ins = dve.memset(w[tuple(slice(None) for _ in w.shape)], 0.0)
            ins.then_inc(preset, 1)
            if not wide:
                dve.wait_ge(preset, 2)
                for v in vst:
                    ins = dve.memset(v[:, :, :, sh.dh:sh.dh + 1], 1.0)
                ins.then_inc(preset, 1)
            stats_of_all(dve)
            dve.wait_ge(loaded, 16 * n_loads)
            if ipa:
                dve.tensor_scalar(alpha[:, :], alpha[:, :], 1.0 / RANK, None, ALU.mult).then_inc(preset, 1)
                dve.wait_ge(preset, 3)
                dve.wait_ge(lora_ready, 1)
                for i, (w, r) in enumerate(((wq, D), (wk, DC), (wv, DC))):
                    for half in range(2):
                        cols = w[0:r, half * 512:(half + 1) * 512]
                        dve.scalar_tensor_tensor(cols, lora_ps(2 * i + half)[0:r, :], alpha[0:r, i:i + 1], cols,
                                                 ALU.mult, ALU.add)
                for i in range(2):
                    four = wo[:, 4 * i:4 * i + 4, :].rearrange("p i n -> p (i n)")
                    ins = dve.scalar_tensor_tensor(four, lora_ps(6 + i), alpha[:, 3:4], four, ALU.mult, ALU.add)
            elif not wide:
                for w, w_in, r in ((wq, wq_in, P), (wk, wk_in, DC + 1 if sh.bias else DC)):
                    dst = w[0:r, :, :].rearrange("p g (j s d) -> p (g j) s d", j=HG, s=4)
                    src = w_in[0:r, :].rearrange("p (h d) -> p h d", d=sh.dh)
                    for s in range(3):
                        dve.tensor_copy(dst[:, :, s, :], src)
                ins = dve.tensor_scalar(q_add_hi[:, :], q_add[:, :], cvec[:, 1:2], None, ALU.mult)
            if ipa or not wide:
                ins.then_inc(weights_ok, 1)
            if wide:
                def halves(k, n):
                    return [lora_ps(k + i)[:, 0:4 * n].rearrange("p (i n) -> p i n", i=4) for i in range(2)]
                if ipa:
                    dve.wait_ge(weights_ok, 1)
                dve.tensor_scalar(wv_pair[0][0:DC, :], wv[0:DC, :], W_SCALE, None, ALU.mult).then_inc(pair_step, 1)
                dve.wait_ge(pair_step, 1)
                dve.scalar_tensor_tensor(wv_pair[1][0:DC, :], wv[0:DC, :], W_SCALE, wv_pair[0][0:DC, :],
                                         ALU.mult, ALU.subtract)
                dve.wait_ge(setup_pe, 1)
                for k, (dst, (_, r)) in enumerate(zip((wqT, wkT, wkiT if ipa else None), turned)):
                    for i, src in enumerate(halves(2 * k, r)):
                        ins = dve.tensor_copy(dst[:, 4 * i:4 * i + 4, :], src)
                ins.then_inc(setup_sb, 1)
                dve.wait_ge(setup_pe, 2)
                hi, lo = (w[:, :, :].rearrange("p (i j) n -> p i j n", j=2) for w in wqk)
                for j in range(2):
                    for i, src in enumerate(halves(2 * j, DC)):
                        ins = dve.tensor_scalar(hi[:, 4 * i:4 * i + 4, j, :], src, W_SCALE, None, ALU.mult)
                ins.then_inc(pair_step, 1)
                dve.wait_ge(pair_step, 2)
                for j in range(2):
                    for i, src in enumerate(halves(2 * j, DC)):
                        ins = dve.scalar_tensor_tensor(lo[:, 4 * i:4 * i + 4, j, :], src, W_SCALE,
                                                       hi[:, 4 * i:4 * i + 4, j, :], ALU.mult, ALU.subtract)
                ins.then_inc(setup_sb, 1)
                if ipa:
                    dve.wait_ge(setup_pe, 3)
                    heads = wkq_i[:, :, :].rearrange("p (i j) n -> p i j n", j=2)
                    for j in range(2):
                        for i, src in enumerate(halves(4 + 2 * j, D)):
                            ins = dve.tensor_copy(heads[0:DC, 4 * i:4 * i + 4, j, :], src[0:DC])
                    ins.then_inc(setup_sb, 1)

            def pair(kind, b, key, what, unit):
                name, i = what
                idx = i if wide else int(name == "Q")
                ub = (key[0] + 2) % 4 if kind != "opening" else key[0]
                dve.wait_ge(bank_full, sh.turn(kind, b, key) + 1)
                dve.wait_ge(hi_ready, sh.pairs * unit + idx + 1)
                bank, free = shared(kind, key)
                if wide:
                    src = bank[0:DC, :].rearrange("p (h q) -> p h q", h=2)
                    dst, hi = (q[ub][0:DC, 2 * i:2 * i + 2, :] for q in (q_lo, q_hi))
                    dve.scalar_tensor_tensor(dst, src, 1.0 / W_SCALE, hi, ALU.mult, ALU.subtract).then_inc(free, 1)
                    return
                elif name == "K":
                    src, hi, dst = bank[:, :], chi_k[:, :], kst[ub][:, :]
                else:
                    src, hi, dst = bank[:, 0:SQ], chi_q[:, :], qst[ub][:, :]
                if name == "Q":
                    dve.scalar_tensor_tensor(dst, src, q_add[:, ub:ub + 1], hi, ALU.add, ALU.subtract).then_inc(free, 1)
                    return
                dve.tensor_tensor(dst, src, hi, ALU.subtract).then_inc(free, 1)

            def normalise(b):
                dve.wait_ge(rstd_ready, 2)
                x = x_of(b)
                for t in range(QT):
                    at = bass.ds(b * QT + t, 1)
                    ins = dve.tensor_scalar(xn[:, t, :], x[:, t, :], mv[:, at, 0:1].rearrange("p a n -> p (a n)"),
                                            rstd[:, at], ALU.subtract, ALU.mult)
                ins.then_inc(xn_ready, 1)

            def clip_one(g, u, h):
                dve.wait_ge(exp_ready, u * 2 * HG + (2 * h + 2))
                cap(dve, g, h).then_inc(capped, 1)

            def row_max(u1, h, t):
                dve.wait_ge(rows_ready, u1 * (HG * QT) + (h * QT + t + 1))
                dve.tensor_reduce(neg_max[:, h, t:t + 1], rowmax_ps[:, t, 0:sh.keys], AXX, ALU.max, negate=True)\
                   .then_inc(max_ready, 1)

            def split_max(u1):
                steps = 5 if clip else 4
                at = 1
                dve.wait_ge(max_ready, u1 * (HG * QT) + HG * QT)
                if clip:
                    bound = CLAMP / sh.scale
                    dve.tensor_scalar(neg_max[:, :, :], neg_max[:, :, :], -bound, bound, ALU.max, ALU.min)\
                       .then_inc(parts_step, 1)
                    at = 2
                    dve.wait_ge(parts_step, u1 * steps + 1)
                dve.tensor_scalar(neg_max[:, :, :], neg_max[:, :, :], 1.0 / sh.shift_k, None, ALU.mult)\
                   .then_inc(parts_step, 1)
                dve.wait_ge(parts_step, u1 * steps + at)
                part = [shift_parts[:, :, :, sh.shift_row + k] for k in range(3)]
                negated = neg_max[:, :, :].rearrange("p h t -> p t h")
                left = rest[:, :, :].rearrange("p h t -> p t h")
                dve.tensor_copy(part[0], negated).then_inc(parts_step, 1)
                dve.wait_ge(parts_step, u1 * steps + at + 1)
                dve.tensor_tensor(left, negated, part[0], ALU.subtract).then_inc(parts_step, 1)
                dve.wait_ge(parts_step, u1 * steps + at + 2)
                dve.tensor_copy(part[1], left).then_inc(parts_step, 1)
                dve.wait_ge(parts_step, u1 * steps + at + 3)
                dve.tensor_tensor(part[2], left, part[1], ALU.subtract)\
                   .then_inc(parts_ready, 1)

            def divide(g, u, part):
                n = u * sh.parts + part

                def invert(*cols):
                    dve.wait_ge(pv_ready if wide else div_ready, n + 1)
                    cols = slice(*cols)
                    dve.reciprocal(r_sum[:, cols], u_ps[:, 1, cols]).then_inc(rsum_ready, 1)

                def multiply():
                    dve.wait_ge(rsum_ready, n * 2 + 2)
                    dve.tensor_tensor(attn[:, g * sh.parts + part, :], u_ps[:, 0, :] if wide else u_sb[:, :], r_sum[:, :],
                                      ALU.mult).then_inc(attn_ready, 1)
                return [lambda: invert(0, P), lambda: invert(P, SQ), multiply]

            def take_maxima(kind, b, key, g1):
                dve.wait_ge(bank_full, (sh.end_turn() if key is None else sh.turn(kind, b, key)) + 1)
                bank, free = shared(kind, key)
                if wide:
                    dve.tensor_copy(q_hi[g1][DC:P, :, :],
                                    bank[:, :].bitcast(F16)[DC:P, :].rearrange("p (h q) -> p h q", h=HG))\
                       .then_inc(free, 1)
                else:
                    dve.tensor_tensor(qst[g1][:, :], bank[:, :].bitcast(F16)[:, 0:SQ], qst[g1][:, :], ALU.add)\
                       .then_inc(free, 1)

            def turned_rows(kind, b, key, n):
                dve.wait_ge(bank_full, sh.turn(kind, b, key) + 1)
                dve.wait_ge(xnT_ready, n + 1)
                bank, free = shared(kind, key)
                dve.tensor_tensor(xnT_pair[1][:, :], bank[:, 0:SQ], xnT_pair[0][:, :], ALU.subtract).then_inc(free, 1)

            def add_residual(kind, b, key, b_of):
                dve.wait_ge(bank_full, (sh.end_turn() if key is None else sh.turn(kind, b, key)) + 1)
                bank, free = shared(kind, key)
                x = x_of(b_of)
                dve.scalar_tensor_tensor(x, bank[:, 0:QT * D].rearrange("p (t n) -> p t n", t=QT),
                                         gates[:, sh.gate:sh.gate + 1], x, ALU.mult, ALU.add).then_inc(free, 1)

            def small_softmax_scores(kind, b, key):
                dve.wait_ge(bank_full, (sh.end_turn() if key is None else sh.turn(kind, b, key)) + 1)
                bank, free = shared(kind, key)
                flat = bank[:, 0:QT * HEADS * IPA].rearrange("p (a t) -> p a t", t=IPA)
                dve.tensor_reduce(m_ipa[:, :], flat, AXX, ALU.max).then_inc(ipa_step, 1)
                dve.wait_ge(ipa_step, 4 * b + 1)
                dve.tensor_tensor(s_ipa[:, :, :, :].rearrange("p a h t -> p (a h) t"), flat,
                                  m_ipa[:, :].unsqueeze(2).broadcast_to([P, QT * HEADS, IPA]),
                                  ALU.subtract).then_inc(free, 1)

            def small_softmax(b):
                dve.wait_ge(ipa_exp, b + 1)
                dve.reduce_sum(r_ipa[:, :], e_ipa[:, :, :], AXX).then_inc(ipa_step, 1)
                dve.wait_ge(ipa_step, 4 * b + 2)
                dve.reciprocal(m_ipa[:, :], r_ipa[:, :]).then_inc(ipa_step, 1)
                dve.wait_ge(ipa_step, 4 * b + 3)
                dve.tensor_tensor(p_ipa[:, :, :], e_ipa[:, :, :],
                                  m_ipa[:, :].unsqueeze(2).broadcast_to([P, QT * HEADS, IPA]), ALU.mult)\
                   .then_inc(ipa_step, 1)

            normalise(0)
            if wide:
                turned_rows("opening", 0, ("XT",), 0)
            for key in sh.opening():
                if key[0] in (0, 1) and key[1] != "V":
                    pair("opening", 0, key, key[1:], key[0])
                elif key[0] == "MT":
                    for h in range(HG):
                        for t in range(QT):
                            row_max(0, h, t)
                    split_max(0)
                    take_maxima("opening", 0, key, 0)

            def body(kind, b, par):
                for g, s, p1, p2, tiles, tail in sh.slots(kind):
                    u = b * NG + g
                    g1 = (g + 1) % 4
                    due = []
                    if wide and s == 0 and not (kind == "first" and g <= 1):
                        due = divide((g - 2) % 4, u - 2, 1)
                    if not wide and s == 0 and not (kind == "first" and g <= 1):
                        due = divide((g - 2) % 4, u - 2, 0)[1:]
                    if wide and s == 2 and not (kind == "first" and g == 0):
                        due = divide((g - 1) % 4, u - 1, 0)
                        due.pop(0)()
                    for i in range(max(2, len(tiles))):
                        if i < len(tiles):
                            row_max(u + 1, *tiles[i])
                        if i == 0 and p1 and p1[0] != "V":
                            pair(kind, b, (g, s) + p1, p1, u + 2)
                        for _ in range(2 if s == 2 else 1):
                            if due:
                                due.pop(0)()
                    for piece in due:
                        piece()
                    if (g, s) == (1, 0) and kind != "last":
                        normalise(b + 1)
                    if ipa and (g, s) == (3, 0):
                        small_softmax(b)
                    if (HG - 1, QT - 1) in tiles:
                        split_max(u + 1)
                    if ("MT",) in tail:
                        take_maxima(kind, b, (g, s, "MT"), g1)
                    if not wide and s == 2 and not (kind == "first" and g == 0):
                        divide((g - 1) % 4, u - 1, 0)[0]()
                    if clip and s == 1:
                        p, at = floor_place(kind, g)
                        dve.wait_ge(bank_free[p], at)
                    if clip and s in (1, 3):
                        for h in {1: (0, 1), 3: (2,)}[s]:
                            clip_one(g, u, h)
                    elif clip and s == 0 and not (kind == "first" and g == 0):
                        clip_one((g - 1) % 4, u - 1, HG - 1)
                    for t in tail:
                        if t[0] == "OP":
                            add_residual(kind, b, (g, s) + t, b - 1)
                        if t[0] == "SI":
                            small_softmax_scores(kind, b, (g, s) + t)
                        if t[0] == "XT" and wide:
                            turned_rows(kind, b, (g, s) + t, b + 1)
            batches(body, dve)
            if clip:
                clip_one(3, B * NG - 1, HG - 1)
            if not wide:
                for piece in divide(2, B * NG - 2, 0)[1:]:
                    piece()
            for g, part in ([(2, 1)] if wide else []) + [(3, part) for part in range(sh.parts)]:
                for piece in divide(g, (B - 1) * NG + g, part):
                    piece()
            add_residual("last", B - 1, None, B - 1)


def layernorm_all(nc, name, x_res, xn, xnT, const, loads):
    ident, _, _, _, _, eps = const
    with ExitStack() as ctx:
        sb, ps, sem = alloc(nc, ctx, name + "n")
        stats, mv = sb("stats", [P, NT, 6]), sb("mv", [P, NT, 2])
        lnv, rstd = sb("lnv", [P, NT]), sb("rstd", [P, NT])
        turned = [ps(f"turned{i}", [P, 4, P]) for i in range(2)]
        loaded = sem("loaded")
        stats_ready = sem("stats_ready")
        rstd_ready = sem("rstd_ready")
        xn_ready = sem("xn_ready")
        turned_ready = sem("turned_ready")
        xnT_ready = sem("xnT_ready")
        with nc.Block() as block:
            @block.sync
            def _(sp):
                for dst, src in loads:
                    sp.dma_start(dst, src).then_inc(loaded, 16)
                if loads:
                    sp.wait_ge(loaded, 16 * len(loads))

            @block.vector
            def _(dve):
                for t in range(NT):
                    ins = dve.bn_stats(stats[:, t, :], x_res[:, t, :])
                ins.then_inc(stats_ready, 1)
                dve.wait_ge(stats_ready, 1)
                for t in range(NT):
                    ins = dve.bn_aggr(mv[:, t, :], stats[:, t, :])
                ins.then_inc(stats_ready, 1)
                dve.wait_ge(rstd_ready, 2)
                for t in range(NT):
                    ins = dve.tensor_scalar(xn[:, t, :], x_res[:, t, :], mv[:, t, 0:1], rstd[:, t:t + 1],
                                            ALU.subtract, ALU.mult)
                    if t % 4 == 3:
                        ins.then_inc(xn_ready, 1)

            @block.scalar
            def _(act):
                act.wait_ge(stats_ready, 2)
                act.activation(lnv[:, :], mv[:, :, 1], ACT.Ln, bias=eps[:, 0:1]).then_inc(rstd_ready, 1)
                act.wait_ge(rstd_ready, 1)
                act.activation(rstd[:, :], lnv[:, :], ACT.Exp, scale=-0.5).then_inc(rstd_ready, 1)
                for k in range(NT // 4):
                    act.wait_ge(turned_ready, k + 1)
                    act.copy(xnT[:, k * 512:(k + 1) * 512], turned[k % 2][:, :, :].rearrange("p t n -> p (t n)"))\
                       .then_inc(xnT_ready, 1)

            @block.tensor
            def _(pe):
                for k in range(NT // 4):
                    pe.wait_ge(xn_ready, k + 1)
                    if k >= 2:
                        pe.wait_ge(xnT_ready, k - 1)
                    for t in range(4):
                        ins = pe.transpose(turned[k % 2][:, t, :], xn[:, 4 * k + t, :], ident[:, :])
                    ins.then_inc(turned_ready, 1)


TB = 512
TT = TB // P


def mlp(nc, name, x_res, xnT, ones, func, jobs, scale=1.0):
    split = isinstance(xnT, tuple)
    gated = jobs[0]["up"][0][1] is not None
    items = sum(len(j["up"]) for j in jobs)
    experts = sum(len(j["down"]) for j in jobs)
    dbufs = min(2, experts)
    with ExitStack() as ctx:
        sb, ps, sem = alloc(nc, ctx, name + "m")
        chunks = max(len(j["up"]) for j in jobs)
        hid = [[sb(f"hid{i}_{c}", [P, TB]) for c in range(chunks)] for i in range(2)]
        sg = [sb(f"sg{i}", [P, TB]) for i in range(2)] if gated else None
        up_ps = [ps(f"up{i}", [P, TB]) for i in range(2)]
        gate_ps = [ps(f"gate{i}", [P, TB]) for i in range(2)] if gated else None
        down_ps = [ps(f"down{i}", [P, TT, D]) for i in range(2)]
        up_ready = sem("up_ready")
        sg_ready = sem("sg_ready")
        hid_ready = sem("hid_ready")
        down_ready = sem("down_ready")
        down_free = sem("down_free")

        with nc.Block() as block:
            @block.tensor
            def _(pe):
                def up(tb, n, k, item):
                    w, wg, _, width = item
                    pe.wait_ge(hid_ready, n + 1)
                    at = bass.ds(tb * TB, TB)
                    if split:
                        for dst, (hi, lo) in ((up_ps, w), (gate_ps, wg))[0:1 + gated]:
                            pe.matmul(dst[k % 2][0:width, :], hi, xnT[1][:, at], start=True, stop=False)
                            pe.matmul(dst[k % 2][0:width, :], lo, xnT[0][:, at], start=False, stop=False)
                            ins = pe.matmul(dst[k % 2][0:width, :], hi, xnT[0][:, at], start=False, stop=True)
                        ins.then_inc(up_ready, 1)
                        return
                    x = xnT[:, at]
                    ins = pe.matmul(up_ps[k % 2][0:width, :], w, x, start=True, stop=True)
                    if gated:
                        ins = pe.matmul(gate_ps[k % 2][0:width, :], wg, x, start=True, stop=True)
                    ins.then_inc(up_ready, 1)

                def down(job_i, job, d, m, t, hid_count):
                    ws, bias, _ = job["down"][d]
                    if t == 0:
                        pe.wait_ge(down_free, m + 1)
                        pe.wait_ge(hid_ready, hid_count + 2)
                    dst = down_ps[m_static[0] % 2][:, t, :]
                    for c, (w, item) in enumerate(zip(ws, job["up"])):
                        ins = pe.matmul(dst, hid[job_i % 2][c][0:item[3], t * P:(t + 1) * P], w,
                                        start=(c == 0), stop=(c == len(ws) - 1 and not bias))
                    for i, row in enumerate(bias):
                        ins = pe.matmul(dst, ones[0:1, 0:P], row, start=False, stop=(i == len(bias) - 1))
                    if t == TT - 1:
                        ins.then_inc(down_ready, 1)
                        m_static[0] += 1

                m_static = [0]
                with pe.Fori(0, NT // TT) as tb:
                    k = m = 0
                    todo = []
                    for j, job in enumerate(jobs):
                        per = -(-len(todo) // len(job["up"]))
                        for item in job["up"]:
                            up(tb, tb * items + k, k, item)
                            k += 1
                            for a in todo[:per]:
                                down(*a)
                            todo = todo[per:]
                        for d in range(len(job["down"])):
                            todo += [(j, job, d, tb * experts + m, t, tb * items + k) for t in range(TT)]
                            m += 1
                    for a in todo:
                        down(*a)

            @block.scalar
            def _(act):
                if not gated:
                    act.sem_inc(hid_ready, 2)
                with act.Fori(0, NT // TT) as tb:
                    k = 0
                    for j, job in enumerate(jobs):
                        for c, (_, _, bias, width) in enumerate(job["up"]):
                            act.wait_ge(up_ready, tb * items + k + 1)
                            if gated:
                                act.activation(sg[k % 2][0:width, :], gate_ps[k % 2][0:width, :], func, scale=scale)\
                                   .then_inc(sg_ready, 1)
                            else:
                                act.activation(hid[j % 2][c][0:width, :], up_ps[k % 2][0:width, :], func, bias=bias,
                                               scale=scale)\
                                   .then_inc(hid_ready, 1)
                            k += 1

            @block.vector
            def _(dve):
                dve.sem_inc(down_free, dbufs)
                if gated:
                    dve.sem_inc(hid_ready, 2)

                def combine(tb, d, m, weight):
                    dve.wait_ge(down_ready, m + 1)
                    dve.wait_ge(down_free, m + dbufs)
                    src = down_ps[d % 2]
                    if weight.shape[1] == 1:
                        x = x_res[:, bass.ds(tb * TT, TT), :]
                        ins = dve.scalar_tensor_tensor(x, src[:, :, :], weight, x, ALU.mult, ALU.add)
                    else:
                        for t in range(TT):
                            x = x_res[:, bass.ds(tb * TT + t, 1), :].rearrange("p a n -> p (a n)")
                            ins = dve.scalar_tensor_tensor(x, src[:, t, :], weight[:, bass.ds(tb * TT + t, 1)], x,
                                                           ALU.mult, ALU.add)
                    ins.then_inc(down_free, 1)

                with dve.Fori(0, NT // TT) as tb:
                    k = m = 0
                    due = []
                    for j, job in enumerate(jobs):
                        for c, (_, _, _, width) in enumerate(job["up"]):
                            if gated:
                                dve.wait_ge(sg_ready, tb * items + k + 1)
                                dve.scalar_tensor_tensor(hid[j % 2][c][0:width, :], up_ps[k % 2][0:width, :], scale,
                                                         sg[k % 2][0:width, :], ALU.mult, ALU.mult).then_inc(hid_ready, 1)
                            k += 1
                        for a in due:
                            combine(*a)
                        due = []
                        for _, _, weight in job["down"]:
                            due.append((tb, m, tb * experts + m, weight))
                            m += 1
                    for a in due:
                        combine(*a)


def butterfly_step(eng, y, t0, t1, w, stage, transposed, chain, count):
    n = 2 ** stage
    v = y.rearrange("p (b a s) -> p b a s", a=2, s=n)
    a, b = v[:, :, 0, :], v[:, :, 1, :]
    wv = w.rearrange("p (b s o i) -> p b s o i", s=n, o=2, i=2)
    w01, w10 = wv[:, :, :, 0, 1], wv[:, :, :, 1, 0]
    if transposed:
        w01, w10 = w10, w01
    t0, t1, t2, t3 = (t.rearrange("p (b s) -> p b s", s=n) for t in (t0[:, 0:256], t0[:, 256:512], t1[:, 0:256], t1[:, 256:512]))
    eng.tensor_tensor(t0, a, wv[:, :, :, 0, 0], ALU.mult)
    eng.tensor_tensor(t1, b, w01, ALU.mult)
    eng.tensor_tensor(t2, a, w10, ALU.mult)
    eng.tensor_tensor(t3, b, wv[:, :, :, 1, 1], ALU.mult).then_inc(chain, 1)
    eng.wait_ge(chain, count + 1)
    eng.tensor_tensor(a, t0, t1, ALU.add)
    eng.tensor_tensor(b, t2, t3, ALU.add).then_inc(chain, 1)
    eng.wait_ge(chain, count + 2)


class Butterflies:
    hidden, stages = 512, 9

    def __init__(self, nc, ctx, name, w):
        sb, _, sem = alloc(nc, ctx, name)
        hidden, stages = self.hidden, self.stages
        self.w = w
        self.w_exp, self.w_conT, self.b_exp = sb("w_exp", [P, hidden]), sb("w_conT", [P, hidden]), sb("b_exp", [1, hidden])
        self.up_bias, self.rows = sb("up_bias", [1, hidden]), sb("rows", [1, 2, D])
        self.up, self.down = sb("up", [P, stages, 1024]), sb("down", [P, stages, 1024])
        self.t = [sb(f"t{i}", [P, hidden]) for i in range(2)]
        self.t_row = [sb(f"t_row{i}", [1, hidden]) for i in range(2)]
        self.loaded = sem("loaded")
        self.step = sem("step")

    def load(self, sp):
        w = self.w
        loads = [(self.w_exp[:, :], w["W_exp"]), (self.w_conT[:, :], w["W_conT"]), (self.b_exp[:, :], w["b_exp"].unsqueeze(0)),
                 (self.up_bias[:, :], w["up_bias"].unsqueeze(0)), (self.rows[:, 0, :], w["b_con"].unsqueeze(0)),
                 (self.rows[:, 1, :], w["down_bias"].unsqueeze(0))]
        for dst, src in ((self.up, w["up_weights"]), (self.down, w["down_weights"])):
            for n in range(self.stages):
                loads.append((dst[:, n, :], src[n].rearrange("k o i -> (k o i)").partition_broadcast(P)))
        for dst, src in loads:
            sp.dma_start(dst, src).then_inc(self.loaded, 16)

    def run(self, pool):
        pool.wait_ge(self.loaded, 16 * (6 + 2 * self.stages))
        count = 0
        for n in range(self.stages):
            butterfly_step(pool, self.w_exp[:, :], *self.t, self.up[:, n, :], n, False, self.step, count)
            butterfly_step(pool, self.b_exp[:, :], *self.t_row, self.up[0:1, n, :], n, False, self.step, count + 2)
            m = self.stages - 1 - n
            butterfly_step(pool, self.w_conT[:, :], *self.t, self.down[:, m, :], m, True, self.step, count + 4)
            count += 6


def butterfly_ffn(nc, name, x_res, gates, const, ready):
    ident, _, _, _, ones, _ = const
    with ExitStack() as ctx:
        sb, ps, sem = alloc(nc, ctx, name)
        xn, xnT = sb("xn", [P, NT, D]), sb("xnT", [P, NT * P])
        w_con = sb("w_con", [P, 4, D])
        bias = sb("bias", [P, 4])
        layernorm_all(nc, name, x_res, xn, xnT, const, [])
        with ExitStack() as c2:
            _, ps, sem = alloc(nc, c2, name + "b")
            turned, column = ps("turned", [P, 4, D]), ps("column", [P, 4])
            turned_ready = sem("turned_ready")
            with nc.Block() as block:
                @block.vector
                def _(dve):
                    dve.wait_ge(turned_ready, 1)
                    dve.tensor_copy(w_con[:, :, :], turned[:, :, :])
                    dve.tensor_copy(bias[:, :], column[:, :])

                @block.tensor
                def _(pe):
                    for c in range(4):
                        at = slice(c * P, (c + 1) * P)
                        pe.matmul(column[:, c:c + 1], ready.b_exp[0:1, at], ones[0:1, 0:1], start=True, stop=False)
                        pe.matmul(column[:, c:c + 1], ready.up_bias[0:1, at], ones[0:1, 0:1], start=False, stop=True)
                    for c in range(4):
                        ins = pe.transpose(turned[:, c, :], ready.w_conT[:, c * P:(c + 1) * P], ident[:, :])
                    ins.then_inc(turned_ready, 1)
        mlp(nc, name, x_res, xnT, ones, ACT.Gelu, [{
            "up": [(ready.w_exp[:, c * P:(c + 1) * P], None, bias[:, c:c + 1], P) for c in range(4)],
            "down": [([w_con[:, c, :] for c in range(4)], [ready.rows[0:1, 0, :], ready.rows[0:1, 1, :]], gates[:, 4:5])]}])


def expert_ffn(nc, name, x_res, gates, const, io, w):
    ones = const[4]
    hidden, routed = 512, 7
    with ExitStack() as ctx:
        sb, ps, sem = alloc(nc, ctx, name)
        xn, xnT = sb("xn", [P, NT, D]), sb("xnT", [P, NT * P])
        wu, wg = sb("wu", [P, routed + 1, hidden]), sb("wg", [P, routed + 1, hidden])
        wd = sb("wd", [P, routed + 1, 4, D])
        pairs = {n: [sb(f"{n}_{part}", [P, routed + 1, hidden], F16) for part in ("hi", "lo")] for n in ("wu", "wg")}
        x_hi, x_lo = sb("x_hi", [P, NT * P], F16), sb("x_lo", [P, NT * P], F16)
        wr, iota = sb("wr", [P, 8]), sb("iota", [P, 8])
        weight = sb("weight", [P, 8, NT])
        layernorm_all(nc, name, x_res, xn, xnT, const, [
            (wr[:, :], w["w_router"]), (iota[:, :], io["c_iota8"]),
            (wu[:, 0:routed, :], w["w_up"].rearrange("e p n -> p e n")), (wu[:, routed, :], w["ws_up"]),
            (wg[:, 0:routed, :], w["w_gate"].rearrange("e p n -> p e n")), (wg[:, routed, :], w["ws_gate"]),
            (wd[:, routed, :, :], w["ws_down"].rearrange("(c p) n -> p c n", p=P))]
            + [(wd[:, e, :, :], w["w_down"][e].rearrange("(c p) n -> p c n", p=P)) for e in range(routed)])
        with ExitStack() as c2:
            sb2, ps, sem = alloc(nc, c2, name + "r")
            logits = ps("logits", [P, NT, 8])
            top, p_top, first = sb2("top", [P, NT]), sb2("p_top", [P, NT]), sb2("first", [P, NT])
            z, e, eq, at = (sb2(n, [P, NT, 8]) for n in ("z", "e", "eq", "at"))
            logits_ready, e_ready, step = sem("logits_ready"), sem("e_ready"), sem("step")
            hi_ready = sem("hi_ready")
            with nc.Block() as block:
                @block.tensor
                def _(pe):
                    for t in range(NT):
                        ins = pe.matmul(logits[:, t, :], xnT[:, t * P:(t + 1) * P], wr[:, :], start=True, stop=True)
                    ins.then_inc(logits_ready, 1)

                @block.scalar
                def _(act):
                    act.copy(x_hi[:, :], xnT[:, :]).then_inc(hi_ready, 1)
                    for n in range(routed + 1):
                        act.activation(pairs["wu"][0][:, n, :], wu[:, n, :], ACT.Copy, scale=W_SCALE)
                        act.activation(pairs["wg"][0][:, n, :], wg[:, n, :], ACT.Copy, scale=W_SCALE).then_inc(hi_ready, 1)
                        if n == 3:
                            act.wait_ge(step, 2)
                            act.activation(e[:, :, :], z[:, :, :], ACT.Exp).then_inc(e_ready, 1)

                @block.vector
                def _(dve):
                    def over(a):
                        return a[:, :].unsqueeze(2).broadcast_to([P, NT, 8])
                    dve.wait_ge(logits_ready, 1)
                    dve.tensor_reduce(top[:, :], logits[:, :, :], AXX, ALU.max).then_inc(step, 1)
                    dve.wait_ge(step, 1)
                    dve.tensor_tensor(z[:, :, :], logits[:, :, :], over(top), ALU.subtract).then_inc(step, 1)
                    dve.wait_ge(hi_ready, 1)
                    dve.tensor_tensor(x_lo[:, :], xnT[:, :], x_hi[:, :], ALU.subtract)
                    for n in range(routed + 1):
                        dve.wait_ge(hi_ready, n + 2)
                        for m, src in (("wu", wu), ("wg", wg)):
                            dve.scalar_tensor_tensor(pairs[m][1][:, n, :], src[:, n, :], W_SCALE, pairs[m][0][:, n, :],
                                                     ALU.mult, ALU.subtract)
                    dve.wait_ge(e_ready, 1)
                    dve.reduce_sum(p_top[:, :], e[:, :, :], AXX).then_inc(step, 1)
                    dve.tensor_tensor(eq[:, :, :], logits[:, :, :], over(top), ALU.is_equal).then_inc(step, 1)
                    dve.wait_ge(step, 4)
                    dve.scalar_tensor_tensor(at[:, :, :], eq[:, :, :], -100.0,
                                             iota[:, :].unsqueeze(1).broadcast_to([P, NT, 8]), ALU.mult, ALU.add).then_inc(step, 1)
                    dve.wait_ge(step, 5)
                    dve.tensor_reduce(first[:, :], at[:, :, :], AXX, ALU.min).then_inc(step, 1)
                    dve.reciprocal(top[:, :], p_top[:, :]).then_inc(step, 1)
                    dve.wait_ge(step, 7)
                    dve.tensor_tensor(eq[:, :, :], at[:, :, :], over(first), ALU.is_equal).then_inc(step, 1)
                    dve.tensor_scalar(p_top[:, :], top[:, :], gates[:, 5:6], 2.0, ALU.mult, ALU.mult).then_inc(step, 1)
                    dve.wait_ge(step, 9)
                    dve.tensor_tensor(weight[:, :, :].rearrange("p e t -> p t e"), eq[:, :, :], over(p_top), ALU.mult)
        jobs = []
        for e in range(routed + 1):
            up = [tuple(tuple(part[:, e, c * P:(c + 1) * P] for part in pairs[n]) for n in ("wu", "wg")) + (None, P)
                  for c in range(4)]
            col = weight[:, e, :] if e < routed else gates[:, 5:6]
            jobs.append({"up": up, "down": [([wd[:, e, c, :] for c in range(4)], [], col)]})
        mlp(nc, name, x_res, (x_hi, x_lo), ones, ACT.Silu, jobs, scale=1.0 / W_SCALE)


def column_ffn(nc, name, x_res, gates, const, io, w):
    ident, _, _, _, ones, eps = const
    cols, neurons, gate_dim = 16, 32, 64
    hidden = cols * neurons
    with ExitStack() as ctx:
        sb, ps, sem = alloc(nc, ctx, name)
        xn, xnT = sb("xn", [P, NT, D]), sb("xnT", [P, NT * P])
        col_emb, ceT = sb("col_emb", [cols, D]), sb("ceT", [P, cols])
        w1, b1, w2, b2 = sb("w1", [P, gate_dim]), sb("b1", [gate_dim, 1]), sb("w2", [gate_dim, cols]), sb("b2", [1, cols])
        w_cols, b_cols = sb("w_cols", [P, cols, neurons]), sb("b_cols", [1, hidden])
        proj_w, proj_b = sb("proj_w", [P, 4, D]), sb("proj_b", [1, D])
        ln_g, ln_b = sb("ln_g", [P, D]), sb("ln_b", [P, D])
        iota = sb("iota", [P, cols])
        weight = sb("weight", [P, NT, cols])
        layernorm_all(nc, name, x_res, xn, xnT, const, [
            (col_emb[:, :], w["col_emb"]), (w1[:, :], w["gate_w1"]), (b1[:, :], w["gate_b1"].unsqueeze(1)),
            (w2[:, :], w["gate_w2"]), (b2[:, :], w["gate_b2"].unsqueeze(0)),
            (w_cols[:, :, :], w["W_cols"].rearrange("c p n -> p c n")),
            (b_cols[:, :], w["b_cols"].rearrange("(a c) n -> a (c n)", a=1)),
            (proj_w[:, :, :], w["proj_w"].rearrange("(c p) n -> p c n", p=P)), (proj_b[:, :], w["proj_b"].unsqueeze(0)),
            (ln_g[:, :], w["ln_g"].partition_broadcast(P)), (ln_b[:, :], w["ln_b"].partition_broadcast(P)),
            (iota[:, :], io["c_iota16"])])

        with ExitStack() as c2:
            sb2, ps, sem = alloc(nc, c2, name + "r")
            hg = sb2("hg", [gate_dim, NT * P])
            sq, norm, n2 = sb2("sq", [P, NT, D]), sb2("norm", [P, NT]), sb2("n2", [P, NT])
            ce2, ce_n, ce_s = sb2("ce2", [cols, D]), sb2("ce_n", [cols, 1]), sb2("ce_s", [cols, D])
            sig, lg, z, e, eq, at = (sb2(n, [P, NT, cols]) for n in ("sig", "lg", "z", "e", "eq", "at"))
            top, total, first, p_top = (sb2(n, [P, NT]) for n in ("top", "total", "first", "p_top"))
            hg_ps = [ps(f"hg_ps{i}", [gate_dim, 512]) for i in range(2)]
            gate_ps, sim_ps, ce_ps = ps("gate_ps", [P, NT, cols]), ps("sim_ps", [P, NT, cols]), ps("ce_ps", [P, cols])
            step, reci = sem("step"), sem("reci")
            act_step = sem("act_step")
            hg_ready, hg_done = sem("hg_ready"), sem("hg_done")
            gate_ready, ce_ready, sim_ready = sem("gate_ready"), sem("ce_ready"), sem("sim_ready")
            with nc.Block() as block:
                @block.tensor
                def _(pe):
                    for k in range(4):
                        if k >= 2:
                            pe.wait_ge(hg_done, k - 1)
                        pe.matmul(hg_ps[k % 2][:, :], w1[:, :], xnT[:, k * 512:(k + 1) * 512], start=True, stop=True)\
                          .then_inc(hg_ready, 1)
                    for t in range(NT):
                        if t % 4 == 0:
                            pe.wait_ge(hg_done, t // 4 + 1)
                        pe.matmul(gate_ps[:, t, :], hg[:, t * P:(t + 1) * P], w2[:, :], start=True, stop=False)
                        ins = pe.matmul(gate_ps[:, t, :], ones[0:1, 0:P], b2[:, :], start=False, stop=True)
                    ins.then_inc(gate_ready, 1)
                    pe.wait_ge(step, 6)
                    pe.transpose(ce_ps[:, :], ce_s[:, :], ident[0:cols, 0:cols]).then_inc(ce_ready, 1)
                    pe.wait_ge(step, 7)
                    for t in range(NT):
                        ins = pe.matmul(sim_ps[:, t, :], xnT[:, t * P:(t + 1) * P], ceT[:, :], start=True, stop=True)
                    ins.then_inc(sim_ready, 1)

                @block.scalar
                def _(act):
                    act.wait_ge(step, 4)
                    act.activation(norm[:, :], n2[:, :], ACT.Sqrt)
                    act.activation(ce_n[:, :], ce_n[:, :], ACT.Sqrt).then_inc(act_step, 1)
                    for k in range(4):
                        act.wait_ge(hg_ready, k + 1)
                        act.activation(hg[:, k * 512:(k + 1) * 512], hg_ps[k % 2][:, :], ACT.Gelu, bias=b1[:, 0:1])\
                           .then_inc(hg_done, 1)
                    act.wait_ge(gate_ready, 1)
                    act.activation(sig[:, :, :], gate_ps[:, :, :], ACT.Sigmoid).then_inc(act_step, 1)
                    act.wait_ge(step, 11)
                    act.activation(e[:, :, :], z[:, :, :], ACT.Exp).then_inc(act_step, 1)

                @block.vector
                def _(dve):
                    def over(a):
                        return a[:, :].unsqueeze(2).broadcast_to([P, NT, cols])
                    dve.tensor_tensor(sq[:, :, :], xn[:, :, :], xn[:, :, :], ALU.mult).then_inc(step, 1)
                    dve.tensor_tensor(ce2[:, :], col_emb[:, :], col_emb[:, :], ALU.mult).then_inc(step, 1)
                    dve.wait_ge(step, 2)
                    dve.reduce_sum(n2[:, :], sq[:, :, :], AXX).then_inc(step, 1)
                    dve.reduce_sum(ce_n[:, :], ce2[:, :], AXX).then_inc(step, 1)
                    dve.wait_ge(act_step, 1)
                    dve.tensor_scalar(ce_n[:, :], ce_n[:, :], 1e-12, None, ALU.max)
                    dve.tensor_scalar(norm[:, :], norm[:, :], 1e-12, None, ALU.max).then_inc(step, 1)
                    dve.wait_ge(step, 5)
                    dve.reciprocal(ce2[:, 0:1], ce_n[:, :])
                    dve.reciprocal(n2[:, :], norm[:, :]).then_inc(reci, 1)
                    dve.wait_ge(reci, 1)
                    dve.tensor_scalar(ce_s[:, :], col_emb[:, :], ce2[:, 0:1], None, ALU.mult).then_inc(step, 1)
                    dve.wait_ge(ce_ready, 1)
                    dve.tensor_copy(ceT[:, :], ce_ps[:, :]).then_inc(step, 1)
                    dve.wait_ge(sim_ready, 1)
                    dve.tensor_tensor(lg[:, :, :], sim_ps[:, :, :], over(n2), ALU.mult).then_inc(step, 1)
                    dve.wait_ge(act_step, 2)
                    dve.wait_ge(step, 8)
                    dve.tensor_tensor(z[:, :, :], lg[:, :, :], sig[:, :, :], ALU.add).then_inc(step, 1)
                    dve.wait_ge(step, 9)
                    dve.tensor_reduce(top[:, :], z[:, :, :], AXX, ALU.max).then_inc(step, 1)
                    dve.wait_ge(step, 10)
                    dve.tensor_tensor(eq[:, :, :], z[:, :, :], over(top), ALU.is_equal)
                    dve.tensor_tensor(z[:, :, :], z[:, :, :], over(top), ALU.subtract).then_inc(step, 1)
                    dve.wait_ge(step, 11)
                    dve.scalar_tensor_tensor(at[:, :, :], eq[:, :, :], -100.0,
                                             iota[:, :].unsqueeze(1).broadcast_to([P, NT, cols]), ALU.mult, ALU.add)\
                       .then_inc(step, 1)
                    dve.wait_ge(step, 12)
                    dve.tensor_reduce(first[:, :], at[:, :, :], AXX, ALU.min).then_inc(step, 1)
                    dve.wait_ge(act_step, 3)
                    dve.reduce_sum(total[:, :], e[:, :, :], AXX).then_inc(step, 1)
                    dve.wait_ge(step, 14)
                    dve.reciprocal(p_top[:, :], total[:, :])
                    dve.tensor_tensor(eq[:, :, :], at[:, :, :], over(first), ALU.is_equal).then_inc(step, 1)
                    dve.wait_ge(step, 15)
                    dve.tensor_tensor(weight[:, :, :], eq[:, :, :], over(p_top), ALU.mult)

        with ExitStack() as c2:
            sb2, ps, sem = alloc(nc, c2, name + "c")
            hc = [sb2(f"hc{i}", [P, cols, neurons]) for i in range(2)]
            hw = [sb2(f"hw{i}", [P, hidden]) for i in range(2)]
            hT = [sb2(f"hT{i}", [P, 4, P]) for i in range(2)]
            y, yn = sb2("y", [P, NT, D]), sb2("yn", [P, NT, D])
            stats, mv = sb2("stats", [P, NT, 6]), sb2("mv", [P, NT, 2])
            lnv, rstd = sb2("lnv", [P, NT]), sb2("rstd", [P, NT])
            up_ps = [ps(f"up{i}", [P, hidden]) for i in range(2)]
            t_ps = [ps(f"t{i}", [P, 4, P]) for i in range(2)]
            y_ps = [ps(f"y{i}", [P, D]) for i in range(2)]
            up_ready = sem("up_ready")
            hc_ready = sem("hc_ready")
            hw_ready = sem("hw_ready")
            t_ready = sem("t_ready")
            hT_ready = sem("hT_ready")
            y_ready = sem("y_ready")
            y_done = sem("y_done")
            step, rstd_ready = sem("step"), sem("rstd_ready")
            with nc.Block() as block:
                @block.tensor
                def _(pe):
                    def up(t, i):
                        if i >= 2:
                            pe.wait_ge(hc_ready, t - 1)
                        pe.matmul(up_ps[i % 2][:, :], xnT_tile(t), w_cols[:, :, :].rearrange("p c n -> p (c n)"),
                                  start=True, stop=False)
                        pe.matmul(up_ps[i % 2][:, :], ones[0:1, 0:P], b_cols[:, :], start=False, stop=True)\
                          .then_inc(up_ready, 1)

                    def xnT_tile(t):
                        return xnT[:, t * P:(t + 1) * P]

                    for t in range(NT + 2):
                        if t < NT:
                            up(t, t)
                        if 1 <= t <= NT:
                            n = t - 1
                            pe.wait_ge(hw_ready, n + 1)
                            if n >= 2:
                                pe.wait_ge(hT_ready, n - 1)
                            for c in range(4):
                                ins = pe.transpose(t_ps[n % 2][:, c, :], hw[n % 2][:, c * P:(c + 1) * P], ident[:, :])
                            ins.then_inc(t_ready, 1)
                        if t >= 2:
                            n = t - 2
                            if n >= 2:
                                pe.wait_ge(y_done, n - 1)
                            pe.wait_ge(hT_ready, n + 1)
                            for c in range(4):
                                pe.matmul(y_ps[n % 2][:, :], hT[n % 2][:, c, :], proj_w[:, c, :], start=(c == 0), stop=False)
                            pe.matmul(y_ps[n % 2][:, :], ones[0:1, 0:P], proj_b[:, :], start=False, stop=True)\
                              .then_inc(y_ready, 1)

                @block.scalar
                def _(act):
                    def hidden_values(t):
                        act.wait_ge(up_ready, t + 1)
                        act.activation(hc[t % 2][:, :, :], up_ps[t % 2][:, :].rearrange("p (c n) -> p c n", c=cols), ACT.Gelu)\
                           .then_inc(hc_ready, 1)
                    hidden_values(0)
                    for t in range(NT):
                        if t + 1 < NT:
                            if t >= 1:
                                act.wait_ge(hw_ready, t)
                            hidden_values(t + 1)
                        act.wait_ge(t_ready, t + 1)
                        act.copy(hT[t % 2][:, :, :], t_ps[t % 2][:, :, :]).then_inc(hT_ready, 1)
                    act.wait_ge(step, 2)
                    act.activation(lnv[:, :], mv[:, :, 1], ACT.Ln, bias=eps[:, 0:1]).then_inc(rstd_ready, 1)
                    act.wait_ge(rstd_ready, 1)
                    act.activation(rstd[:, :], lnv[:, :], ACT.Exp, scale=-0.5).then_inc(rstd_ready, 1)

                @block.vector
                def _(dve):
                    for t in range(NT + 2):
                        if t < NT:
                            dve.wait_ge(hc_ready, t + 1)
                            if t >= 2:
                                dve.wait_ge(t_ready, t - 1)
                            dve.tensor_tensor(hw[t % 2][:, :].rearrange("p (c n) -> p c n", c=cols), hc[t % 2][:, :, :],
                                              weight[:, t, :].unsqueeze(2).broadcast_to([P, cols, neurons]), ALU.mult)\
                               .then_inc(hw_ready, 1)
                        if t >= 2:
                            n = t - 2
                            dve.wait_ge(y_ready, n + 1)
                            dve.tensor_tensor(y[:, n, :], y_ps[n % 2][:, :], xn[:, n, :], ALU.add).then_inc(y_done, 1)
                    dve.wait_ge(y_done, NT)
                    for t in range(NT):
                        ins = dve.bn_stats(stats[:, t, :], y[:, t, :])
                    ins.then_inc(step, 1)
                    dve.wait_ge(step, 1)
                    for t in range(NT):
                        ins = dve.bn_aggr(mv[:, t, :], stats[:, t, :])
                    ins.then_inc(step, 1)
                    dve.wait_ge(rstd_ready, 2)
                    for t in range(NT):
                        ins = dve.tensor_scalar(yn[:, t, :], y[:, t, :], mv[:, t, 0:1], rstd[:, t:t + 1],
                                                ALU.subtract, ALU.mult)
                    ins.then_inc(step, 1)
                    dve.wait_ge(step, 3)
                    every = [P, NT, D]
                    dve.tensor_tensor(y[:, :, :], yn[:, :, :], ln_g[:, :].unsqueeze(1).broadcast_to(every), ALU.mult)\
                       .then_inc(step, 1)
                    dve.wait_ge(step, 4)
                    dve.tensor_tensor(yn[:, :, :], y[:, :, :], ln_b[:, :].unsqueeze(1).broadcast_to(every), ALU.add)\
                       .then_inc(step, 1)
                    dve.wait_ge(step, 5)
                    dve.scalar_tensor_tensor(x_res[:, :, :], yn[:, :, :], gates[:, 6:7], x_res[:, :, :], ALU.mult, ALU.add)


def choice_ffn(nc, name, x_res, gates, const, io, w):
    ident, _, _, _, ones, _ = const
    experts, groups, width = 8, 4, 341
    chosen = NT * P // experts
    rounds, tries = 10, 7
    spans = [(0, P), (P, P), (2 * P, width - 2 * P)]
    with ExitStack() as ctx:
        sb, ps, sem = alloc(nc, ctx, name)
        xn, xnT = sb("xn", [P, NT, D]), sb("xnT", [P, NT * P])
        wr, br = sb("wr", [P, experts]), sb("br", [1, experts])
        wu, bu = sb("wu", [P, groups, width]), sb("bu", [P, 3, groups])
        wu_hi, wu_lo = sb("wu_hi", [P, groups, width], F16), sb("wu_lo", [P, groups, width], F16)
        x_hi, x_lo = sb("x_hi", [P, NT * P], F16), sb("x_lo", [P, NT * P], F16)
        wd, bd = sb("wd", [P, experts, 3, D]), sb("bd", [1, experts, D])
        same, before, masks = sb("same", [P, P]), sb("before", [P, P]), sb("masks", [P, rounds * tries], U32)
        weight = sb("weight", [P, experts, NT])
        loads = [(wr[:, :], w["Wr"]), (br[:, :], w["br"].unsqueeze(0)), (wu[:, :, :], w["W_up"].rearrange("g p f -> p g f")),
                 (bd[:, :, :], w["b_down"].unsqueeze(0)), (same[:, :], io["c_same"]), (before[:, :], io["c_before"]),
                 (masks[:, :], io["c_masks"])]
        for c, (at, n) in enumerate(spans):
            loads.append((bu[0:n, c, :], w["b_upT"][at:at + n, :]))
            loads.append((wd[0:n, :, c, :], w["W_down"][:, at:at + n, :].rearrange("e f n -> f e n")))
        layernorm_all(nc, name, x_res, xn, xnT, const, loads)
        with ExitStack() as c2:
            sb2, ps, sem = alloc(nc, c2, name + "r")
            logits, turned = ps("logits", [P, NT, experts]), ps("turned", [P, P])
            count_ps, back_ps = ps("count", [P, 4]), ps("back", [P, P])
            top, total, z, e, probs = (sb2(n, s) for n, s in (
                ("top", [P, NT]), ("total", [P, NT]), ("z", [P, NT, experts]), ("e", [P, NT, experts]),
                ("probs", [P, NT, experts])))
            p, over_it, gt, eq, rank, chosen_p = (sb2(n, [P, P]) for n in ("p", "over_it", "gt", "eq", "rank", "chosen_p"))
            least, trial, cnt, kept = sb2("least", [P, 1], U32), sb2("trial", [P, tries], U32), sb2("cnt", [P, tries]), sb2("kept", [P, 1])
            over_all = sb2("over_all", [P, tries, P])
            held = sb2("held", [P, 1 + tries])
            n_gt, n_eq, room = sb2("n_gt", [P, 1]), sb2("n_eq", [P, 1]), sb2("room", [P, 1])
            least_f, trial_f = least[:, :].bitcast(F32), trial[:, :].bitcast(F32)
            tries_ps = ps("tries", [P, tries])
            step, e_ready, late = sem("step"), sem("e_ready"), sem("late")
            pe_step = sem("pe_step")
            trial_ready, counted, summed, judged, settled = (
                sem(n) for n in ("trial_ready", "counted", "summed", "judged", "settled"))
            hi_ready = sem("hi_ready")
            with nc.Block() as block:
                @block.gpsimd
                def _(pool):
                    pool.wait_ge(hi_ready, 1)
                    pool.tensor_tensor(x_lo[:, :], xnT[:, :], x_hi[:, :], ALU.subtract)

                @block.tensor
                def _(pe):
                    for t in range(NT):
                        pe.matmul(logits[:, t, :], xnT[:, t * P:(t + 1) * P], wr[:, :], start=True, stop=False)
                        ins = pe.matmul(logits[:, t, :], ones[0:1, 0:P], br[:, :], start=False, stop=True)
                    ins.then_inc(pe_step, 1)
                    pe.wait_ge(step, 5)
                    pe.transpose(turned[:, :], probs[:, :, :].rearrange("p t e -> p (t e)"), ident[:, :]).then_inc(pe_step, 1)
                    with pe.Fori(0, rounds) as i:
                        pe.wait_ge(counted, i + 1)
                        pe.matmul(tries_ps[:, :], same[:, :], cnt[:, :], start=True, stop=True).then_inc(summed, 1)
                    pe.wait_ge(step, 7)
                    pe.matmul(count_ps[:, 1:2], same[:, :], n_gt[:, :], start=True, stop=True)
                    pe.matmul(count_ps[:, 2:3], before[:, :], n_eq[:, :], start=True, stop=True).then_inc(pe_step, 1)
                    pe.wait_ge(step, 12)
                    pe.transpose(back_ps[:, :], chosen_p[:, :], ident[:, :]).then_inc(pe_step, 1)

                @block.scalar
                def _(act):
                    act.copy(x_hi[:, :], xnT[:, :]).then_inc(hi_ready, 1)
                    act.activation(wu_hi[:, :, :], wu[:, :, :], ACT.Copy, scale=W_SCALE).then_inc(hi_ready, 1)
                    act.wait_ge(step, 2)
                    act.activation(e[:, :, :], z[:, :, :], ACT.Exp).then_inc(e_ready, 1)

                @block.vector
                def _(dve):
                    def over(a):
                        return a[:, :].unsqueeze(2).broadcast_to([P, NT, experts])
                    dve.wait_ge(pe_step, 1)
                    dve.tensor_reduce(top[:, :], logits[:, :, :], AXX, ALU.max).then_inc(step, 1)
                    dve.wait_ge(step, 1)
                    dve.tensor_tensor(z[:, :, :], logits[:, :, :], over(top), ALU.subtract).then_inc(step, 1)
                    dve.wait_ge(hi_ready, 2)
                    dve.scalar_tensor_tensor(wu_lo[:, :, :], wu[:, :, :], W_SCALE, wu_hi[:, :, :], ALU.mult, ALU.subtract)
                    dve.wait_ge(e_ready, 1)
                    dve.reduce_sum(total[:, :], e[:, :, :], AXX).then_inc(step, 1)
                    dve.wait_ge(step, 3)
                    dve.reciprocal(top[:, :], total[:, :]).then_inc(step, 1)
                    dve.wait_ge(step, 4)
                    dve.tensor_tensor(probs[:, :, :], e[:, :, :], over(top), ALU.mult).then_inc(step, 1)
                    dve.wait_ge(pe_step, 2)
                    dve.tensor_copy(p[:, :], turned[:, :])
                    dve.memset(least[:, :], 0).then_inc(settled, 1)
                    with dve.Fori(0, rounds) as i:
                        dve.wait_ge(settled, i + 1)
                        dve.tensor_tensor(trial[:, :], least[:, :].broadcast_to([P, tries]),
                                          masks[:, bass.ds(i * tries, tries)], ALU.bitwise_or)
                        dve.tensor_copy(held[:, 0:1], least_f).then_inc(trial_ready, 1)
                        dve.wait_ge(trial_ready, i + 1)
                        for k in range(tries):
                            ins = dve.tensor_scalar(over_all[:, k, :], p[:, :], trial_f[:, k:k + 1], None, ALU.is_ge, ALU.add,
                                                    accum_out=cnt[:, k:k + 1])
                        ins.then_inc(counted, 1)
                        dve.wait_ge(summed, i + 1)
                        dve.scalar_tensor_tensor(held[:, 1:], tries_ps[:, :], chosen - 0.5, trial_f, ALU.is_gt, ALU.mult)\
                           .then_inc(judged, 1)
                        dve.wait_ge(judged, i + 1)
                        dve.tensor_reduce(least_f, held[:, :], AXX, ALU.max).then_inc(settled, 1)
                    dve.wait_ge(settled, rounds + 1)
                    dve.tensor_scalar(gt[:, :], p[:, :], least_f, None, ALU.is_gt, ALU.add, accum_out=n_gt[:, :]).then_inc(step, 1)
                    dve.tensor_scalar(eq[:, :], p[:, :], least_f, None, ALU.is_equal, ALU.add, accum_out=n_eq[:, :]).then_inc(step, 1)
                    dve.wait_ge(step, 7)
                    dve.tensor_tensor_scan(rank[:, :], ones[:, 0:P], eq[:, :], 0.0, ALU.mult, ALU.add).then_inc(step, 1)
                    dve.wait_ge(pe_step, 3)
                    dve.tensor_scalar(kept[:, :], count_ps[:, 1:2], -1.0, float(chosen), ALU.mult, ALU.add).then_inc(step, 1)
                    dve.wait_ge(step, 9)
                    dve.tensor_tensor(room[:, :], kept[:, :], count_ps[:, 2:3], ALU.subtract).then_inc(step, 1)
                    dve.wait_ge(step, 10)
                    dve.scalar_tensor_tensor(over_it[:, :], rank[:, :], room[:, 0:1], eq[:, :], ALU.is_le, ALU.mult)\
                       .then_inc(step, 1)
                    dve.wait_ge(step, 11)
                    dve.tensor_tensor(rank[:, :], over_it[:, :], gt[:, :], ALU.add).then_inc(late, 1)
                    dve.wait_ge(late, 1)
                    dve.tensor_tensor(chosen_p[:, :], rank[:, :], p[:, :], ALU.mult).then_inc(step, 1)
                    dve.wait_ge(pe_step, 4)
                    dve.tensor_scalar(weight[:, :, :].rearrange("p e t -> p t e"),
                                      back_ps[:, :].rearrange("p (t e) -> p t e", e=experts), gates[:, 7:8], None, ALU.mult)
        jobs = []
        for g in range(groups):
            up = [((wu_hi[:, g, at:at + n], wu_lo[:, g, at:at + n]), None, bu[0:n, c, g:g + 1], n) for c, (at, n) in enumerate(spans)]
            jobs.append({"up": up, "down": [([wd[0:n, e, c, :] for c, (_, n) in enumerate(spans)], [bd[0:1, e, :]],
                                             weight[:, e, :]) for e in (2 * g, 2 * g + 1)]})
        mlp(nc, name, x_res, (x_hi, x_lo), ones, ACT.Silu, jobs, scale=1.0 / W_SCALE)


def program(nc, io, layers):
    SEMAPHORES.clear()
    with ExitStack() as ctx:
        sb, ps, sem = alloc(nc, ctx, "top")
        x_res = sb("x_res", [P, NT, D])
        gates = sb("gates", [P, 8])
        gates_in = sb("gates_in", [P, 8])
        ident, bsel, ones = sb("ident", [P, P]), sb("bsel", [P, P]), sb("ones", [P, SK])
        identb, identh = sb("identb", [P, P], BF16), sb("identh", [P, P], F16)
        cvec, eps = sb("cvec", [P, 2]), sb("eps", [P, 1])
        mask_in, mask_f = sb("mask_in", [B, SK], U8), sb("mask_f", [B, SK])
        loaded, ready, stored = sem("loaded"), sem("ready"), sem("stored")
        mask_rows = io["scratch_mask"]

        with nc.Block() as block:
            @block.sync
            def _(sp):
                for dst, src in ((x_res[:, :, :], io["x"].rearrange("b (t p) d -> p (b t) d", p=P)),
                                 (gates_in[:, 0:4], io["g_xattn"].partition_broadcast(P)),
                                 (gates_in[:, 4:8], io["g_ffn"].partition_broadcast(P)),
                                 (ident[:, :], io["c_ident"]), (identh[:, :], io["c_identh"]),
                                 (bsel[:, :], io["c_bsel"]), (cvec[:, :], io["c_vec"]),
                                 (mask_in[:, :], io["mask_BxS2_bf1"])):
                    sp.dma_start(dst, src).then_inc(loaded, 16)
                sp.wait_ge(ready, 4)
                sp.dma_start(mask_rows, mask_f[:, :]).then_inc(stored, 16)
                sp.wait_ge(stored, 16)

            @block.scalar
            def _(act):
                act.wait_ge(loaded, 8 * 16)
                act.activation(gates[:, :], gates_in[:, :], ACT.Tanh).then_inc(ready, 1)

            @block.vector
            def _(dve):
                dve.memset(ones[:, :], 1.0)
                dve.memset(eps[:, :], EPS)
                dve.wait_ge(loaded, 8 * 16)
                dve.tensor_copy(identb[:, :], identh[:, :])
                dve.tensor_copy(mask_f[:, :], mask_in[:, :]).then_inc(ready, 1)
                dve.wait_ge(ready, 2)
                dve.tensor_scalar(mask_f[:, :], mask_f[:, :], 1.0, MASK_K, ALU.subtract, ALU.mult).then_inc(ready, 2)

        const = (ident, identb, cvec, bsel, ones, eps)

        def weights(prefix, names):
            return {n: io[f"{prefix}_{n}"] for n in names}

        shared = {"ctxT": io["ctxT"], "identh": identh, "ctx_tail": io["c_ctx_tail"],
                  "ones_row": io["c_ones"]}
        with ExitStack() as c2:
            folding = Butterflies(nc, c2, "L0w", weights("L0_ffn", "W_exp b_exp up_weights up_bias down_weights W_conT b_con "
                                                         "down_bias".split()))
            if 0 in layers:
                attention(nc, Shape("L0x", wide=False, clip=True, bias=True, gate=0),
                          shared | {"shift_k_row": io["c_shift_k"], "keyrow": io["c_keyrow"]}
                          | weights("L0_xattn", "Wq bqT Wk bk Wv bv Wo bo".split()), (x_res, gates), const, folding)
            if 1 in layers:
                butterfly_ffn(nc, "L0f", x_res, gates, const, folding)
        if 2 in layers:
            attention(nc, Shape("L1x", wide=True, ipa=True, gate=1),
                      shared | {"ctx_tail": io["c_ctx_tail_ipa"]} | weights("L1_xattn", "Wq Wk Wv Wo bo q_downT q_up q_alpha k_downT k_up k_alpha v_downT v_up "
                                       "v_alpha o_downT o_up o_alpha Wk_ipa Wv_ipa".split()), (x_res, gates), const)
        if 3 in layers:
            expert_ffn(nc, "L1f", x_res, gates, const, io,
                       weights("L1_ffn", "w_router w_up w_gate w_down ws_up ws_gate ws_down".split()))
        nc.clear_and_free_semaphores(SEMAPHORES)
        SEMAPHORES.clear()
        nc.all_engine_barrier()
        stored = sem("stored_out")
        if 4 in layers:
            attention(nc, Shape("L2x", wide=True, gate=2),
                      shared | weights("L2_xattn", "Wq Wk Wv Wo bo".split()), (x_res, gates), const)
        if 5 in layers:
            column_ffn(nc, "L2f", x_res, gates, const, io, weights("L2_ffn", "col_emb gate_w1 gate_b1 gate_w2 gate_b2 W_cols "
                                                                   "b_cols proj_w proj_b ln_g ln_b".split()))
        if 6 in layers:
            attention(nc, Shape("L3x", wide=False, mask=True, out_bias=False, gate=3),
                      shared | {"mask_row": mask_rows.unsqueeze(1), "mask_q": io["c_mask_q"],
                                "mask_k_row": io["c_mask_k"],
                                "shift_k_row": io["c_shift_k_mask"]} | weights("L3_xattn", "Wq Wk Wv Wo".split()),
                      (x_res, gates), const)
        if 7 in layers:
            choice_ffn(nc, "L3f", x_res, gates, const, io,
                       weights("L3_ffn", "Wr br W_up b_upT W_down b_down".split()))

        with nc.Block() as block:
            @block.sync
            def _(sp):
                sp.dma_start(io["out"].rearrange("b (t p) d -> p (b t) d", p=P), x_res[:, :, :]).then_inc(stored, 16)
                sp.wait_ge(stored, 16)


def constants():
    row = np.arange(P)
    ctx_tail = {}
    for n, hidden in (("", 0), ("_ipa", IPA)):
        ctx_tail[n] = np.zeros((P - DC, SK), np.float16)
        ctx_tail[n][0:3] = SHIFT_K
        ctx_tail[n][3, SK - hidden:] = HIDE_KEY
    slot = (row % 32) // 8
    vec = np.zeros((P, 2), np.float32)
    vec[:, 0] = slot == 1
    vec[:, 1] = slot == 2
    bsel = np.zeros((P, P), np.float32)
    bsel[(row // 32) * 32 + 8, row] = 1.0
    mask_q, mask_k = np.zeros((P, NG), np.float32), np.zeros((1, NG, P), np.float32)
    mask_q[24::32] = MASK_Q
    mask_k[:, :, 24::32] = 1.0
    shift_k = np.zeros((1, NG, P), np.float32)
    for part in range(3):
        shift_k[:, :, 25 + part::32] = 1.0
    keyrow = np.zeros((P, HG, P), np.float16)
    for h in range(HG):
        keyrow[32 * h + 25:32 * h + 28, h] = SHIFT_K
    return {"c_ctx_tail": ctx_tail[""], "c_ctx_tail_ipa": ctx_tail["_ipa"], "c_keyrow": keyrow, "c_vec": vec, "c_bsel": bsel, "c_mask_q": mask_q, "c_mask_k": mask_k,
            "c_ident": np.eye(P, dtype=np.float32),
            "c_iota8": np.tile(np.arange(8, dtype=np.float32), (P, 1)),
            "c_iota16": np.tile(np.arange(16, dtype=np.float32), (P, 1)),
            "c_identh": np.eye(P, dtype=np.float16), "c_shift_k": shift_k * SHIFT_K,
            "c_shift_k_mask": shift_k * MASK_K,
            "c_same": (row[:, None] % 8 == row % 8).astype(np.float32),
            "c_before": ((row[:, None] % 8 == row % 8) & (row[:, None] < row)).astype(np.float32),
            "c_masks": np.tile((np.arange(1, 8, dtype=np.uint32) << np.arange(27, -1, -3, dtype=np.uint32)[:, None])
                               .reshape(-1), (P, 1)),
            "c_ones": np.ones((1, SK), np.float32)}


LAYERS = (0, 1, 2, 3, 4, 5, 6, 7)


def kernel(**inputs):
    import concourse.bacc as bacc
    from concourse.bass_utils import run_bass_kernel_spmd

    nc = bacc.Bacc("TRN2", target_bir_lowering=False, num_devices=1)
    arrays = {n: np.ascontiguousarray(a) for n, a in inputs.items() if n != "ctx_768"}
    arrays["mask_BxS2_bf1"] = arrays["mask_BxS2_bf1"].view(np.uint8)
    arrays["ctxT"] = np.ascontiguousarray(np.asarray(inputs["ctx_768"]).transpose(0, 2, 1))
    for n in "qkvo":
        arrays[f"L1_xattn_{n}_downT"] = np.ascontiguousarray(np.asarray(arrays.pop(f"L1_xattn_{n}_down")).T)
    arrays["L0_xattn_bqT"] = np.ascontiguousarray(
        np.asarray(arrays.pop("L0_xattn_bq")).reshape(NG, HG, D // HEADS).transpose(1, 2, 0))
    arrays["L0_ffn_W_conT"] = np.ascontiguousarray(np.asarray(arrays.pop("L0_ffn_W_con")).T)
    arrays["L3_ffn_b_upT"] = np.ascontiguousarray(np.asarray(arrays.pop("L3_ffn_b_up")).T)
    arrays |= constants()
    io = {n: nc.dram_tensor(f"in_{n}", a.shape, mybir.dt.from_np(a.dtype), kind="ExternalInput").ap()
          for n, a in arrays.items()}
    io["scratch_mask"] = nc.dram_tensor("scratch_mask", (B, SK), F32).ap()
    io["out"] = nc.dram_tensor("out_x", (B, SQ, D), F32, kind="ExternalOutput").ap()
    program(nc, io, LAYERS)
    result = run_bass_kernel_spmd(nc, [{f"in_{n}": a for n, a in arrays.items()}], core_ids=[0])
    return result.results[0]["out_x"]
```
